# Optimizing a Trainium2 kernel written in Bass

```python
import numpy as np
import jax
import jax.numpy as jnp

def _softmax(x, axis=-1):
    return jax.nn.softmax(x, axis=axis)

def _gelu(x):
    return jax.nn.gelu(x, approximate=True)

def _silu(x):
    return jax.nn.silu(x)

def _sigmoid(x):
    return jax.nn.sigmoid(x)

def _layernorm(x, axis=-1, eps=1e-05):
    m = jnp.mean(x, axis=axis, keepdims=True)
    v = jnp.var(x, axis=axis, keepdims=True)
    return (x - m) / jnp.sqrt(v + eps)

def _scatter_add(tgt, idx, src, axis=0):
    return tgt.at[idx].add(src)

def _segment_sum(src, seg, n):
    return jax.ops.segment_sum(src, seg, n)
kernel_name = 'mk_adj_resnorm_d2_adj_r2_9dc927'

def setup_inputs(seed: int=0):
    np.random.seed(seed)
    _w = jnp.asarray

    def _rec_inputs():
        import jax
        import jax.numpy as jnp
        _gk = jax.random.key(seed)
        x = -0.000929 + 1 * jax.random.normal(jax.random.fold_in(_gk, 1), (4096, 128), jnp.float32)
        _a = jax.random.bernoulli(jax.random.fold_in(_gk, 2), 0.00390625, (4096, 4096))
        _a = jnp.logical_or(_a, jnp.eye(4096, dtype=bool))
        _af = _a.astype(jnp.float32)
        _af = _af * jax.random.uniform(jax.random.fold_in(_gk, 3), (4096, 4096), jnp.float32, 0.05, 1)
        adj = _af
        return (x, adj)
    x, adj = _rec_inputs()

    def _L0_gnn_setup():
        import jax, jax.numpy as jnp
        import numpy as np
        N, H, HEADS = (2048, 128, 3)
        ALPHA = 0.2
        NEG_INF = -9000000000000000.0

        def _sign_adj(key, n, density):
            k1, k2 = jax.random.split(key)
            mask = jax.random.uniform(k1, (n, n)) < density
            sign = jnp.where(jax.random.uniform(k2, (n, n)) < 0.5, -1.0, 1.0)
            adj = jnp.where(mask, sign, 0.0).astype(jnp.float32)
            idx = jnp.arange(n)
            return adj.at[idx, idx].set(1.0)

        def _gru_cell(x, hstate, Wih, Whh, bih, bhh):
            gi = x @ Wih.T + bih
            gh = hstate @ Whh.T + bhh
            ir, iz, inn = jnp.split(gi, 3, axis=1)
            hr, hz, hn = jnp.split(gh, 3, axis=1)
            r = jax.nn.sigmoid(ir + hr)
            z = jax.nn.sigmoid(iz + hz)
            n = jnp.tanh(inn + r * hn)
            return (1.0 - z) * n + z * hstate

        def _gat_head(h, node_adj, edge_adj, W, a):
            hW = h @ W
            hp = (node_adj > 0).astype(hW.dtype) @ hW
            hm = (node_adj < 0).astype(hW.dtype) @ hW
            e_plus = jax.nn.leaky_relu(jnp.concatenate([hp, hm], axis=1) @ a, ALPHA)[:, 0]
            e_minus = jax.nn.leaky_relu(jnp.concatenate([hm, hp], axis=1) @ a, ALPHA)[:, 0]
            att = jnp.where(edge_adj > 0, e_plus[None, :], NEG_INF)
            att = jnp.where(edge_adj < 0, e_minus[None, :], att)
            att = jax.nn.softmax(att, axis=1)
            return att * edge_adj @ hW
        key = jax.random.key(seed)
        ks = jax.random.split(key, 16)
        std = 0.01
        gain = 1.414
        return {'h': jax.random.normal(ks[0], (N, H), jnp.float32), 'node_adj': _sign_adj(ks[1], N, 0.005), 'edge_adj': _sign_adj(ks[2], N, 0.005), 'gat_W': jax.random.normal(ks[3], (HEADS, H, H), jnp.float32) * (gain / np.sqrt(H, dtype=np.float32)), 'gat_a': jax.random.normal(ks[4], (HEADS, 2 * H, 1), jnp.float32) * 0.1, 'edge_Wih': jax.random.normal(ks[5], (3 * H, H), jnp.float32) * std, 'edge_Whh': jax.random.normal(ks[6], (3 * H, H), jnp.float32) * std, 'edge_bih': jnp.zeros((3 * H,), jnp.float32), 'edge_bhh': jnp.zeros((3 * H,), jnp.float32), 'node_Wih': jax.random.normal(ks[7], (3 * H, H), jnp.float32) * std, 'node_Whh': jax.random.normal(ks[8], (3 * H, H), jnp.float32) * std, 'node_bih': jnp.zeros((3 * H,), jnp.float32), 'node_bhh': jnp.zeros((3 * H,), jnp.float32)}
    _L0_gnn_all = _L0_gnn_setup()
    _L0_gnn_in = {k: v for k, v in _L0_gnn_all.items() if k in ('gat_W', 'gat_a', 'edge_Wih', 'edge_Whh', 'edge_bih', 'edge_bhh', 'node_Wih', 'node_Whh', 'node_bih', 'node_bhh')}
    del _L0_gnn_all

    def _L1_gnn_setup():
        import jax, jax.numpy as jnp
        import numpy as np
        N = 4096
        D_IN = 128
        D_OUT = 128
        key = jax.random.key(seed)
        k1, k2, k3 = jax.random.split(key, 3)
        x = jax.random.normal(k1, (N, D_IN), dtype=jnp.float32)
        adj = jax.random.uniform(k2, (N, N), dtype=jnp.float32)
        W = jax.random.normal(k3, (D_OUT, D_IN), dtype=jnp.float32) * (1.0 / np.sqrt(D_IN))
        return {'x': x, 'adj': adj, 'W': W}
    _L1_gnn_all = _L1_gnn_setup()
    _L1_gnn_in = {k: v for k, v in _L1_gnn_all.items() if k in ('W',)}
    del _L1_gnn_all
    return {'x': x, 'adj': adj, 'L0_gnn_gat_W': _L0_gnn_in['gat_W'], 'L0_gnn_gat_a': _L0_gnn_in['gat_a'], 'L0_gnn_edge_Wih': _L0_gnn_in['edge_Wih'], 'L0_gnn_edge_Whh': _L0_gnn_in['edge_Whh'], 'L0_gnn_edge_bih': _L0_gnn_in['edge_bih'], 'L0_gnn_edge_bhh': _L0_gnn_in['edge_bhh'], 'L0_gnn_node_Wih': _L0_gnn_in['node_Wih'], 'L0_gnn_node_Whh': _L0_gnn_in['node_Whh'], 'L0_gnn_node_bih': _L0_gnn_in['node_bih'], 'L0_gnn_node_bhh': _L0_gnn_in['node_bhh'], 'L1_gnn_W': _L1_gnn_in['W']}

def reference(x, adj, L0_gnn_gat_W, L0_gnn_gat_a, L0_gnn_edge_Wih, L0_gnn_edge_Whh, L0_gnn_edge_bih, L0_gnn_edge_bhh, L0_gnn_node_Wih, L0_gnn_node_Whh, L0_gnn_node_bih, L0_gnn_node_bhh, L1_gnn_W):
    import jax
    import jax.numpy as jnp

    def _L0_gnn_ref(h, node_adj, edge_adj, gat_W, gat_a, edge_Wih, edge_Whh, edge_bih, edge_bhh, node_Wih, node_Whh, node_bih, node_bhh):
        import jax, jax.numpy as jnp
        import numpy as np
        N, H, HEADS = (2048, 128, 3)
        ALPHA = 0.2
        NEG_INF = -9000000000000000.0

        def _sign_adj(key, n, density):
            k1, k2 = jax.random.split(key)
            mask = jax.random.uniform(k1, (n, n)) < density
            sign = jnp.where(jax.random.uniform(k2, (n, n)) < 0.5, -1.0, 1.0)
            adj = jnp.where(mask, sign, 0.0).astype(jnp.float32)
            idx = jnp.arange(n)
            return adj.at[idx, idx].set(1.0)

        def _gru_cell(x, hstate, Wih, Whh, bih, bhh):
            gi = x @ Wih.T + bih
            gh = hstate @ Whh.T + bhh
            ir, iz, inn = jnp.split(gi, 3, axis=1)
            hr, hz, hn = jnp.split(gh, 3, axis=1)
            r = jax.nn.sigmoid(ir + hr)
            z = jax.nn.sigmoid(iz + hz)
            n = jnp.tanh(inn + r * hn)
            return (1.0 - z) * n + z * hstate

        def _gat_head(h, node_adj, edge_adj, W, a):
            hW = h @ W
            hp = (node_adj > 0).astype(hW.dtype) @ hW
            hm = (node_adj < 0).astype(hW.dtype) @ hW
            e_plus = jax.nn.leaky_relu(jnp.concatenate([hp, hm], axis=1) @ a, ALPHA)[:, 0]
            e_minus = jax.nn.leaky_relu(jnp.concatenate([hm, hp], axis=1) @ a, ALPHA)[:, 0]
            att = jnp.where(edge_adj > 0, e_plus[None, :], NEG_INF)
            att = jnp.where(edge_adj < 0, e_minus[None, :], att)
            att = jax.nn.softmax(att, axis=1)
            return att * edge_adj @ hW
        dn = jnp.diag(node_adj)
        de = jnp.diag(edge_adj)
        idx = jnp.arange(node_adj.shape[0])
        node_adj_norm = node_adj.at[idx, idx].add(-dn)
        edge_adj_norm = edge_adj.at[idx, idx].add(-de)
        node_support = node_adj_norm @ h
        edge_output = _gru_cell(node_support, h, edge_Wih, edge_Whh, edge_bih, edge_bhh)
        edge_support = _gat_head(h, node_adj_norm, edge_adj_norm, gat_W[0], gat_a[0])
        for i in range(1, HEADS):
            edge_support = edge_support + _gat_head(h, node_adj_norm, edge_adj_norm, gat_W[i], gat_a[i])
        edge_support = edge_support / HEADS
        node_output = _gru_cell(edge_support, h, node_Wih, node_Whh, node_bih, node_bhh)
        return de[:, None] * edge_output + dn[:, None] * node_output

    def _L1_gnn_ref(x, adj, W):
        import jax, jax.numpy as jnp
        import numpy as np
        N = 4096
        D_IN = 128
        D_OUT = 128
        A_hat = adj + jnp.eye(adj.shape[0], dtype=adj.dtype)
        d_inv_sqrt = jnp.sum(A_hat, axis=1) ** (-0.5)
        A_norm = d_inv_sqrt[:, None] * A_hat * d_inv_sqrt[None, :]
        support = x @ W.T
        out = A_norm @ support
        return jax.nn.relu(out)
    x = _layernorm(x + _L0_gnn_ref(x, adj, adj, L0_gnn_gat_W, L0_gnn_gat_a, L0_gnn_edge_Wih, L0_gnn_edge_Whh, L0_gnn_edge_bih, L0_gnn_edge_bhh, L0_gnn_node_Wih, L0_gnn_node_Whh, L0_gnn_node_bih, L0_gnn_node_bhh), axis=-1)
    x = _layernorm(x + _L1_gnn_ref(x, adj, L1_gnn_W), axis=-1)
    return x

_drawn_inputs = setup_inputs


def setup_inputs(seed=0):
    import zlib

    import numpy as np

    out = dict(_drawn_inputs(seed))
    spreads = {'L0_gnn_edge_bih': (0.0, 0.369),
     'L0_gnn_edge_bhh': (0.0, 0.651),
     'L0_gnn_node_bih': (0.0, 0.388),
     'L0_gnn_node_bhh': (0.0, 0.615)}
    factors = {'L0_gnn_gat_W': 6.327,
     'L0_gnn_gat_a': 6.814,
     'L0_gnn_edge_Whh': 4.186,
     'L0_gnn_node_Wih': 6.328,
     'L0_gnn_node_Whh': 4.127}
    for name, (base, spread) in spreads.items():
        noise = np.random.default_rng([zlib.crc32(name.encode()), seed]).standard_normal(out[name].shape)
        drawn = base * np.exp(spread * noise) if base else spread * noise
        out[name] = jnp.asarray(drawn.astype(out[name].dtype))
    for name, factor in factors.items():
        out[name] = (out[name] * factor).astype(out[name].dtype)
    return out
```

```python
from contextlib import ExitStack

import numpy as np

import concourse.bass as bass
from concourse import mybir
from concourse.alu_op_type import AluOpType as ALU

F32 = mybir.dt.float32
BF16 = mybir.dt.bfloat16
I32 = mybir.dt.int32
ACT = mybir.ActivationFunctionType
AX_X = mybir.AxisListType.X

P = 128
N = 4096
H = 128
HEADS = 3
TILES = N // P
CHUNK = 512
CHUNKS = N // CHUNK
ROWS = CHUNK // P
GROUP = 4
GROUPS = TILES // GROUP
QUARTERS = 4
QUARTER = N // QUARTERS
SPLITS = 3
SCORES = 2 * HEADS
PARTS = 1 + SPLITS * SCORES
NEG, POS, NEG_DIAG, POS_DIAG = 0, 32, 64, 96
BIG = 1e30
ALPHA = 0.2
EPS = 1e-5


def memory(nc, stack):
    def sbuf(name, shape, dtype=F32):
        return stack.enter_context(nc.sbuf_tensor(name, shape, dtype))

    def psum(name, shape, dtype=F32):
        return stack.enter_context(nc.psum_tensor(name, shape, dtype))

    def semaphore(name):
        return stack.enter_context(nc.semaphore(name))

    return sbuf, psum, semaphore


def wait(engine, semaphore, count):
    if not isinstance(count, int) or count > 0:
        engine.wait_ge(semaphore, count)


def wait_apart(engine, semaphore, count, passed):
    wait(engine, semaphore, count)
    if not isinstance(count, int):
        engine.sem_inc(passed, 1)


def score_phase(nc, io, dram):
    with ExitStack() as stack:
        sbuf, psum, semaphore = memory(nc, stack)
        RING = 4
        x_rows = sbuf("p0_x_rows", [P, TILES, H])
        x_cols = sbuf("p0_x_cols", [H, N])
        w = sbuf("p0_w", [H, HEADS, H])
        a = sbuf("p0_a", [H, SCORES])
        wa = sbuf("p0_wa", [H, SCORES])
        wa_placed = sbuf("p0_wa_placed", [H, P])
        select = sbuf("p0_select", [P, SCORES])
        u = sbuf("p0_u", [P, TILES, SCORES])
        rest = sbuf("p0_rest", [P, 2, TILES, SCORES])
        u_parts = sbuf("p0_u_parts", [P, TILES, PARTS], BF16)
        diag_terms = sbuf("p0_diag_terms", [P, N])
        adj_t = sbuf("p0_adj_t", [P, RING, ROWS, GROUP, P])
        masks = sbuf("p0_masks", [P, 2, 2, ROWS, GROUP, P], BF16)
        diag = sbuf("p0_diag", [P, 2, CHUNK])
        diag_x = sbuf("p0_diag_x", [P, CHUNK])
        sums = sbuf("p0_sums", [P, 2, CHUNK])
        terms = sbuf("p0_terms", [P, 2, CHUNK])
        raw = sbuf("p0_raw", [SCORES, 2, CHUNK])
        scores = sbuf("p0_scores", [SCORES, 2, CHUNK])
        most = sbuf("p0_most", [1, CHUNK])
        flag = sbuf("p0_flag", [1, 1], I32)
        ps_sums = [psum(f"p0_ps_sums{i}", [P, CHUNK]) for i in range(2)]
        ps_masks = [psum(f"p0_ps_masks{i}", [P, CHUNK]) for i in range(2)]
        ps_scores = psum("p0_ps_scores", [P, CHUNK])
        ps_setup = psum("p0_ps_setup", [P, CHUNK])
        ps_diag = [psum(f"p0_ps_diag{i}", [P, CHUNK]) for i in range(2)]

        in_w = semaphore("p0_in_w")
        in_x = semaphore("p0_in_x")
        in_adj = [semaphore(f"p0_in_adj{i}") for i in range(RING)]
        in_diag = [semaphore(f"p0_in_diag{i}") for i in range(2)]
        wa_summed = semaphore("p0_wa_summed")
        wa_ready = semaphore("p0_wa_ready")
        u_summed = semaphore("p0_u_summed")
        u_step = semaphore("p0_u_step")
        u_ready = semaphore("p0_u_ready")
        cleared = semaphore("p0_cleared")
        diag_summed = semaphore("p0_diag_summed")
        diag_copied = semaphore("p0_diag_copied")
        masks_ready = semaphore("p0_masks_ready")
        group_done = semaphore("p0_group_done")
        sums_ready = semaphore("p0_sums_ready")
        diag_x_ready = semaphore("p0_diag_x_ready")
        terms_ready = semaphore("p0_terms_ready")
        scores_summed = semaphore("p0_scores_summed")
        raw_ready = semaphore("p0_raw_ready")
        scores_ready = semaphore("p0_scores_ready")
        most_ready = semaphore("p0_most_ready")
        out_sums = [semaphore(f"p0_out_sums{i}") for i in range(2)]
        out_scores = [semaphore(f"p0_out_scores{i}") for i in range(2)]
        flag_ready = semaphore("p0_flag_ready")
        out_flag = semaphore("p0_out_flag")

        block = stack.enter_context(nc.Block())

        @block.sync
        def _(sync):
            sync.dma_start(w[:], io["w_t"]).then_inc(in_w, 16)
            sync.dma_start(a[:], io["a"]).then_inc(in_w, 16)
            sync.dma_start(select[:], io["select"]).then_inc(in_w, 16)
            sync.dma_start(x_cols[:], io["x_cols"]).then_inc(in_x, 16)
            sync.dma_start(x_rows[:], io["x"].rearrange("(t p) h -> p t h", p=P)).then_inc(in_x, 16)

            def load_chunk(c):
                for g in range(GROUPS):
                    slot = g % RING
                    wait(sync, group_done, GROUPS * c + g - RING + 1)
                    wait(sync, masks_ready, GROUPS * c + g - RING + 1)
                    sync.dma_start(
                        adj_t[:, slot],
                        io["adj_t"][bass.ds(c * ROWS, ROWS), :, g * GROUP:(g + 1) * GROUP, :]
                        .rearrange("j p c r -> p j c r")).then_inc(in_adj[slot], 16)

            load_chunk(0)
            with sync.Fori(1, CHUNKS) as c:
                load_chunk(c)
            sync.wait_ge(flag_ready, 1)
            sync.dma_start(dram["flag"], flag[:]).then_inc(out_flag, 16)
            sync.wait_ge(out_flag, 16)

        @block.scalar
        def _(act):
            for half in range(2):
                act.dma_start(diag[:, half], io["diag_row"][:, half * CHUNK:(half + 1) * CHUNK]
                              .broadcast_to([P, CHUNK])).then_inc(in_diag[half], 16)
            act.wait_ge(wa_summed, 1)
            nc.scalar.copy(wa[:], ps_setup[:, 0:SCORES]).then_inc(wa_ready, 1)
            for c in range(CHUNKS):
                act.wait_ge(diag_summed, c + 1)
                nc.scalar.copy(diag_terms[:, c * CHUNK:(c + 1) * CHUNK], ps_diag[c % 2][:]) \
                  .then_inc(diag_copied, 1)

            def chunk_pair(i, last):
                for half in range(2):
                    c = 2 * i + half
                    act.wait_ge(scores_summed, c + 1)
                    wait(act, scores_ready, c - 1)
                    nc.scalar.copy(raw[:, half], ps_scores[0:SCORES, :]).then_inc(raw_ready, 1)
                    act.wait_ge(sums_ready, c + 1)
                    act.dma_start(dram["sums"][:, bass.ds(c * CHUNK, CHUNK)], sums[:, half]) \
                       .then_inc(out_sums[half], 16)
                    act.wait_ge(scores_ready, c + 1)
                    act.dma_start(dram["scores"][:, bass.ds(c * CHUNK, CHUNK)], scores[:, half]) \
                       .then_inc(out_scores[half], 16)
                    if not last:
                        act.dma_start(diag[:, half], io["diag_row"][:, bass.ds((c + 2) * CHUNK, CHUNK)]
                                      .broadcast_to([P, CHUNK])).then_inc(in_diag[half], 16)

            chunk_pair(0, False)
            with act.Fori(1, CHUNKS // 2 - 1) as i:
                chunk_pair(i, False)
            chunk_pair(CHUNKS // 2 - 1, True)
            for half in range(2):
                act.wait_ge(out_sums[half], 16 * CHUNKS // 2)
                act.wait_ge(out_scores[half], 16 * CHUNKS // 2)

        @block.vector
        def _(dve):
            nc.vector.memset(terms[:], 0.0).then_inc(cleared, 1)
            nc.vector.memset(wa_placed[:], 0.0).then_inc(cleared, 1)
            nc.vector.memset(u_parts[:, :, 0:1], 1.0).then_inc(cleared, 1)
            nc.vector.memset(most[:], 0.0).then_inc(cleared, 1)
            dve.wait_ge(wa_ready, 1)
            dve.wait_ge(cleared, 4)
            for at in (NEG_DIAG, POS_DIAG):
                nc.vector.tensor_copy(wa_placed[:, at:at + SCORES], wa[:]).then_inc(wa_ready, 1)
            dve.wait_ge(u_summed, 1)
            nc.vector.tensor_copy(u[:], ps_setup[:, 0:TILES * SCORES]
                                  .rearrange("p (t s) -> p t s", s=SCORES)).then_inc(u_step, 1)
            dve.wait_ge(u_step, 1)
            source = u[:]
            for s in range(SPLITS):
                part = u_parts[:, :, 1 + s * SCORES:1 + (s + 1) * SCORES]
                nc.vector.tensor_copy(part, source).then_inc(u_step, 1)
                dve.wait_ge(u_step, 2 * s + 2)
                if s < SPLITS - 1:
                    nc.vector.tensor_tensor(rest[:, s], source, part, ALU.subtract).then_inc(u_step, 1)
                    dve.wait_ge(u_step, 2 * s + 3)
                    source = rest[:, s]
            nc.vector.tensor_copy(flag[:], most[:, 0:1]).then_inc(u_ready, 1)

            def chunk_pair(i):
                for half in range(2):
                    c = 2 * i + half
                    for g in range(GROUPS):
                        slot = g % RING
                        n = GROUPS * c + g
                        dve.wait_ge(in_adj[slot], 16 * (GROUPS // RING * c + g // RING + 1))
                        wait(dve, group_done, n - 1)
                        nc.vector.tensor_scalar(masks[:, g % 2, 0], adj_t[:, slot], 0.0, None, ALU.is_lt)
                        nc.vector.tensor_scalar(masks[:, g % 2, 1], adj_t[:, slot], 0.0, None, ALU.is_gt) \
                          .then_inc(masks_ready, 1)
                    dve.wait_ge(in_diag[half], 16 * (i + 1))
                    wait(dve, diag_copied, CHUNKS)
                    wait(dve, scores_summed, c - 1)
                    for at, sign in ((NEG_DIAG, ALU.is_lt), (POS_DIAG, ALU.is_gt)):
                        nc.vector.scalar_tensor_tensor(
                            terms[at:at + SCORES, half], diag[at:at + SCORES, half], 0.0,
                            diag_terms[at:at + SCORES, bass.ds(c * CHUNK, CHUNK)], sign, ALU.mult)
                    dve.wait_ge(group_done, GROUPS * (c + 1))
                    nc.vector.tensor_copy(terms[POS:POS + PARTS, half], ps_masks[half][POS:POS + PARTS, :])
                    nc.vector.tensor_copy(terms[NEG:NEG + PARTS, half], ps_masks[half][NEG:NEG + PARTS, :]) \
                      .then_inc(terms_ready, 1)
                    dve.wait_ge(terms_ready, c + 1)
                    wait(dve, most_ready, c)
                    nc.vector.tensor_tensor(most[:], most[:], terms[NEG:NEG + 1, half], ALU.max) \
                      .then_inc(most_ready, 1)
                    nc.vector.tensor_tensor(diag_x[:], diag[:, half], x_cols[:, bass.ds(c * CHUNK, CHUNK)],
                                            ALU.mult).then_inc(diag_x_ready, 1)
                    dve.wait_ge(diag_x_ready, c + 1)
                    wait(dve, out_sums[half], 16 * i)
                    nc.vector.tensor_tensor(sums[:, half], ps_sums[half][:], diag_x[:], ALU.subtract) \
                      .then_inc(sums_ready, 1)
                    dve.wait_ge(raw_ready, c + 1)
                    wait(dve, out_scores[half], 16 * i)
                    nc.vector.scalar_tensor_tensor(scores[:, half], raw[:, half], ALPHA, raw[:, half],
                                                   ALU.mult, ALU.min).then_inc(scores_ready, 1)

            dve.wait_ge(in_x, 32)
            chunk_pair(0)
            with dve.Fori(1, CHUNKS // 2) as i:
                chunk_pair(i)
            dve.wait_ge(most_ready, CHUNKS)
            nc.vector.tensor_reduce(flag[:], most[:], AX_X, ALU.max).then_inc(flag_ready, 1)

        @block.tensor
        def _(pe):
            pe.wait_ge(in_w, 48)
            for h in range(HEADS):
                last = nc.tensor.matmul(ps_setup[:, 2 * h:2 * h + 2], w[:, h, :], a[:, 2 * h:2 * h + 2],
                                        start=True, stop=True)
            last.then_inc(wa_summed, 1)
            pe.wait_ge(in_x, 32)
            pe.wait_ge(wa_ready, 3)
            for t in range(TILES):
                last = nc.tensor.matmul(ps_setup[:, t * SCORES:(t + 1) * SCORES],
                                        x_cols[:, t * P:(t + 1) * P], wa[:], start=True, stop=True)
            last.then_inc(u_summed, 1)
            for c in range(CHUNKS):
                wait(pe, diag_copied, c - 1)
                nc.tensor.matmul(ps_diag[c % 2][:], wa_placed[:], x_cols[:, c * CHUNK:(c + 1) * CHUNK],
                                 start=True, stop=True).then_inc(diag_summed, 1)
            pe.wait_ge(u_ready, 1)

            def chunk_pair(i):
                for half in range(2):
                    c = 2 * i + half
                    wait(pe, sums_ready, c - 1)
                    wait(pe, terms_ready, c - 1)
                    for g in range(GROUPS):
                        slot = g % RING
                        pe.wait_ge(in_adj[slot], 16 * (GROUPS // RING * c + g // RING + 1))
                        pe.wait_ge(masks_ready, GROUPS * c + g + 1)
                        for k in range(GROUP):
                            t = g * GROUP + k
                            first, final = t == 0, t == TILES - 1
                            nc.tensor.matmul(ps_sums[half][:], x_rows[:, t, :], adj_t[:, slot, :, k, :],
                                             start=first, stop=final)
                            nc.tensor.matmul(ps_masks[half][NEG:NEG + PARTS, :], u_parts[:, t, :],
                                             masks[:, g % 2, 0, :, k, :], start=first, stop=final)
                            last = nc.tensor.matmul(ps_masks[half][POS:POS + PARTS, :], u_parts[:, t, :],
                                                    masks[:, g % 2, 1, :, k, :], start=first, stop=final)
                        last.then_inc(group_done, 1)
                    pe.wait_ge(terms_ready, c + 1)
                    wait(pe, raw_ready, c)
                    nc.tensor.matmul(ps_scores[0:SCORES, :], select[:], terms[:, half],
                                     start=True, stop=True).then_inc(scores_summed, 1)

            chunk_pair(0)
            with pe.Fori(1, CHUNKS // 2) as i:
                chunk_pair(i)


def attention_phase(nc, io, dram):
    with ExitStack() as stack:
        sbuf, psum, semaphore = memory(nc, stack)
        STAGES = QUARTERS
        RING = 4
        x_rows = sbuf("p1_x_rows", [P, TILES, H])
        neg_e = sbuf("p1_neg_e", [P, HEADS, N])
        identity = sbuf("p1_identity", [P, P])
        big_diag = sbuf("p1_big_diag", [P, P], BF16)
        w = sbuf("p1_w", [H, HEADS, H])
        stage = sbuf("p1_stage", [P, STAGES, QUARTER])
        spare = sbuf("p1_spare", [P, QUARTER], BF16)
        absent = sbuf("p1_absent", [P, 2, N], BF16)
        att = sbuf("p1_att", [P, 2, HEADS, N])
        adj_t = sbuf("p1_adj_t", [P, RING, GROUP, P])
        weighted = sbuf("p1_weighted", [P, 2, GROUP, HEADS, P])
        least = sbuf("p1_least", [P, 2, HEADS, QUARTERS])
        total = sbuf("p1_total", [P, 2, HEADS])
        inverse = sbuf("p1_inverse", [P, 2, 2, HEADS])
        row_parts = sbuf("p1_row_parts", [P, QUARTERS, TILES])
        gathered = sbuf("p1_gathered", [H, HEADS, P])
        by_head = sbuf("p1_by_head", [P, HEADS, H])
        pair_sum = sbuf("p1_pair_sum", [P, H])
        support = sbuf("p1_support", [P, H])
        support_t = sbuf("p1_support_t", [H, 2, P])
        ps_att = [psum(f"p1_ps_att{i}", [P, GROUP, HEADS, P]) for i in range(2)]
        ps_gathered = psum("p1_ps_gathered", [P, CHUNK])
        ps_support = psum("p1_ps_support", [P, CHUNK])

        in_const = semaphore("p1_in_const")
        in_e = semaphore("p1_in_e")
        in_stage = [semaphore(f"p1_in_stage{i}") for i in range(STAGES)]
        in_adj = [semaphore(f"p1_in_adj{i}") for i in range(RING)]
        rows_summed = semaphore("p1_rows_summed")
        quarter_masked = semaphore("p1_quarter_masked")
        absent_ready = semaphore("p1_absent_ready")
        masked = semaphore("p1_masked")
        att_ready = semaphore("p1_att_ready")
        turned = semaphore("p1_turned")
        weighted_ready = semaphore("p1_weighted_ready")
        gathered_part = semaphore("p1_gathered_part")
        gathered_ready = semaphore("p1_gathered_ready")
        inverse_step = semaphore("p1_inverse_step")
        inverse_ready = semaphore("p1_inverse_ready")
        head_summed = semaphore("p1_head_summed")
        by_head_ready = semaphore("p1_by_head_ready")
        pair_ready = semaphore("p1_pair_ready")
        support_ready = semaphore("p1_support_ready")
        support_turned = semaphore("p1_support_turned")
        support_copied = semaphore("p1_support_copied")
        out_support = [semaphore(f"p1_out_support{i}") for i in range(2)]
        out_rows = semaphore("p1_out_rows")
        passed = semaphore("p1_passed")

        block = stack.enter_context(nc.Block())

        @block.sync
        def _(sync):
            sync.dma_start(identity[:], io["identity"]).then_inc(in_const, 16)
            sync.dma_start(w[:], io["w"]).then_inc(in_const, 16)

            def load_tile(t):
                for q in range(QUARTERS):
                    wait(sync, rows_summed, QUARTERS * (t - 1) + q + 1)
                    wait(sync, quarter_masked, QUARTERS * (t - 1) + q + 1)
                    sync.dma_start(stage[:, q], io["adj"][bass.ds(t * P, P), q * QUARTER:(q + 1) * QUARTER]) \
                        .then_inc(in_stage[q], 16)

            def load_turned(t):
                for g in range(GROUPS):
                    slot = g % RING
                    wait(sync, weighted_ready, GROUPS * t + g - RING + 1)
                    sync.dma_start(
                        adj_t[:, slot],
                        io["adj_t"][bass.ds(t, 1), :, g * GROUP:(g + 1) * GROUP, :]
                        .rearrange("j p c r -> p (j c) r")).then_inc(in_adj[slot], 16)

            load_tile(0)
            for h in range(HEADS):
                sync.dma_start(neg_e[:, h, :], dram["scores"][h:h + 1, :].broadcast_to([P, N])) \
                    .then_inc(in_e, 16)
            sync.dma_start(x_rows[:], io["x"].rearrange("(t p) h -> p t h", p=P)).then_inc(in_const, 16)
            load_tile(1)
            load_turned(0)
            with sync.Fori(1, TILES - 1) as t:
                load_tile(t + 1)
                load_turned(t)
            load_turned(TILES - 1)

        @block.gpsimd
        def _(pool):
            pool.wait_ge(in_const, 48)
            nc.gpsimd.tensor_scalar(big_diag[:], identity[:], BIG, None, ALU.mult).then_inc(support_ready, 1)
            pool.wait_ge(support_ready, 1)

            def mask_tile(t, slot):
                wait(pool, masked, QUARTERS * HEADS * (t - 1))
                for q in range(QUARTERS):
                    wait_apart(pool, in_stage[q], 16 * (t + 1), passed)
                    nc.gpsimd.tensor_scalar(absent[:, slot, q * QUARTER:(q + 1) * QUARTER], stage[:, q],
                                            0.0, BIG, ALU.is_le, ALU.mult).then_inc(quarter_masked, 1)
                pool.wait_ge(quarter_masked, QUARTERS * (t + 1))
                own = absent[:, slot, bass.ds(t * P, P)]
                nc.gpsimd.tensor_tensor(own, own, big_diag[:], ALU.add).then_inc(absent_ready, 1)

            def add_heads(t):
                pool.wait_ge(by_head_ready, t + 1)
                nc.gpsimd.tensor_tensor(pair_sum[:], by_head[:, 0], by_head[:, 1], ALU.add) \
                  .then_inc(pair_ready, 1)
                pool.wait_ge(pair_ready, t + 1)
                wait(pool, support_turned, t)
                nc.gpsimd.tensor_tensor(support[:], pair_sum[:], by_head[:, 2], ALU.add) \
                  .then_inc(support_ready, 1)

            def pair(i, last):
                for slot in range(2):
                    t = 2 * i + slot
                    if not (last and slot):
                        mask_tile(t + 1, 1 - slot)
                    add_heads(t)

            mask_tile(0, 0)
            pair(0, False)
            with pool.Fori(1, TILES // 2 - 1) as i:
                pair(i, False)
            pair(TILES // 2 - 1, True)

        @block.scalar
        def _(act):
            def attend(t, slot):
                for q in range(QUARTERS):
                    act.wait_ge(in_stage[q], 16 * (t + 1))
                    wait(act, rows_summed, QUARTERS * t + q)
                    nc.scalar.activation(spare[:], stage[:, q], ACT.Copy,
                                         accum_out=row_parts[:, q, bass.ds(t, 1)]).then_inc(rows_summed, 1)
                wait(act, inverse_ready, t - 1)
                for h in range(HEADS):
                    act.wait_ge(masked, QUARTERS * HEADS * t + QUARTERS * (h + 1))
                    nc.scalar.activation(att[:, slot, h, :], att[:, slot, h, :], ACT.Exp,
                                         bias=least[:, slot, h, QUARTERS - 1:QUARTERS], scale=-1.0,
                                         accum_out=total[:, slot, h:h + 1]).then_inc(att_ready, 1)

            def finish(t, slot):
                act.wait_ge(gathered_part, GROUPS * (t + 1))
                nc.scalar.copy(gathered[:], ps_gathered[:, 0:HEADS * P]
                               .rearrange("p (h r) -> p h r", h=HEADS)).then_inc(gathered_ready, 1)
                act.wait_ge(head_summed, t + 1)
                act.wait_ge(inverse_ready, t + 1)
                wait(act, support_ready, t + 1)
                for h in range(HEADS):
                    last = nc.scalar.activation(by_head[:, h], ps_support[:, h * P:(h + 1) * P], ACT.Copy,
                                                scale=inverse[:, slot, 1, h:h + 1])
                last.then_inc(by_head_ready, 1)
                act.wait_ge(support_turned, t + 1)
                wait(act, out_support[slot], 8 * (t - slot))
                nc.scalar.copy(support_t[:, slot], ps_support[:, HEADS * P:(HEADS + 1) * P]) \
                  .then_inc(support_copied, 1)
                act.wait_ge(support_copied, t + 1)
                act.dma_start(dram["support"][:, bass.ds(t * P, P)], support_t[:, slot]) \
                   .then_inc(out_support[slot], 16)

            def pair(i, last):
                for slot in range(2):
                    t = 2 * i + slot
                    if not (last and slot):
                        attend(t + 1, 1 - slot)
                    finish(t, slot)

            attend(0, 0)
            pair(0, False)
            with act.Fori(1, TILES // 2 - 1) as i:
                pair(i, False)
            pair(TILES // 2 - 1, True)
            act.wait_ge(rows_summed, QUARTERS * TILES)
            act.dma_start(dram["row_parts"], row_parts[:]).then_inc(out_rows, 16)
            act.wait_ge(out_rows, 16)
            for slot in range(2):
                act.wait_ge(out_support[slot], 16 * TILES // 2)

        @block.vector
        def _(dve):
            def mask_scores(t, slot, k):
                h, q = divmod(k, QUARTERS)
                if k == 0:
                    dve.wait_ge(absent_ready, t + 1)
                    wait(dve, turned, GROUPS * (t - 1))
                    wait_apart(dve, att_ready, HEADS * (t - 1), passed)
                if q:
                    wait_apart(dve, masked, QUARTERS * HEADS * t + k, passed)
                cut = slice(q * QUARTER, (q + 1) * QUARTER)
                nc.vector.tensor_tensor_reduce(
                    out=att[:, slot, h, cut], in0=absent[:, slot, cut], in1=neg_e[:, h, cut],
                    scale=1.0, scalar=least[:, slot, h, q - 1:q] if q else 3e38,
                    op0=ALU.add, op1=ALU.min, accum_out=least[:, slot, h, q:q + 1]).then_inc(masked, 1)

            def weigh(t, g):
                n = GROUPS * t + g
                slot = g % RING
                dve.wait_ge(turned, n + 1)
                dve.wait_ge(in_adj[slot], 16 * (GROUPS // RING * t + g // RING + 1))
                wait(dve, gathered_part, n - 1)
                tile = adj_t[:, slot]
                nc.vector.tensor_tensor(weighted[:, g % 2], ps_att[g % 2][:],
                                        tile.unsqueeze(2).broadcast_to([P, GROUP, HEADS, P]), ALU.mult) \
                  .then_inc(weighted_ready, 1)

            def invert(t, slot):
                dve.wait_ge(att_ready, HEADS * (t + 1))
                wait(dve, by_head_ready, t - 1)
                nc.vector.tensor_scalar(inverse[:, slot, 0], total[:, slot], float(HEADS), None, ALU.mult) \
                  .then_inc(inverse_step, 1)
                dve.wait_ge(inverse_step, t + 1)
                nc.vector.reciprocal(inverse[:, slot, 1], inverse[:, slot, 0]).then_inc(inverse_ready, 1)

            def pair(i, last):
                for slot in range(2):
                    t = 2 * i + slot
                    k = 0
                    for g in range(GROUPS):
                        weigh(t, g)
                        if g == 0:
                            invert(t, slot)
                        if last and slot:
                            continue
                        for _ in range(1 + g % 2):
                            mask_scores(t + 1, 1 - slot, k)
                            k += 1

            dve.wait_ge(in_e, 16 * HEADS)
            for k in range(QUARTERS * HEADS):
                mask_scores(0, 0, k)
            pair(0, False)
            with dve.Fori(1, TILES // 2 - 1) as i:
                pair(i, False)
            pair(TILES // 2 - 1, True)

        @block.tensor
        def _(pe):
            def turn(t, slot, g):
                n = GROUPS * t + g
                if g == 0:
                    pe.wait_ge(att_ready, HEADS * (t + 1))
                wait(pe, weighted_ready, n - 1)
                for k in range(GROUP):
                    c = g * GROUP + k
                    for h in range(HEADS):
                        last = nc.tensor.transpose(ps_att[g % 2][:, k, h, :],
                                                   att[:, slot, h, c * P:(c + 1) * P], identity[:])
                last.then_inc(turned, 1)

            def gather(t, g):
                pe.wait_ge(weighted_ready, GROUPS * t + g + 1)
                if g == 0:
                    wait(pe, gathered_ready, t)
                for k in range(GROUP):
                    c = g * GROUP + k
                    last = nc.tensor.matmul(ps_gathered[:, 0:HEADS * P], x_rows[:, c, :],
                                            weighted[:, g % 2, k].rearrange("p h r -> p (h r)"),
                                            start=c == 0, stop=c == TILES - 1)
                last.then_inc(gathered_part, 1)

            def project(t):
                pe.wait_ge(gathered_ready, t + 1)
                wait(pe, support_copied, t)
                for h in range(HEADS):
                    last = nc.tensor.matmul(ps_support[:, h * P:(h + 1) * P], gathered[:, h, :], w[:, h, :],
                                            start=True, stop=True)
                last.then_inc(head_summed, 1)

            def turn_support(t):
                pe.wait_ge(support_ready, t + 2)
                nc.tensor.transpose(ps_support[:, HEADS * P:(HEADS + 1) * P], support[:], identity[:]) \
                  .then_inc(support_turned, 1)

            def pair(i, first, last):
                for slot in range(2):
                    t = 2 * i + slot
                    for g in range(GROUPS):
                        if g < GROUPS - 1:
                            turn(t, slot, g + 1)
                        elif not (last and slot):
                            turn(t + 1, 1 - slot, 0)
                        gather(t, g)
                        if not (first and slot == 0):
                            if g == 0:
                                project(t - 1)
                            if g == 3:
                                turn_support(t - 1)

            pe.wait_ge(in_const, 48)
            turn(0, 0, 0)
            pair(0, True, False)
            with pe.Fori(1, TILES // 2 - 1) as i:
                pair(i, False, False)
            pair(TILES // 2 - 1, False, True)
            project(TILES - 1)
            turn_support(TILES - 1)


def update_phase(nc, io, dram):
    with ExitStack() as stack:
        sbuf, psum, semaphore = memory(nc, stack)
        GATES = 3
        CELLS = 2
        w_in = sbuf("p2_w_in", [H, CELLS, GATES, H])
        w_state = sbuf("p2_w_state", [H, CELLS, GATES, H])
        bias_in = sbuf("p2_bias_in", [H, CELLS, GATES])
        bias_state = sbuf("p2_bias_state", [H, CELLS, GATES])
        bias_sum = sbuf("p2_bias_sum", [H, CELLS, GATES])
        bias_half = sbuf("p2_bias_half", [H, CELLS, GATES])
        bias_state_half = sbuf("p2_bias_state_half", [H, CELLS, GATES])
        identity = sbuf("p2_identity", [P, P])
        diag = sbuf("p2_diag", [P, TILES])
        support = sbuf("p2_support", [H, 2, CELLS, CHUNK])
        state = sbuf("p2_state", [H, 2, CHUNK])
        x_rows = sbuf("p2_x_rows", [P, TILES, H])
        reset = sbuf("p2_reset", [H, CHUNK])
        update = sbuf("p2_update", [H, CHUNK])
        half_state = sbuf("p2_half_state", [H, CHUNK])
        gated = sbuf("p2_gated", [H, CHUNK])
        pre = sbuf("p2_pre", [H, CHUNK])
        new = sbuf("p2_new", [H, CHUNK])
        change = sbuf("p2_change", [H, CHUNK])
        scaled = sbuf("p2_scaled", [H, CHUNK])
        cell_out = sbuf("p2_cell_out", [H, CELLS, CHUNK])
        both = sbuf("p2_both", [H, CHUNK])
        mixed = sbuf("p2_mixed", [P, TILES, H])
        stats = sbuf("p2_stats", [P, TILES, nc.vector.BN_STATS_DIM])
        moments = sbuf("p2_moments", [P, TILES, 2])
        row_parts = sbuf("p2_row_parts", [P, QUARTERS, TILES])
        row_sum = sbuf("p2_row_sum", [P, 3, TILES])
        roots = sbuf("p2_roots", [P, 2, TILES])
        inverse = sbuf("p2_inverse", [P, 2, TILES])
        variance = sbuf("p2_variance", [P, TILES])
        gates = [[psum(f"p2_gate{c}{g}", [P, CHUNK]) for g in range(4)] for c in range(CELLS)]

        in_const = semaphore("p2_in_const")
        in_chunk = [semaphore(f"p2_in_chunk{i}") for i in range(2)]
        bias_step = semaphore("p2_bias_step")
        bias_ready = semaphore("p2_bias_ready")
        gates_summed = semaphore("p2_gates_summed")
        act_gates = semaphore("p2_act_gates")
        gated_ready = semaphore("p2_gated_ready")
        pre_ready = semaphore("p2_pre_ready")
        new_ready = semaphore("p2_new_ready")
        change_ready = semaphore("p2_change_ready")
        scaled_ready = semaphore("p2_scaled_ready")
        cell_ready = semaphore("p2_cell_ready")
        both_ready = semaphore("p2_both_ready")
        both_turned = semaphore("p2_both_turned")
        mixed_ready = semaphore("p2_mixed_ready")
        stats_ready = semaphore("p2_stats_ready")
        moments_ready = semaphore("p2_moments_ready")
        end_step = semaphore("p2_end_step")
        roots_ready = semaphore("p2_roots_ready")
        inverse_ready = semaphore("p2_inverse_ready")
        normed = semaphore("p2_normed")
        scaled_x = semaphore("p2_scaled_x")
        out_x = semaphore("p2_out_x")
        passed = semaphore("p2_passed")

        block = stack.enter_context(nc.Block())

        @block.sync
        def _(sync):
            for c, cell in enumerate(("edge", "node")):
                sync.dma_start(w_in[:, c], io[f"{cell}_w_in"]).then_inc(in_const, 16)
                sync.dma_start(w_state[:, c], io[f"{cell}_w_state"]).then_inc(in_const, 16)
                sync.dma_start(bias_in[:, c], io[f"{cell}_bias_in"]).then_inc(in_const, 16)
                sync.dma_start(bias_state[:, c], io[f"{cell}_bias_state"]).then_inc(in_const, 16)
            sync.dma_start(identity[:], io["identity"]).then_inc(in_const, 16)
            sync.dma_start(diag[:], io["diag_cols"]).then_inc(in_const, 16)
            sync.dma_start(row_parts[:], dram["row_parts"]).then_inc(in_const, 16)
            sync.dma_start(x_rows[:], io["x"].rearrange("(t p) h -> p t h", p=P)).then_inc(in_const, 16)

            def pair(i):
                for half in range(2):
                    c = 2 * i + half
                    wait(sync, cell_ready, 2 * (c - 1))
                    wait(sync, gates_summed, 2 * (c - 1))
                    wait(sync, change_ready, 2 * (c - 1))
                    at = bass.ds(c * CHUNK, CHUNK)
                    sync.dma_start(support[:, half, 0], dram["sums"][:, at]).then_inc(in_chunk[half], 16)
                    sync.dma_start(support[:, half, 1], dram["support"][:, at]).then_inc(in_chunk[half], 16)
                    sync.dma_start(state[:, half], io["x_cols"][:, at]).then_inc(in_chunk[half], 16)

            pair(0)
            with sync.Fori(1, CHUNKS // 2) as i:
                pair(i)
            sync.wait_ge(normed, TILES)
            sync.dma_start(dram["x1"], mixed[:]).then_inc(out_x, 16)
            sync.wait_ge(scaled_x, TILES)
            sync.dma_start(dram["x1_scaled"], x_rows[:]).then_inc(out_x, 16)
            sync.wait_ge(out_x, 32)

        @block.gpsimd
        def _(pool):
            def cell(n, half):
                pool.wait_ge(new_ready, n + 1)
                wait(pool, scaled_ready, n)
                nc.gpsimd.tensor_tensor(change[:], state[:, half], new[:], ALU.subtract) \
                  .then_inc(change_ready, 1)

            def pair(i):
                for half in range(2):
                    for k in range(CELLS):
                        cell(CELLS * (2 * i + half) + k, half)
                    c = 2 * i + half
                    pool.wait_ge(cell_ready, CELLS * (c + 1))
                    wait(pool, both_turned, c)
                    nc.gpsimd.tensor_tensor(both[:], cell_out[:, 0], cell_out[:, 1], ALU.add) \
                      .then_inc(both_ready, 1)

            pool.wait_ge(in_chunk[0], 48)
            pool.wait_ge(in_chunk[1], 48)
            pair(0)
            with pool.Fori(1, CHUNKS // 2) as i:
                for half in range(2):
                    pool.wait_ge(in_chunk[half], 48 * (i + 1))
                pair(i)

        @block.scalar
        def _(act):
            act.wait_ge(bias_ready, 1)

            def cell(n, k):
                ps = gates[k]
                act.wait_ge(gates_summed, n + 1)
                wait(act, gated_ready, n)
                wait(act, scaled_ready, n)
                nc.scalar.activation(reset[:], ps[0][:], ACT.Tanh, bias=bias_half[:, k, 0:1], scale=0.5)
                nc.scalar.activation(half_state[:], ps[3][:], ACT.Identity,
                                     bias=bias_state_half[:, k, 2:3], scale=0.5)
                nc.scalar.activation(update[:], ps[1][:], ACT.Tanh, bias=bias_half[:, k, 1:2], scale=0.5) \
                  .then_inc(act_gates, 1)
                act.wait_ge(pre_ready, n + 1)
                wait(act, change_ready, n)
                wait(act, cell_ready, n)
                nc.scalar.activation(new[:], pre[:], ACT.Tanh, bias=bias_in[:, k, 2:3]) \
                  .then_inc(new_ready, 1)

            for k in range(CELLS):
                cell(k, k)
            with act.Fori(1, CHUNKS) as c:
                for k in range(CELLS):
                    cell(CELLS * c + k, k)
            act.wait_ge(end_step, 5)
            nc.scalar.activation(roots[:, 0], variance[:], ACT.Sqrt)
            nc.scalar.activation(roots[:, 1], row_sum[:, 2], ACT.Sqrt).then_inc(roots_ready, 1)
            act.wait_ge(inverse_ready, 1)
            for t in range(TILES):
                act.wait_ge(normed, t + 1)
                nc.scalar.activation(x_rows[:, t], mixed[:, t], ACT.Copy, scale=inverse[:, 1, t:t + 1]) \
                  .then_inc(scaled_x, 1)

        @block.vector
        def _(dve):
            dve.wait_ge(in_const, 16 * 12)
            nc.vector.tensor_tensor(bias_sum[:], bias_in[:], bias_state[:], ALU.add).then_inc(bias_step, 1)
            nc.vector.tensor_scalar(bias_state_half[:], bias_state[:], 0.5, None, ALU.mult)
            dve.wait_ge(bias_step, 1)
            nc.vector.tensor_scalar(bias_half[:], bias_sum[:], 0.5, None, ALU.mult).then_inc(bias_ready, 1)

            def cell(c, n, k):
                ps = gates[k]
                dve.wait_ge(act_gates, n + 1)
                nc.vector.scalar_tensor_tensor(gated[:], reset[:], 1.0, half_state[:], ALU.add, ALU.mult) \
                  .then_inc(gated_ready, 1)
                dve.wait_ge(gated_ready, n + 1)
                wait(dve, new_ready, n)
                nc.vector.tensor_tensor(pre[:], ps[2][:], gated[:], ALU.add).then_inc(pre_ready, 1)
                dve.wait_ge(change_ready, n + 1)
                nc.vector.scalar_tensor_tensor(scaled[:], update[:], 1.0, change[:], ALU.add, ALU.mult) \
                  .then_inc(scaled_ready, 1)
                dve.wait_ge(scaled_ready, n + 1)
                wait(dve, both_ready, c)
                nc.vector.scalar_tensor_tensor(cell_out[:, k], scaled[:], 0.5, new[:], ALU.mult, ALU.add) \
                  .then_inc(cell_ready, 1)

            def chunk(c):
                for k in range(CELLS):
                    cell(c, CELLS * c + k, k)
                dve.wait_ge(both_turned, c + 1)
                turned = gates[0][0][:].rearrange("p (j h) -> p j h", j=ROWS)
                for j in range(ROWS):
                    last = nc.vector.scalar_tensor_tensor(
                        mixed[:, bass.ds(c * ROWS + j, 1), :].rearrange("p j h -> p (j h)"),
                        turned[:, j], diag[:, bass.ds(c * ROWS + j, 1)],
                        x_rows[:, bass.ds(c * ROWS + j, 1), :].rearrange("p j h -> p (j h)"),
                        ALU.mult, ALU.add)
                last.then_inc(mixed_ready, 1)
                wait_apart(dve, mixed_ready, c + 1, passed)
                for j in range(ROWS):
                    last = nc.vector.bn_stats(
                        stats[:, bass.ds(c * ROWS + j, 1), :].rearrange("p j s -> p (j s)"),
                        mixed[:, bass.ds(c * ROWS + j, 1), :].rearrange("p j h -> p (j h)"))
                last.then_inc(stats_ready, 1)

            chunk(0)
            with dve.Fori(1, CHUNKS) as c:
                chunk(c)
            dve.wait_ge(stats_ready, CHUNKS)
            for t in range(TILES):
                last = nc.vector.bn_aggr(moments[:, t], stats[:, t])
            last.then_inc(moments_ready, 1)
            dve.wait_ge(moments_ready, 1)
            nc.vector.tensor_scalar(variance[:], moments[:, :, 1], EPS, None, ALU.add).then_inc(end_step, 1)
            for k in range(2):
                nc.vector.tensor_tensor(row_sum[:, k], row_parts[:, 2 * k], row_parts[:, 2 * k + 1], ALU.add) \
                  .then_inc(end_step, 1)
            dve.wait_ge(end_step, 3)
            nc.vector.tensor_tensor(row_sum[:, 0], row_sum[:, 0], row_sum[:, 1], ALU.add).then_inc(end_step, 1)
            dve.wait_ge(end_step, 4)
            nc.vector.tensor_scalar(row_sum[:, 2], row_sum[:, 0], 1.0, None, ALU.add).then_inc(end_step, 1)
            dve.wait_ge(roots_ready, 1)
            nc.vector.reciprocal(inverse[:], roots[:]).then_inc(inverse_ready, 1)
            dve.wait_ge(inverse_ready, 1)
            for t in range(TILES):
                nc.vector.tensor_scalar(mixed[:, t], mixed[:, t], moments[:, t, 0:1], inverse[:, 0, t:t + 1],
                                        ALU.subtract, ALU.mult).then_inc(normed, 1)
            dve.wait_ge(normed, TILES)
            nc.vector.tensor_copy(dram["d_inverse"][:], inverse[:, 1]).then_inc(end_step, 1)

        @block.tensor
        def _(pe):
            pe.wait_ge(in_const, 16 * 12)

            def cell(n, k, half):
                ps = gates[k]
                wait(pe, pre_ready, n - 1)
                wait(pe, act_gates, n - 1)
                s, x = support[:, half, k], state[:, half]
                for g in range(2):
                    nc.tensor.matmul(ps[g][:], w_in[:, k, g], s, start=True, stop=False)
                    nc.tensor.matmul(ps[g][:], w_state[:, k, g], x, start=False, stop=True)
                nc.tensor.matmul(ps[2][:], w_in[:, k, 2], s, start=True, stop=True)
                nc.tensor.matmul(ps[3][:], w_state[:, k, 2], x, start=True, stop=True) \
                  .then_inc(gates_summed, 1)

            def turn(c):
                pe.wait_ge(both_ready, c + 1)
                for j in range(ROWS):
                    last = nc.tensor.transpose(gates[0][0][:, j * P:(j + 1) * P], both[:, j * P:(j + 1) * P],
                                               identity[:])
                last.then_inc(both_turned, 1)

            def pair(i):
                for half in range(2):
                    c = 2 * i + half
                    wait(pe, mixed_ready, c)
                    pe.wait_ge(in_chunk[half], 48 * (i + 1))
                    for k in range(CELLS):
                        cell(CELLS * c + k, k, half)
                    turn(c)

            pair(0)
            with pe.Fori(1, CHUNKS // 2) as i:
                pair(i)


def propagate_phase(nc, io, dram, out):
    with ExitStack() as stack:
        sbuf, psum, semaphore = memory(nc, stack)
        RING = 4
        x1 = sbuf("p3_x1", [P, TILES, H])
        scaled = sbuf("p3_scaled", [P, TILES, H])
        own = sbuf("p3_own", [P, ROWS, H])
        identity = sbuf("p3_identity", [P, P])
        w1 = sbuf("p3_w1", [H, H])
        adj_t = sbuf("p3_adj_t", [P, RING, ROWS, GROUP, P])
        gathered = sbuf("p3_gathered", [H, CHUNK])
        relu = sbuf("p3_relu", [P, ROWS, H])
        mixed = sbuf("p3_mixed", [P, ROWS, H])
        stats = sbuf("p3_stats", [P, ROWS, nc.vector.BN_STATS_DIM])
        moments = sbuf("p3_moments", [P, ROWS, 2])
        variance = sbuf("p3_variance", [P, ROWS])
        root = sbuf("p3_root", [P, ROWS])
        inverse = sbuf("p3_inverse", [P, ROWS])
        result = sbuf("p3_result", [P, 2, ROWS, H])
        ps_gathered = [psum(f"p3_ps_gathered{i}", [P, CHUNK]) for i in range(2)]
        ps_out = [psum(f"p3_ps_out{i}", [P, ROWS, H]) for i in range(2)]

        in_const = semaphore("p3_in_const")
        in_adj = [semaphore(f"p3_in_adj{i}") for i in range(RING)]
        own_ready = semaphore("p3_own_ready")
        group_done = semaphore("p3_group_done")
        chunk_done = semaphore("p3_chunk_done")
        gathered_ready = semaphore("p3_gathered_ready")
        out_summed = semaphore("p3_out_summed")
        relu_ready = semaphore("p3_relu_ready")
        mixed_ready = semaphore("p3_mixed_ready")
        stats_ready = semaphore("p3_stats_ready")
        moments_ready = semaphore("p3_moments_ready")
        variance_ready = semaphore("p3_variance_ready")
        root_ready = semaphore("p3_root_ready")
        inverse_ready = semaphore("p3_inverse_ready")
        result_ready = semaphore("p3_result_ready")
        out_done = [semaphore(f"p3_out_done{i}") for i in range(2)]
        passed = semaphore("p3_passed")

        block = stack.enter_context(nc.Block())

        @block.sync
        def _(sync):
            sync.dma_start(scaled[:], dram["x1_scaled"]).then_inc(in_const, 16)

            def load_chunk(c):
                for g in range(GROUPS):
                    slot = g % RING
                    wait(sync, group_done, GROUPS * c + g - RING + 1)
                    sync.dma_start(
                        adj_t[:, slot],
                        io["adj_t"][bass.ds(c * ROWS, ROWS), :, g * GROUP:(g + 1) * GROUP, :]
                        .rearrange("j p c r -> p j c r")).then_inc(in_adj[slot], 16)
                    if isinstance(c, int) and g == 0:
                        sync.dma_start(identity[:], io["identity"]).then_inc(in_const, 16)
                        sync.dma_start(w1[:], io["w1_t"]).then_inc(in_const, 16)
                        sync.dma_start(x1[:], dram["x1"]).then_inc(in_const, 16)

            load_chunk(0)
            with sync.Fori(1, CHUNKS) as c:
                load_chunk(c)

        @block.gpsimd
        def _(pool):
            pool.wait_ge(in_const, 64)

            def chunk(c):
                wait(pool, chunk_done, c)
                nc.gpsimd.tensor_copy(own[:], scaled[:, bass.ds(c * ROWS, ROWS), :]).then_inc(own_ready, 1)

            chunk(0)
            with pool.Fori(1, CHUNKS) as c:
                chunk(c)

        @block.scalar
        def _(act):
            def chunk(c, half):
                act.wait_ge(chunk_done, c + 1)
                wait(act, out_summed, c)
                nc.scalar.copy(gathered[:], ps_gathered[half][:]).then_inc(gathered_ready, 1)
                act.wait_ge(out_summed, c + 1)
                wait(act, mixed_ready, c)
                for j in range(ROWS):
                    last = nc.scalar.activation(relu[:, j], ps_out[half][:, j], ACT.Relu,
                                                scale=dram["d_inverse"][:, bass.ds(c * ROWS + j, 1)])
                last.then_inc(relu_ready, 1)
                act.wait_ge(variance_ready, c + 1)
                nc.scalar.activation(root[:], variance[:], ACT.Sqrt).then_inc(root_ready, 1)
                act.wait_ge(result_ready, c + 1)
                act.dma_start(out[bass.ds(c * CHUNK, CHUNK), :].rearrange("(j p) h -> p j h", p=P),
                              result[:, half]).then_inc(out_done[half], 16)

            def pair(i):
                for half in range(2):
                    chunk(2 * i + half, half)

            pair(0)
            with act.Fori(1, CHUNKS // 2) as i:
                pair(i)
            for half in range(2):
                act.wait_ge(out_done[half], 16 * CHUNKS // 2)

        @block.vector
        def _(dve):
            dve.wait_ge(in_const, 64)

            def chunk(c, i, half):
                dve.wait_ge(relu_ready, c + 1)
                nc.vector.tensor_tensor(mixed[:], relu[:], x1[:, bass.ds(c * ROWS, ROWS), :], ALU.add) \
                  .then_inc(mixed_ready, 1)
                dve.wait_ge(mixed_ready, c + 1)
                for j in range(ROWS):
                    last = nc.vector.bn_stats(stats[:, j], mixed[:, j])
                last.then_inc(stats_ready, 1)
                wait_apart(dve, stats_ready, c + 1, passed)
                for j in range(ROWS):
                    last = nc.vector.bn_aggr(moments[:, j], stats[:, j])
                last.then_inc(moments_ready, 1)
                dve.wait_ge(moments_ready, c + 1)
                wait(dve, root_ready, c)
                nc.vector.tensor_scalar(variance[:], moments[:, :, 1], EPS, None, ALU.add) \
                  .then_inc(variance_ready, 1)
                dve.wait_ge(root_ready, c + 1)
                nc.vector.reciprocal(inverse[:], root[:]).then_inc(inverse_ready, 1)
                dve.wait_ge(inverse_ready, c + 1)
                wait(dve, out_done[half], 16 * i)
                for j in range(ROWS):
                    last = nc.vector.tensor_scalar(result[:, half, j], mixed[:, j], moments[:, j, 0:1],
                                                   inverse[:, j:j + 1], ALU.subtract, ALU.mult)
                last.then_inc(result_ready, 1)

            def pair(i):
                for half in range(2):
                    chunk(2 * i + half, i, half)

            pair(0)
            with dve.Fori(1, CHUNKS // 2) as i:
                pair(i)

        @block.tensor
        def _(pe):
            pe.wait_ge(in_const, 64)

            def chunk(c, half):
                wait(pe, gathered_ready, c - 1)
                for g in range(GROUPS):
                    slot = g % RING
                    pe.wait_ge(in_adj[slot], 16 * (GROUPS // RING * c + g // RING + 1))
                    for k in range(GROUP):
                        t = g * GROUP + k
                        last = nc.tensor.matmul(ps_gathered[half][:], scaled[:, t, :], adj_t[:, slot, :, k, :],
                                                start=t == 0, stop=False)
                    last.then_inc(group_done, 1)
                pe.wait_ge(own_ready, c + 1)
                for j in range(ROWS):
                    last = nc.tensor.matmul(ps_gathered[half][:, j * P:(j + 1) * P], own[:, j], identity[:],
                                            start=False, stop=j == ROWS - 1)
                last.then_inc(chunk_done, 1)
                pe.wait_ge(gathered_ready, c + 1)
                wait(pe, relu_ready, c - 1)
                for j in range(ROWS):
                    last = nc.tensor.matmul(ps_out[half][:, j], gathered[:, j * P:(j + 1) * P], w1[:],
                                            start=True, stop=True)
                last.then_inc(out_summed, 1)

            def pair(i):
                for half in range(2):
                    chunk(2 * i + half, half)

            pair(0)
            with pe.Fori(1, CHUNKS // 2) as i:
                pair(i)


def two_layers(nc, io, out):
    dram = {
        "scores": nc.dram_tensor("neg_scores", [SCORES, N], F32).ap(),
        "sums": nc.dram_tensor("neighbour_sums", [H, N], F32).ap(),
        "support": nc.dram_tensor("edge_support", [H, N], F32).ap(),
        "row_parts": nc.dram_tensor("row_parts", [P, QUARTERS, TILES], F32).ap(),
        "flag": nc.dram_tensor("negative_flag", [1, 1], I32).ap(),
        "x1": nc.dram_tensor("x1", [P, TILES, H], F32).ap(),
        "x1_scaled": nc.dram_tensor("x1_scaled", [P, TILES, H], F32).ap(),
    }
    with nc.sbuf_tensor("d_inverse", [P, TILES], F32) as d_inverse:
        dram["d_inverse"] = d_inverse
        score_phase(nc, io, dram)
        attention_phase(nc, io, dram)
        update_phase(nc, io, dram)
        propagate_phase(nc, io, dram, out)


def score_selection():
    select = np.zeros((P, SCORES), np.float32)
    for h in range(HEADS):
        for score, positive_half in ((h, 0), (HEADS + h, 1)):
            for at, diag_at, half in ((POS, POS_DIAG, positive_half), (NEG, NEG_DIAG, 1 - positive_half)):
                column = 2 * h + half
                for s in range(SPLITS):
                    select[at + 1 + s * SCORES + column, score] = -1.0
                select[diag_at + column, score] = 1.0
    return select


def kernel(x, adj, L0_gnn_gat_W, L0_gnn_gat_a, L0_gnn_edge_Wih, L0_gnn_edge_Whh, L0_gnn_edge_bih,
           L0_gnn_edge_bhh, L0_gnn_node_Wih, L0_gnn_node_Whh, L0_gnn_node_bih, L0_gnn_node_bhh, L1_gnn_W):
    import concourse.bacc as bacc
    from concourse.bass_utils import run_bass_kernel_spmd

    x, adj = np.asarray(x), np.asarray(adj)
    gat_w, gat_a = np.asarray(L0_gnn_gat_W), np.asarray(L0_gnn_gat_a)
    diag = np.diagonal(adj)

    def gate_rows(w):
        return np.asarray(w).reshape(3, H, H).transpose(2, 0, 1)

    def gate_bias(b):
        return np.asarray(b).reshape(3, H).T

    arrays = {
        "x": x,
        "x_cols": x.T,
        "adj": adj,
        "adj_t": adj.reshape(TILES, P, TILES, P).transpose(0, 3, 2, 1),
        "diag_row": diag.reshape(1, N),
        "diag_cols": diag.reshape(TILES, P).T,
        "w": gat_w.transpose(1, 0, 2),
        "w_t": gat_w.transpose(2, 0, 1),
        "a": gat_a.reshape(HEADS, 2, H).transpose(2, 0, 1).reshape(H, SCORES),
        "edge_w_in": gate_rows(L0_gnn_edge_Wih),
        "edge_w_state": gate_rows(L0_gnn_edge_Whh),
        "edge_bias_in": gate_bias(L0_gnn_edge_bih),
        "edge_bias_state": gate_bias(L0_gnn_edge_bhh),
        "node_w_in": gate_rows(L0_gnn_node_Wih),
        "node_w_state": gate_rows(L0_gnn_node_Whh),
        "node_bias_in": gate_bias(L0_gnn_node_bih),
        "node_bias_state": gate_bias(L0_gnn_node_bhh),
        "w1_t": np.asarray(L1_gnn_W).T,
        "identity": np.eye(P, dtype=np.float32),
        "select": score_selection(),
    }
    arrays = {name: np.ascontiguousarray(a) for name, a in arrays.items()}
    nc = bacc.Bacc("TRN2", target_bir_lowering=False, num_devices=1, dynamic_dma_scratch_size=1024)
    io = {name: nc.dram_tensor(f"in_{name}", a.shape, mybir.dt.from_np(a.dtype), kind="ExternalInput").ap()
          for name, a in arrays.items()}
    out = nc.dram_tensor("out", (N, H), F32, kind="ExternalOutput").ap()
    two_layers(nc, io, out)
    ran = run_bass_kernel_spmd(nc, [{f"in_{name}": a for name, a in arrays.items()}], core_ids=[0])
    return ran.results[0]["out"]
```

```python
from contextlib import ExitStack

import numpy as np

import concourse.bass as bass
from concourse import mybir
from concourse.alu_op_type import AluOpType as ALU

F32 = mybir.dt.float32
BF16 = mybir.dt.bfloat16
I32 = mybir.dt.int32
ACT = mybir.ActivationFunctionType
AX_X = mybir.AxisListType.X

P = 128
N = 4096
H = 128
HEADS = 3
TILES = N // P
CHUNK = 512
CHUNKS = N // CHUNK
ROWS = CHUNK // P
GROUP = 4
GROUPS = TILES // GROUP
QUARTERS = 4
QUARTER = N // QUARTERS
SPLITS = 3
SCORES = 2 * HEADS
PARTS = 1 + SPLITS * SCORES
NEG, POS, NEG_DIAG, POS_DIAG = 0, 32, 64, 96
BIG = 1e30
ALPHA = 0.2
EPS = 1e-5


def memory(nc, stack):
    def sbuf(name, shape, dtype=F32):
        return stack.enter_context(nc.sbuf_tensor(name, shape, dtype))

    def psum(name, shape, dtype=F32):
        return stack.enter_context(nc.psum_tensor(name, shape, dtype))

    def semaphore(name):
        return stack.enter_context(nc.semaphore(name))

    return sbuf, psum, semaphore


def wait(engine, semaphore, count):
    if not isinstance(count, int) or count > 0:
        engine.wait_ge(semaphore, count)


def wait_apart(engine, semaphore, count, passed):
    wait(engine, semaphore, count)
    if not isinstance(count, int):
        engine.sem_inc(passed, 1)


def score_phase(nc, io, dram):
    with ExitStack() as stack:
        sbuf, psum, semaphore = memory(nc, stack)
        RING = 4
        x_rows = sbuf("p0_x_rows", [P, TILES, H])
        x_cols = sbuf("p0_x_cols", [H, N])
        w = sbuf("p0_w", [H, HEADS, H])
        a = sbuf("p0_a", [H, SCORES])
        wa = sbuf("p0_wa", [H, SCORES])
        wa_placed = sbuf("p0_wa_placed", [H, P])
        select = sbuf("p0_select", [P, SCORES])
        u = sbuf("p0_u", [P, TILES, SCORES])
        rest = sbuf("p0_rest", [P, 2, TILES, SCORES])
        u_parts = sbuf("p0_u_parts", [P, TILES, PARTS], BF16)
        diag_terms = sbuf("p0_diag_terms", [P, N])
        adj_t = sbuf("p0_adj_t", [P, RING, ROWS, GROUP, P])
        masks = sbuf("p0_masks", [P, 2, 2, ROWS, GROUP, P], BF16)
        diag = sbuf("p0_diag", [P, 2, CHUNK])
        diag_x = sbuf("p0_diag_x", [P, CHUNK])
        sums = sbuf("p0_sums", [P, 2, CHUNK])
        terms = sbuf("p0_terms", [P, 2, CHUNK])
        raw = sbuf("p0_raw", [SCORES, 2, CHUNK])
        scores = sbuf("p0_scores", [SCORES, 2, CHUNK])
        most = sbuf("p0_most", [1, CHUNK])
        flag = sbuf("p0_flag", [1, 1], I32)
        ps_sums = [psum(f"p0_ps_sums{i}", [P, CHUNK]) for i in range(2)]
        ps_masks = [psum(f"p0_ps_masks{i}", [P, CHUNK]) for i in range(2)]
        ps_scores = psum("p0_ps_scores", [P, CHUNK])
        ps_setup = psum("p0_ps_setup", [P, CHUNK])
        ps_diag = [psum(f"p0_ps_diag{i}", [P, CHUNK]) for i in range(2)]

        in_w = semaphore("p0_in_w")
        in_x = semaphore("p0_in_x")
        in_adj = [semaphore(f"p0_in_adj{i}") for i in range(RING)]
        in_diag = [semaphore(f"p0_in_diag{i}") for i in range(2)]
        wa_summed = semaphore("p0_wa_summed")
        wa_ready = semaphore("p0_wa_ready")
        u_summed = semaphore("p0_u_summed")
        u_step = semaphore("p0_u_step")
        u_ready = semaphore("p0_u_ready")
        cleared = semaphore("p0_cleared")
        diag_summed = semaphore("p0_diag_summed")
        diag_copied = semaphore("p0_diag_copied")
        masks_ready = semaphore("p0_masks_ready")
        group_done = semaphore("p0_group_done")
        sums_ready = semaphore("p0_sums_ready")
        diag_x_ready = semaphore("p0_diag_x_ready")
        terms_ready = semaphore("p0_terms_ready")
        scores_summed = semaphore("p0_scores_summed")
        raw_ready = semaphore("p0_raw_ready")
        scores_ready = semaphore("p0_scores_ready")
        most_ready = semaphore("p0_most_ready")
        out_sums = [semaphore(f"p0_out_sums{i}") for i in range(2)]
        out_scores = [semaphore(f"p0_out_scores{i}") for i in range(2)]
        flag_ready = semaphore("p0_flag_ready")
        out_flag = semaphore("p0_out_flag")

        block = stack.enter_context(nc.Block())

        @block.sync
        def _(sync):
            sync.dma_start(w[:], io["w_t"]).then_inc(in_w, 16)
            sync.dma_start(a[:], io["a"]).then_inc(in_w, 16)
            sync.dma_start(select[:], io["select"]).then_inc(in_w, 16)
            sync.dma_start(x_cols[:], io["x_cols"]).then_inc(in_x, 16)
            sync.dma_start(x_rows[:], io["x"].rearrange("(t p) h -> p t h", p=P)).then_inc(in_x, 16)

            def load_chunk(c):
                for g in range(GROUPS):
                    slot = g % RING
                    wait(sync, group_done, GROUPS * c + g - RING + 1)
                    wait(sync, masks_ready, GROUPS * c + g - RING + 1)
                    sync.dma_start(
                        adj_t[:, slot],
                        io["adj_t"][bass.ds(c * ROWS, ROWS), :, g * GROUP:(g + 1) * GROUP, :]
                        .rearrange("j p c r -> p j c r")).then_inc(in_adj[slot], 16)

            load_chunk(0)
            with sync.Fori(1, CHUNKS) as c:
                load_chunk(c)
            sync.wait_ge(flag_ready, 1)
            sync.dma_start(dram["flag"], flag[:]).then_inc(out_flag, 16)
            sync.wait_ge(out_flag, 16)

        @block.scalar
        def _(act):
            for half in range(2):
                act.dma_start(diag[:, half], io["diag_row"][:, half * CHUNK:(half + 1) * CHUNK]
                              .broadcast_to([P, CHUNK])).then_inc(in_diag[half], 16)
            act.wait_ge(wa_summed, 1)
            nc.scalar.copy(wa[:], ps_setup[:, 0:SCORES]).then_inc(wa_ready, 1)
            for c in range(CHUNKS):
                act.wait_ge(diag_summed, c + 1)
                nc.scalar.copy(diag_terms[:, c * CHUNK:(c + 1) * CHUNK], ps_diag[c % 2][:]) \
                  .then_inc(diag_copied, 1)

            def chunk_pair(i, last):
                for half in range(2):
                    c = 2 * i + half
                    act.wait_ge(scores_summed, c + 1)
                    wait(act, scores_ready, c - 1)
                    nc.scalar.copy(raw[:, half], ps_scores[0:SCORES, :]).then_inc(raw_ready, 1)
                    act.wait_ge(sums_ready, c + 1)
                    act.dma_start(dram["sums"][:, bass.ds(c * CHUNK, CHUNK)], sums[:, half]) \
                       .then_inc(out_sums[half], 16)
                    act.wait_ge(scores_ready, c + 1)
                    act.dma_start(dram["scores"][:, bass.ds(c * CHUNK, CHUNK)], scores[:, half]) \
                       .then_inc(out_scores[half], 16)
                    if not last:
                        act.dma_start(diag[:, half], io["diag_row"][:, bass.ds((c + 2) * CHUNK, CHUNK)]
                                      .broadcast_to([P, CHUNK])).then_inc(in_diag[half], 16)

            chunk_pair(0, False)
            with act.Fori(1, CHUNKS // 2 - 1) as i:
                chunk_pair(i, False)
            chunk_pair(CHUNKS // 2 - 1, True)
            for half in range(2):
                act.wait_ge(out_sums[half], 16 * CHUNKS // 2)
                act.wait_ge(out_scores[half], 16 * CHUNKS // 2)

        @block.vector
        def _(dve):
            nc.vector.memset(terms[:], 0.0).then_inc(cleared, 1)
            nc.vector.memset(wa_placed[:], 0.0).then_inc(cleared, 1)
            nc.vector.memset(u_parts[:, :, 0:1], 1.0).then_inc(cleared, 1)
            nc.vector.memset(most[:], 0.0).then_inc(cleared, 1)
            dve.wait_ge(wa_ready, 1)
            dve.wait_ge(cleared, 4)
            for at in (NEG_DIAG, POS_DIAG):
                nc.vector.tensor_copy(wa_placed[:, at:at + SCORES], wa[:]).then_inc(wa_ready, 1)
            dve.wait_ge(u_summed, 1)
            nc.vector.tensor_copy(u[:], ps_setup[:, 0:TILES * SCORES]
                                  .rearrange("p (t s) -> p t s", s=SCORES)).then_inc(u_step, 1)
            dve.wait_ge(u_step, 1)
            source = u[:]
            for s in range(SPLITS):
                part = u_parts[:, :, 1 + s * SCORES:1 + (s + 1) * SCORES]
                nc.vector.tensor_copy(part, source).then_inc(u_step, 1)
                dve.wait_ge(u_step, 2 * s + 2)
                if s < SPLITS - 1:
                    nc.vector.tensor_tensor(rest[:, s], source, part, ALU.subtract).then_inc(u_step, 1)
                    dve.wait_ge(u_step, 2 * s + 3)
                    source = rest[:, s]
            nc.vector.tensor_copy(flag[:], most[:, 0:1]).then_inc(u_ready, 1)

            def chunk_pair(i):
                for half in range(2):
                    c = 2 * i + half
                    for g in range(GROUPS):
                        slot = g % RING
                        n = GROUPS * c + g
                        dve.wait_ge(in_adj[slot], 16 * (GROUPS // RING * c + g // RING + 1))
                        wait(dve, group_done, n - 1)
                        nc.vector.tensor_scalar(masks[:, g % 2, 0], adj_t[:, slot], 0.0, None, ALU.is_lt)
                        nc.vector.tensor_scalar(masks[:, g % 2, 1], adj_t[:, slot], 0.0, None, ALU.is_gt) \
                          .then_inc(masks_ready, 1)
                    dve.wait_ge(in_diag[half], 16 * (i + 1))
                    wait(dve, diag_copied, CHUNKS)
                    wait(dve, scores_summed, c - 1)
                    for at, sign in ((NEG_DIAG, ALU.is_lt), (POS_DIAG, ALU.is_gt)):
                        nc.vector.scalar_tensor_tensor(
                            terms[at:at + SCORES, half], diag[at:at + SCORES, half], 0.0,
                            diag_terms[at:at + SCORES, bass.ds(c * CHUNK, CHUNK)], sign, ALU.mult)
                    dve.wait_ge(group_done, GROUPS * (c + 1))
                    nc.vector.tensor_copy(terms[POS:POS + PARTS, half], ps_masks[half][POS:POS + PARTS, :])
                    nc.vector.tensor_copy(terms[NEG:NEG + PARTS, half], ps_masks[half][NEG:NEG + PARTS, :]) \
                      .then_inc(terms_ready, 1)
                    dve.wait_ge(terms_ready, c + 1)
                    wait(dve, most_ready, c)
                    nc.vector.tensor_tensor(most[:], most[:], terms[NEG:NEG + 1, half], ALU.max) \
                      .then_inc(most_ready, 1)
                    nc.vector.tensor_tensor(diag_x[:], diag[:, half], x_cols[:, bass.ds(c * CHUNK, CHUNK)],
                                            ALU.mult).then_inc(diag_x_ready, 1)
                    dve.wait_ge(diag_x_ready, c + 1)
                    wait(dve, out_sums[half], 16 * i)
                    nc.vector.tensor_tensor(sums[:, half], ps_sums[half][:], diag_x[:], ALU.subtract) \
                      .then_inc(sums_ready, 1)
                    dve.wait_ge(raw_ready, c + 1)
                    wait(dve, out_scores[half], 16 * i)
                    nc.vector.scalar_tensor_tensor(scores[:, half], raw[:, half], ALPHA, raw[:, half],
                                                   ALU.mult, ALU.min).then_inc(scores_ready, 1)

            dve.wait_ge(in_x, 32)
            chunk_pair(0)
            with dve.Fori(1, CHUNKS // 2) as i:
                chunk_pair(i)
            dve.wait_ge(most_ready, CHUNKS)
            nc.vector.tensor_reduce(flag[:], most[:], AX_X, ALU.max).then_inc(flag_ready, 1)

        @block.tensor
        def _(pe):
            pe.wait_ge(in_w, 48)
            for h in range(HEADS):
                last = nc.tensor.matmul(ps_setup[:, 2 * h:2 * h + 2], w[:, h, :], a[:, 2 * h:2 * h + 2],
                                        start=True, stop=True)
            last.then_inc(wa_summed, 1)
            pe.wait_ge(in_x, 32)
            pe.wait_ge(wa_ready, 3)
            for t in range(TILES):
                last = nc.tensor.matmul(ps_setup[:, t * SCORES:(t + 1) * SCORES],
                                        x_cols[:, t * P:(t + 1) * P], wa[:], start=True, stop=True)
            last.then_inc(u_summed, 1)
            for c in range(CHUNKS):
                wait(pe, diag_copied, c - 1)
                nc.tensor.matmul(ps_diag[c % 2][:], wa_placed[:], x_cols[:, c * CHUNK:(c + 1) * CHUNK],
                                 start=True, stop=True).then_inc(diag_summed, 1)
            pe.wait_ge(u_ready, 1)

            def chunk_pair(i):
                for half in range(2):
                    c = 2 * i + half
                    wait(pe, sums_ready, c - 1)
                    wait(pe, terms_ready, c - 1)
                    for g in range(GROUPS):
                        slot = g % RING
                        pe.wait_ge(in_adj[slot], 16 * (GROUPS // RING * c + g // RING + 1))
                        pe.wait_ge(masks_ready, GROUPS * c + g + 1)
                        for k in range(GROUP):
                            t = g * GROUP + k
                            first, final = t == 0, t == TILES - 1
                            nc.tensor.matmul(ps_sums[half][:], x_rows[:, t, :], adj_t[:, slot, :, k, :],
                                             start=first, stop=final)
                            nc.tensor.matmul(ps_masks[half][NEG:NEG + PARTS, :], u_parts[:, t, :],
                                             masks[:, g % 2, 0, :, k, :], start=first, stop=final)
                            last = nc.tensor.matmul(ps_masks[half][POS:POS + PARTS, :], u_parts[:, t, :],
                                                    masks[:, g % 2, 1, :, k, :], start=first, stop=final)
                        last.then_inc(group_done, 1)
                    pe.wait_ge(terms_ready, c + 1)
                    wait(pe, raw_ready, c)
                    nc.tensor.matmul(ps_scores[0:SCORES, :], select[:], terms[:, half],
                                     start=True, stop=True).then_inc(scores_summed, 1)

            chunk_pair(0)
            with pe.Fori(1, CHUNKS // 2) as i:
                chunk_pair(i)


def attention_phase(nc, io, dram):
    with ExitStack() as stack:
        sbuf, psum, semaphore = memory(nc, stack)
        STAGES = QUARTERS
        RING = 4
        x_rows = sbuf("p1_x_rows", [P, TILES, H])
        identity = sbuf("p1_identity", [P, P])
        flag = sbuf("p1_flag", [1, 1], I32)
        big_diag = sbuf("p1_big_diag", [P, P], BF16)
        w = sbuf("p1_w", [H, HEADS, H])
        least = sbuf("p1_least", [P, 2, HEADS, QUARTERS])
        total = sbuf("p1_total", [P, 2, HEADS])
        inverse = sbuf("p1_inverse", [P, 2, 2, HEADS])
        row_parts = sbuf("p1_row_parts", [P, QUARTERS, TILES])
        gathered = sbuf("p1_gathered", [H, HEADS, P])
        by_head = sbuf("p1_by_head", [P, HEADS, H])
        pair_sum = sbuf("p1_pair_sum", [P, H])
        support = sbuf("p1_support", [P, H])
        support_t = sbuf("p1_support_t", [H, 2, P])
        with ExitStack() as plain:
            place, _, _ = memory(nc, plain)
            any_rows = place("p1_any_rows", [P, N])
            any_adj_t = place("p1_any_adj_t", [P, TILES, P])
            any_neg_e = place("p1_any_neg_e", [P, 2, N])
            any_att = place("p1_any_att", [P, 2, N])
            any_weighted = place("p1_any_weighted", [P, 2, GROUP, P])
            any_off_diag = place("p1_any_off_diag", [P, P])
        neg_e = sbuf("p1_neg_e", [P, HEADS, N])
        stage = sbuf("p1_stage", [P, STAGES, QUARTER])
        spare = sbuf("p1_spare", [P, QUARTER], BF16)
        absent = sbuf("p1_absent", [P, 2, N], BF16)
        att = sbuf("p1_att", [P, 2, HEADS, N])
        adj_t = sbuf("p1_adj_t", [P, RING, GROUP, P])
        weighted = sbuf("p1_weighted", [P, 2, GROUP, HEADS, P])
        ps_att = [psum(f"p1_ps_att{i}", [P, GROUP, HEADS, P]) for i in range(2)]
        ps_gathered = psum("p1_ps_gathered", [P, CHUNK])
        ps_support = psum("p1_ps_support", [P, CHUNK])

        in_const = semaphore("p1_in_const")
        in_x = semaphore("p1_in_x")
        in_any_const = semaphore("p1_in_any_const")
        in_flag = semaphore("p1_in_flag")
        in_any_rows = semaphore("p1_in_any_rows")
        in_any_adj = semaphore("p1_in_any_adj")
        in_any_e = semaphore("p1_in_any_e")
        any_step = semaphore("p1_any_step")
        in_e = semaphore("p1_in_e")
        in_stage = [semaphore(f"p1_in_stage{i}") for i in range(STAGES)]
        in_adj = [semaphore(f"p1_in_adj{i}") for i in range(RING)]
        rows_summed = semaphore("p1_rows_summed")
        quarter_masked = semaphore("p1_quarter_masked")
        absent_ready = semaphore("p1_absent_ready")
        masked = semaphore("p1_masked")
        att_ready = semaphore("p1_att_ready")
        turned = semaphore("p1_turned")
        weighted_ready = semaphore("p1_weighted_ready")
        gathered_part = semaphore("p1_gathered_part")
        gathered_ready = semaphore("p1_gathered_ready")
        inverse_step = semaphore("p1_inverse_step")
        inverse_ready = semaphore("p1_inverse_ready")
        head_summed = semaphore("p1_head_summed")
        by_head_ready = semaphore("p1_by_head_ready")
        pair_ready = semaphore("p1_pair_ready")
        support_ready = semaphore("p1_support_ready")
        support_turned = semaphore("p1_support_turned")
        support_copied = semaphore("p1_support_copied")
        out_support = [semaphore(f"p1_out_support{i}") for i in range(2)]
        out_rows = semaphore("p1_out_rows")
        passed = semaphore("p1_passed")

        block = stack.enter_context(nc.Block())

        @block.sync
        def _(sync):
            sync.dma_start(flag[:], dram["flag"]).then_inc(in_flag, 16)
            sync.dma_start(identity[:], io["identity"]).then_inc(in_const, 16)
            sync.dma_start(w[:], io["w"]).then_inc(in_const, 16)

            def load_any(t):
                wait(sync, weighted_ready, HEADS * GROUPS * t)
                sync.dma_start(any_rows[:], io["adj"][bass.ds(t * P, P), :]).then_inc(in_any_rows, 16)
                sync.dma_start(any_adj_t[:], io["adj_t"][bass.ds(t, 1)].rearrange("j p c r -> p (j c) r")) \
                    .then_inc(in_any_adj, 16)
                for h in range(HEADS):
                    wait(sync, masked, HEADS * t + h)
                    for sign in range(2):
                        row = dram["scores"][sign * HEADS + h:sign * HEADS + h + 1, :]
                        sync.dma_start(any_neg_e[:, sign], row.broadcast_to([P, N])).then_inc(in_any_e, 16)

            def load_quarter(t, q):
                wait(sync, rows_summed, QUARTERS * (t - 1) + q + 1)
                wait(sync, quarter_masked, QUARTERS * (t - 1) + q + 1)
                sync.dma_start(stage[:, q], io["adj"][bass.ds(t * P, P), q * QUARTER:(q + 1) * QUARTER]) \
                    .then_inc(in_stage[q], 16)

            def load_turned(t, g):
                slot = g % RING
                wait(sync, weighted_ready, GROUPS * t + g - RING + 1)
                sync.dma_start(
                    adj_t[:, slot],
                    io["adj_t"][bass.ds(t, 1), :, g * GROUP:(g + 1) * GROUP, :]
                    .rearrange("j p c r -> p (j c) r")).then_inc(in_adj[slot], 16)

            def load(t, ahead):
                for g in range(GROUPS):
                    load_turned(t, g)
                    if ahead and g >= GROUPS - QUARTERS:
                        load_quarter(t + 3, g - (GROUPS - QUARTERS))

            sync.wait_ge(in_flag, 16)
            negative = sync.value_load(flag[0:1, 0:1], min_val=0, max_val=N)
            with sync.If(negative > 0):
                sync.dma_start(any_off_diag[:], io["off_diagonal"]).then_inc(in_any_const, 16)
                sync.dma_start(x_rows[:], io["x"].rearrange("(t p) h -> p t h", p=P)).then_inc(in_x, 16)
                load_any(0)
                with sync.Fori(1, TILES) as t:
                    load_any(t)
            with sync.Else():
                for q in range(QUARTERS):
                    load_quarter(0, q)
                for h in range(HEADS):
                    sync.dma_start(neg_e[:, h, :], dram["scores"][h:h + 1, :].broadcast_to([P, N])) \
                        .then_inc(in_e, 16)
                sync.dma_start(x_rows[:], io["x"].rearrange("(t p) h -> p t h", p=P)).then_inc(in_x, 16)
                for t in (1, 2):
                    for q in range(QUARTERS):
                        load_quarter(t, q)
                load(0, True)
                with sync.Fori(1, TILES - 3) as t:
                    load(t, True)
                for t in range(TILES - 3, TILES):
                    load(t, False)

        @block.gpsimd
        def _(pool):
            pool.wait_ge(in_const, 32)
            nc.gpsimd.tensor_scalar(big_diag[:], identity[:], BIG, None, ALU.mult).then_inc(support_ready, 1)
            pool.wait_ge(support_ready, 1)

            def mask_tile(t, slot):
                wait(pool, masked, QUARTERS * HEADS * (t - 1))
                for q in range(QUARTERS):
                    wait_apart(pool, in_stage[q], 16 * (t + 1), passed)
                    nc.gpsimd.tensor_scalar(absent[:, slot, q * QUARTER:(q + 1) * QUARTER], stage[:, q],
                                            0.0, BIG, ALU.is_le, ALU.mult).then_inc(quarter_masked, 1)
                pool.wait_ge(quarter_masked, QUARTERS * (t + 1))
                own = absent[:, slot, bass.ds(t * P, P)]
                nc.gpsimd.tensor_tensor(own, own, big_diag[:], ALU.add).then_inc(absent_ready, 1)

            def add_heads(t):
                pool.wait_ge(by_head_ready, t + 1)
                nc.gpsimd.tensor_tensor(pair_sum[:], by_head[:, 0], by_head[:, 1], ALU.add) \
                  .then_inc(pair_ready, 1)
                pool.wait_ge(pair_ready, t + 1)
                wait(pool, support_turned, t)
                nc.gpsimd.tensor_tensor(support[:], pair_sum[:], by_head[:, 2], ALU.add) \
                  .then_inc(support_ready, 1)

            def pair(i, first, last):
                for slot in range(2):
                    t = 2 * i + slot
                    if not last:
                        mask_tile(t + 2, slot)
                    if not (first and slot == 0):
                        add_heads(t - 1)

            pool.wait_ge(in_flag, 16)
            negative = pool.value_load(flag[0:1, 0:1], min_val=0, max_val=N)
            with pool.If(negative > 0):
                add_heads(0)
                with pool.Fori(1, TILES) as t:
                    add_heads(t)
            with pool.Else():
                mask_tile(0, 0)
                mask_tile(1, 1)
                pair(0, True, False)
                with pool.Fori(1, TILES // 2 - 1) as i:
                    pair(i, False, False)
                pair(TILES // 2 - 1, False, True)
                add_heads(TILES - 1)

        @block.scalar
        def _(act):
            def sum_rows(t, q):
                act.wait_ge(in_stage[q], 16 * (t + 1))
                wait(act, rows_summed, QUARTERS * t + q)
                nc.scalar.activation(spare[:], stage[:, q], ACT.Copy,
                                     accum_out=row_parts[:, q, bass.ds(t, 1)]).then_inc(rows_summed, 1)

            def exponentiate(t, slot, h):
                act.wait_ge(masked, QUARTERS * HEADS * t + QUARTERS * (h + 1))
                if h == 0:
                    wait(act, inverse_ready, t - 1)
                nc.scalar.activation(att[:, slot, h, :], att[:, slot, h, :], ACT.Exp,
                                     bias=least[:, slot, h, QUARTERS - 1:QUARTERS], scale=-1.0,
                                     accum_out=total[:, slot, h:h + 1]).then_inc(att_ready, 1)

            def exponentiate_any(t):
                for h in range(HEADS):
                    act.wait_ge(masked, HEADS * t + h + 1)
                    if h == 0:
                        wait(act, inverse_ready, t)
                    nc.scalar.activation(any_att[:, 0], any_att[:, 0], ACT.Exp, bias=least[:, 0, h, 0:1],
                                         scale=-1.0, accum_out=total[:, 0, h:h + 1]).then_inc(att_ready, 1)

            def scale_heads(t, slot, parts=GROUPS):
                act.wait_ge(gathered_part, parts * (t + 1))
                nc.scalar.copy(gathered[:], ps_gathered[:, 0:HEADS * P]
                               .rearrange("p (h r) -> p h r", h=HEADS)).then_inc(gathered_ready, 1)
                act.wait_ge(head_summed, t + 1)
                act.wait_ge(inverse_ready, t + 1)
                wait(act, support_ready, t + 1)
                for h in range(HEADS):
                    last = nc.scalar.activation(by_head[:, h], ps_support[:, h * P:(h + 1) * P], ACT.Copy,
                                                scale=inverse[:, slot, 1, h:h + 1])
                last.then_inc(by_head_ready, 1)

            def store_support(t, slot, i):
                act.wait_ge(support_turned, t + 1)
                wait(act, out_support[slot], 16 * i)
                nc.scalar.copy(support_t[:, slot], ps_support[:, HEADS * P:(HEADS + 1) * P]) \
                  .then_inc(support_copied, 1)
                act.wait_ge(support_copied, t + 1)
                act.dma_start(dram["support"][:, bass.ds(t * P, P)], support_t[:, slot]) \
                   .then_inc(out_support[slot], 16)

            def pair(i, first, last):
                for slot in range(2):
                    t = 2 * i + slot
                    before, attend = not (first and slot == 0), not (last and slot)
                    if before:
                        scale_heads(t - 1, 1 - slot)
                    for h in range(HEADS):
                        if attend:
                            exponentiate(t + 1, 1 - slot, h)
                        if h < HEADS - 1 and not last:
                            sum_rows(t + 2, 2 * h)
                            sum_rows(t + 2, 2 * h + 1)
                    if before:
                        store_support(t - 1, 1 - slot, i - 1 + slot)

            act.wait_ge(in_flag, 16)
            negative = act.value_load(flag[0:1, 0:1], min_val=0, max_val=N)
            with act.If(negative > 0):
                def any_tile(t):
                    exponentiate_any(t)
                    scale_heads(t, 0, HEADS * GROUPS)
                    store_support(t, 0, t)

                any_tile(0)
                with act.Fori(1, TILES) as t:
                    any_tile(t)
                act.dma_start(dram["row_parts"], row_parts[:]).then_inc(out_rows, 16)
                act.wait_ge(out_rows, 16)
                act.wait_ge(out_support[0], 16 * TILES)
            with act.Else():
                for t in range(2):
                    for q in range(QUARTERS):
                        sum_rows(t, q)
                for h in range(HEADS):
                    exponentiate(0, 0, h)
                pair(0, True, False)
                with act.Fori(1, TILES // 2 - 1) as i:
                    pair(i, False, False)
                pair(TILES // 2 - 1, False, True)
                scale_heads(TILES - 1, 1)
                store_support(TILES - 1, 1, TILES // 2 - 1)
                act.wait_ge(rows_summed, QUARTERS * TILES)
                act.dma_start(dram["row_parts"], row_parts[:]).then_inc(out_rows, 16)
                act.wait_ge(out_rows, 16)
                for slot in range(2):
                    act.wait_ge(out_support[slot], 16 * TILES // 2)

        @block.vector
        def _(dve):
            def mask_scores(t, slot, k):
                h, q = divmod(k, QUARTERS)
                if k == 0:
                    dve.wait_ge(absent_ready, t + 1)
                    wait(dve, att_ready, HEADS * (t - 1))
                if h == 0:
                    wait_apart(dve, turned, GROUPS * (t - 2) + GROUPS // QUARTERS * (q + 1), passed)
                if q:
                    wait_apart(dve, masked, QUARTERS * HEADS * t + k, passed)
                cut = slice(q * QUARTER, (q + 1) * QUARTER)
                nc.vector.tensor_tensor_reduce(
                    out=att[:, slot, h, cut], in0=absent[:, slot, cut], in1=neg_e[:, h, cut],
                    scale=1.0, scalar=least[:, slot, h, q - 1:q] if q else 3e38,
                    op0=ALU.add, op1=ALU.min, accum_out=least[:, slot, h, q:q + 1]).then_inc(masked, 1)

            def weigh(t, g):
                n = GROUPS * t + g
                slot = g % RING
                dve.wait_ge(turned, n + 1)
                dve.wait_ge(in_adj[slot], 16 * (GROUPS // RING * t + g // RING + 1))
                wait(dve, gathered_part, n - 1)
                tile = adj_t[:, slot]
                nc.vector.tensor_tensor(weighted[:, g % 2], ps_att[g % 2][:],
                                        tile.unsqueeze(2).broadcast_to([P, GROUP, HEADS, P]), ALU.mult) \
                  .then_inc(weighted_ready, 1)

            def invert(t, slot, former=1):
                dve.wait_ge(att_ready, HEADS * (t + 1))
                wait(dve, by_head_ready, t - former)
                nc.vector.tensor_scalar(inverse[:, slot, 0], total[:, slot], float(HEADS), None, ALU.mult) \
                  .then_inc(inverse_step, 1)
                dve.wait_ge(inverse_step, t + 1)
                nc.vector.reciprocal(inverse[:, slot, 1], inverse[:, slot, 0]).then_inc(inverse_ready, 1)

            STEPS = 2 + 5 * HEADS

            def mask_any(t):
                def settled(n, instruction):
                    instruction.then_inc(any_step, 1)
                    dve.wait_ge(any_step, STEPS * t + n + 2)

                dve.wait_ge(in_any_rows, 16 * (t + 1))
                settled(0, nc.vector.tensor_reduce(row_parts[:, 0, bass.ds(t, 1)], any_rows[:], AX_X, ALU.add))
                own = any_rows[:, bass.ds(t * P, P)]
                settled(1, nc.vector.tensor_tensor(own, own, any_off_diag[:], ALU.mult))
                for h in range(HEADS):
                    dve.wait_ge(in_any_e, 32 * (HEADS * t + h + 1))
                    wait(dve, turned, GROUPS * (HEADS * t + h))
                    n = 2 + 5 * h
                    settled(n, nc.vector.tensor_scalar(any_att[:, 0], any_rows[:], 0.0, BIG,
                                                       ALU.is_le, ALU.mult))
                    settled(n + 1, nc.vector.tensor_tensor(any_att[:, 0], any_att[:, 0], any_neg_e[:, 0],
                                                           ALU.add))
                    settled(n + 2, nc.vector.tensor_scalar(any_att[:, 1], any_rows[:], 0.0, BIG,
                                                           ALU.is_ge, ALU.mult))
                    settled(n + 3, nc.vector.tensor_tensor(any_att[:, 1], any_att[:, 1], any_neg_e[:, 1],
                                                           ALU.add))
                    settled(n + 4, nc.vector.tensor_tensor(any_att[:, 0], any_att[:, 0], any_att[:, 1],
                                                           ALU.min))
                    nc.vector.tensor_reduce(least[:, 0, h, 0:1], any_att[:, 0], AX_X, ALU.min) \
                      .then_inc(masked, 1)
                    dve.wait_ge(in_any_adj, 16 * (t + 1))
                    for g in range(GROUPS):
                        m = GROUPS * (HEADS * t + h) + g
                        dve.wait_ge(turned, m + 1)
                        wait(dve, gathered_part, m - 1)
                        nc.vector.tensor_tensor(any_weighted[:, g % 2], ps_att[g % 2][:, :, 0, :],
                                                any_adj_t[:, g * GROUP:(g + 1) * GROUP], ALU.mult) \
                          .then_inc(weighted_ready, 1)
                invert(t, 0, former=0)

            AHEAD = 3
            PER_TILE = QUARTERS * HEADS

            def pair(i, last):
                for slot in range(2):
                    t = 2 * i + slot
                    for g in range(GROUPS):
                        weigh(t, g)
                        if g == 0:
                            invert(t, slot)
                        for k in range(AHEAD + PER_TILE * g // GROUPS, AHEAD + PER_TILE * (g + 1) // GROUPS):
                            if k < PER_TILE and not (last and slot):
                                mask_scores(t + 1, 1 - slot, k)
                            elif k >= PER_TILE and not last:
                                mask_scores(t + 2, slot, k - PER_TILE)

            dve.wait_ge(in_flag, 16)
            negative = dve.value_load(flag[0:1, 0:1], min_val=0, max_val=N)
            with dve.If(negative > 0):
                dve.wait_ge(in_any_const, 16)
                nc.vector.memset(row_parts[:], 0.0).then_inc(any_step, 1)
                dve.wait_ge(any_step, 1)
                mask_any(0)
                with dve.Fori(1, TILES) as t:
                    mask_any(t)
            with dve.Else():
                dve.wait_ge(in_e, 16 * HEADS)
                for k in range(PER_TILE):
                    mask_scores(0, 0, k)
                for k in range(AHEAD):
                    mask_scores(1, 1, k)
                pair(0, False)
                with dve.Fori(1, TILES // 2 - 1) as i:
                    pair(i, False)
                pair(TILES // 2 - 1, True)

        @block.tensor
        def _(pe):
            pe.wait_ge(in_const, 32)

            def turn(t, slot, g):
                n = GROUPS * t + g
                if g == 0:
                    pe.wait_ge(att_ready, HEADS * (t + 1))
                wait(pe, weighted_ready, n - 1)
                for k in range(GROUP):
                    c = g * GROUP + k
                    for h in range(HEADS):
                        last = nc.tensor.transpose(ps_att[g % 2][:, k, h, :],
                                                   att[:, slot, h, c * P:(c + 1) * P], identity[:])
                last.then_inc(turned, 1)

            def gather(t, g):
                pe.wait_ge(weighted_ready, GROUPS * t + g + 1)
                if g == 0:
                    wait(pe, gathered_ready, t)
                for k in range(GROUP):
                    c = g * GROUP + k
                    last = nc.tensor.matmul(ps_gathered[:, 0:HEADS * P], x_rows[:, c, :],
                                            weighted[:, g % 2, k].rearrange("p h r -> p (h r)"),
                                            start=c == 0, stop=c == TILES - 1)
                last.then_inc(gathered_part, 1)

            def project(t):
                pe.wait_ge(gathered_ready, t + 1)
                wait(pe, support_copied, t)
                for h in range(HEADS):
                    last = nc.tensor.matmul(ps_support[:, h * P:(h + 1) * P], gathered[:, h, :], w[:, h, :],
                                            start=True, stop=True)
                last.then_inc(head_summed, 1)

            def turn_support(t):
                pe.wait_ge(support_ready, t + 2)
                nc.tensor.transpose(ps_support[:, HEADS * P:(HEADS + 1) * P], support[:], identity[:]) \
                  .then_inc(support_turned, 1)

            def any_tile(t):
                for h in range(HEADS):
                    pe.wait_ge(att_ready, HEADS * t + h + 1)
                    if h == 0:
                        wait(pe, gathered_ready, t)
                    for g in range(GROUPS):
                        m = GROUPS * (HEADS * t + h) + g
                        wait(pe, weighted_ready, m - 1)
                        for k in range(GROUP):
                            c = g * GROUP + k
                            last = nc.tensor.transpose(ps_att[g % 2][:, k, 0, :],
                                                       any_att[:, 0, c * P:(c + 1) * P], identity[:])
                        last.then_inc(turned, 1)
                        pe.wait_ge(weighted_ready, m + 1)
                        for k in range(GROUP):
                            c = g * GROUP + k
                            last = nc.tensor.matmul(ps_gathered[:, h * P:(h + 1) * P], x_rows[:, c, :],
                                                    any_weighted[:, g % 2, k], start=c == 0,
                                                    stop=c == TILES - 1)
                        last.then_inc(gathered_part, 1)
                project(t)
                turn_support(t)

            def pair(i, first, last):
                for slot in range(2):
                    t = 2 * i + slot
                    for g in range(GROUPS):
                        if g < GROUPS - 1:
                            turn(t, slot, g + 1)
                        elif not (last and slot):
                            turn(t + 1, 1 - slot, 0)
                        gather(t, g)
                        if not (first and slot == 0):
                            if g == 0:
                                project(t - 1)
                            if g == 5:
                                turn_support(t - 1)

            pe.wait_ge(in_flag, 16)
            negative = pe.value_load(flag[0:1, 0:1], min_val=0, max_val=N)
            with pe.If(negative > 0):
                pe.wait_ge(in_x, 16)
                any_tile(0)
                with pe.Fori(1, TILES) as t:
                    any_tile(t)
            with pe.Else():
                pe.wait_ge(in_x, 16)
                turn(0, 0, 0)
                pair(0, True, False)
                with pe.Fori(1, TILES // 2 - 1) as i:
                    pair(i, False, False)
                pair(TILES // 2 - 1, False, True)
                project(TILES - 1)
                turn_support(TILES - 1)


def update_phase(nc, io, dram):
    with ExitStack() as stack:
        sbuf, psum, semaphore = memory(nc, stack)
        GATES = 3
        CELLS = 2
        w_in = sbuf("p2_w_in", [H, CELLS, GATES, H])
        w_state = sbuf("p2_w_state", [H, CELLS, GATES, H])
        bias_in = sbuf("p2_bias_in", [H, CELLS, GATES])
        bias_state = sbuf("p2_bias_state", [H, CELLS, GATES])
        bias_sum = sbuf("p2_bias_sum", [H, CELLS, GATES])
        bias_half = sbuf("p2_bias_half", [H, CELLS, GATES])
        bias_state_half = sbuf("p2_bias_state_half", [H, CELLS, GATES])
        identity = sbuf("p2_identity", [P, P])
        diag = sbuf("p2_diag", [P, TILES])
        support = sbuf("p2_support", [H, 2, CELLS, CHUNK])
        state = sbuf("p2_state", [H, 2, CHUNK])
        x_rows = sbuf("p2_x_rows", [P, TILES, H])
        reset = sbuf("p2_reset", [H, CHUNK])
        update = sbuf("p2_update", [H, CHUNK])
        half_state = sbuf("p2_half_state", [H, CHUNK])
        gated = sbuf("p2_gated", [H, CHUNK])
        pre = sbuf("p2_pre", [H, CHUNK])
        new = sbuf("p2_new", [H, CHUNK])
        change = sbuf("p2_change", [H, CHUNK])
        scaled = sbuf("p2_scaled", [H, CHUNK])
        cell_out = sbuf("p2_cell_out", [H, CELLS, CHUNK])
        both = sbuf("p2_both", [H, CHUNK])
        mixed = sbuf("p2_mixed", [P, TILES, H])
        stats = sbuf("p2_stats", [P, TILES, nc.vector.BN_STATS_DIM])
        moments = sbuf("p2_moments", [P, TILES, 2])
        row_parts = sbuf("p2_row_parts", [P, QUARTERS, TILES])
        row_sum = sbuf("p2_row_sum", [P, 3, TILES])
        roots = sbuf("p2_roots", [P, 2, TILES])
        inverse = sbuf("p2_inverse", [P, 2, TILES])
        variance = sbuf("p2_variance", [P, TILES])
        gates = [[psum(f"p2_gate{c}{g}", [P, CHUNK]) for g in range(4)] for c in range(CELLS)]

        in_const = semaphore("p2_in_const")
        in_chunk = [semaphore(f"p2_in_chunk{i}") for i in range(2)]
        bias_step = semaphore("p2_bias_step")
        bias_ready = semaphore("p2_bias_ready")
        gates_summed = semaphore("p2_gates_summed")
        act_gates = semaphore("p2_act_gates")
        gated_ready = semaphore("p2_gated_ready")
        pre_ready = semaphore("p2_pre_ready")
        new_ready = semaphore("p2_new_ready")
        change_ready = semaphore("p2_change_ready")
        scaled_ready = semaphore("p2_scaled_ready")
        cell_ready = semaphore("p2_cell_ready")
        both_ready = semaphore("p2_both_ready")
        both_turned = semaphore("p2_both_turned")
        mixed_ready = semaphore("p2_mixed_ready")
        stats_ready = semaphore("p2_stats_ready")
        moments_ready = semaphore("p2_moments_ready")
        end_step = semaphore("p2_end_step")
        roots_ready = semaphore("p2_roots_ready")
        inverse_ready = semaphore("p2_inverse_ready")
        normed = semaphore("p2_normed")
        scaled_x = semaphore("p2_scaled_x")
        out_x = semaphore("p2_out_x")
        passed = semaphore("p2_passed")

        block = stack.enter_context(nc.Block())

        @block.sync
        def _(sync):
            for c, cell in enumerate(("edge", "node")):
                sync.dma_start(w_in[:, c], io[f"{cell}_w_in"]).then_inc(in_const, 16)
                sync.dma_start(w_state[:, c], io[f"{cell}_w_state"]).then_inc(in_const, 16)
                sync.dma_start(bias_in[:, c], io[f"{cell}_bias_in"]).then_inc(in_const, 16)
                sync.dma_start(bias_state[:, c], io[f"{cell}_bias_state"]).then_inc(in_const, 16)
            sync.dma_start(identity[:], io["identity"]).then_inc(in_const, 16)
            sync.dma_start(diag[:], io["diag_cols"]).then_inc(in_const, 16)
            sync.dma_start(row_parts[:], dram["row_parts"]).then_inc(in_const, 16)
            sync.dma_start(x_rows[:], io["x"].rearrange("(t p) h -> p t h", p=P)).then_inc(in_const, 16)

            def pair(i):
                for half in range(2):
                    c = 2 * i + half
                    wait(sync, cell_ready, 2 * (c - 1))
                    wait(sync, gates_summed, 2 * (c - 1))
                    wait(sync, change_ready, 2 * (c - 1))
                    at = bass.ds(c * CHUNK, CHUNK)
                    sync.dma_start(support[:, half, 0], dram["sums"][:, at]).then_inc(in_chunk[half], 16)
                    sync.dma_start(support[:, half, 1], dram["support"][:, at]).then_inc(in_chunk[half], 16)
                    sync.dma_start(state[:, half], io["x_cols"][:, at]).then_inc(in_chunk[half], 16)

            pair(0)
            with sync.Fori(1, CHUNKS // 2) as i:
                pair(i)
            sync.wait_ge(normed, TILES)
            sync.dma_start(dram["x1"], mixed[:]).then_inc(out_x, 16)
            sync.wait_ge(scaled_x, TILES)
            sync.dma_start(dram["x1_scaled"], x_rows[:]).then_inc(out_x, 16)
            sync.wait_ge(out_x, 32)

        @block.gpsimd
        def _(pool):
            def cell(n, half):
                pool.wait_ge(new_ready, n + 1)
                wait(pool, scaled_ready, n)
                nc.gpsimd.tensor_tensor(change[:], state[:, half], new[:], ALU.subtract) \
                  .then_inc(change_ready, 1)

            def pair(i):
                for half in range(2):
                    for k in range(CELLS):
                        cell(CELLS * (2 * i + half) + k, half)
                    c = 2 * i + half
                    pool.wait_ge(cell_ready, CELLS * (c + 1))
                    wait(pool, both_turned, c)
                    nc.gpsimd.tensor_tensor(both[:], cell_out[:, 0], cell_out[:, 1], ALU.add) \
                      .then_inc(both_ready, 1)

            pool.wait_ge(in_chunk[0], 48)
            pool.wait_ge(in_chunk[1], 48)
            pair(0)
            with pool.Fori(1, CHUNKS // 2) as i:
                for half in range(2):
                    pool.wait_ge(in_chunk[half], 48 * (i + 1))
                pair(i)

        @block.scalar
        def _(act):
            act.wait_ge(bias_ready, 1)

            def cell(n, k):
                ps = gates[k]
                act.wait_ge(gates_summed, n + 1)
                wait(act, gated_ready, n)
                wait(act, scaled_ready, n)
                nc.scalar.activation(reset[:], ps[0][:], ACT.Tanh, bias=bias_half[:, k, 0:1], scale=0.5)
                nc.scalar.activation(half_state[:], ps[3][:], ACT.Identity,
                                     bias=bias_state_half[:, k, 2:3], scale=0.5)
                nc.scalar.activation(update[:], ps[1][:], ACT.Tanh, bias=bias_half[:, k, 1:2], scale=0.5) \
                  .then_inc(act_gates, 1)
                act.wait_ge(pre_ready, n + 1)
                wait(act, change_ready, n)
                wait(act, cell_ready, n)
                nc.scalar.activation(new[:], pre[:], ACT.Tanh, bias=bias_in[:, k, 2:3]) \
                  .then_inc(new_ready, 1)

            for k in range(CELLS):
                cell(k, k)
            with act.Fori(1, CHUNKS) as c:
                for k in range(CELLS):
                    cell(CELLS * c + k, k)
            act.wait_ge(end_step, 5)
            nc.scalar.activation(roots[:, 0], variance[:], ACT.Sqrt)
            nc.scalar.activation(roots[:, 1], row_sum[:, 2], ACT.Sqrt).then_inc(roots_ready, 1)
            act.wait_ge(inverse_ready, 1)
            for t in range(TILES):
                act.wait_ge(normed, t + 1)
                nc.scalar.activation(x_rows[:, t], mixed[:, t], ACT.Copy, scale=inverse[:, 1, t:t + 1]) \
                  .then_inc(scaled_x, 1)

        @block.vector
        def _(dve):
            dve.wait_ge(in_const, 16 * 12)
            nc.vector.tensor_tensor(bias_sum[:], bias_in[:], bias_state[:], ALU.add).then_inc(bias_step, 1)
            nc.vector.tensor_scalar(bias_state_half[:], bias_state[:], 0.5, None, ALU.mult)
            dve.wait_ge(bias_step, 1)
            nc.vector.tensor_scalar(bias_half[:], bias_sum[:], 0.5, None, ALU.mult).then_inc(bias_ready, 1)

            def cell(c, n, k):
                ps = gates[k]
                dve.wait_ge(act_gates, n + 1)
                nc.vector.scalar_tensor_tensor(gated[:], reset[:], 1.0, half_state[:], ALU.add, ALU.mult) \
                  .then_inc(gated_ready, 1)
                dve.wait_ge(gated_ready, n + 1)
                wait(dve, new_ready, n)
                nc.vector.tensor_tensor(pre[:], ps[2][:], gated[:], ALU.add).then_inc(pre_ready, 1)
                dve.wait_ge(change_ready, n + 1)
                nc.vector.scalar_tensor_tensor(scaled[:], update[:], 1.0, change[:], ALU.add, ALU.mult) \
                  .then_inc(scaled_ready, 1)
                dve.wait_ge(scaled_ready, n + 1)
                wait(dve, both_ready, c)
                nc.vector.scalar_tensor_tensor(cell_out[:, k], scaled[:], 0.5, new[:], ALU.mult, ALU.add) \
                  .then_inc(cell_ready, 1)

            def chunk(c):
                for k in range(CELLS):
                    cell(c, CELLS * c + k, k)
                dve.wait_ge(both_turned, c + 1)
                turned = gates[0][0][:].rearrange("p (j h) -> p j h", j=ROWS)
                for j in range(ROWS):
                    last = nc.vector.scalar_tensor_tensor(
                        mixed[:, bass.ds(c * ROWS + j, 1), :].rearrange("p j h -> p (j h)"),
                        turned[:, j], diag[:, bass.ds(c * ROWS + j, 1)],
                        x_rows[:, bass.ds(c * ROWS + j, 1), :].rearrange("p j h -> p (j h)"),
                        ALU.mult, ALU.add)
                last.then_inc(mixed_ready, 1)
                wait_apart(dve, mixed_ready, c + 1, passed)
                for j in range(ROWS):
                    last = nc.vector.bn_stats(
                        stats[:, bass.ds(c * ROWS + j, 1), :].rearrange("p j s -> p (j s)"),
                        mixed[:, bass.ds(c * ROWS + j, 1), :].rearrange("p j h -> p (j h)"))
                last.then_inc(stats_ready, 1)

            chunk(0)
            with dve.Fori(1, CHUNKS) as c:
                chunk(c)
            dve.wait_ge(stats_ready, CHUNKS)
            for t in range(TILES):
                last = nc.vector.bn_aggr(moments[:, t], stats[:, t])
            last.then_inc(moments_ready, 1)
            dve.wait_ge(moments_ready, 1)
            nc.vector.tensor_scalar(variance[:], moments[:, :, 1], EPS, None, ALU.add).then_inc(end_step, 1)
            for k in range(2):
                nc.vector.tensor_tensor(row_sum[:, k], row_parts[:, 2 * k], row_parts[:, 2 * k + 1], ALU.add) \
                  .then_inc(end_step, 1)
            dve.wait_ge(end_step, 3)
            nc.vector.tensor_tensor(row_sum[:, 0], row_sum[:, 0], row_sum[:, 1], ALU.add).then_inc(end_step, 1)
            dve.wait_ge(end_step, 4)
            nc.vector.tensor_scalar(row_sum[:, 2], row_sum[:, 0], 1.0, None, ALU.add).then_inc(end_step, 1)
            dve.wait_ge(roots_ready, 1)
            nc.vector.reciprocal(inverse[:], roots[:]).then_inc(inverse_ready, 1)
            dve.wait_ge(inverse_ready, 1)
            for t in range(TILES):
                nc.vector.tensor_scalar(mixed[:, t], mixed[:, t], moments[:, t, 0:1], inverse[:, 0, t:t + 1],
                                        ALU.subtract, ALU.mult).then_inc(normed, 1)
            dve.wait_ge(normed, TILES)
            nc.vector.tensor_copy(dram["d_inverse"][:], inverse[:, 1]).then_inc(end_step, 1)

        @block.tensor
        def _(pe):
            pe.wait_ge(in_const, 16 * 12)

            def cell(n, k, half):
                ps = gates[k]
                wait(pe, pre_ready, n - 1)
                wait(pe, act_gates, n - 1)
                s, x = support[:, half, k], state[:, half]
                for g in range(2):
                    nc.tensor.matmul(ps[g][:], w_in[:, k, g], s, start=True, stop=False)
                    nc.tensor.matmul(ps[g][:], w_state[:, k, g], x, start=False, stop=True)
                nc.tensor.matmul(ps[2][:], w_in[:, k, 2], s, start=True, stop=True)
                nc.tensor.matmul(ps[3][:], w_state[:, k, 2], x, start=True, stop=True) \
                  .then_inc(gates_summed, 1)

            def turn(c):
                pe.wait_ge(both_ready, c + 1)
                for j in range(ROWS):
                    last = nc.tensor.transpose(gates[0][0][:, j * P:(j + 1) * P], both[:, j * P:(j + 1) * P],
                                               identity[:])
                last.then_inc(both_turned, 1)

            def pair(i):
                for half in range(2):
                    c = 2 * i + half
                    wait(pe, mixed_ready, c)
                    pe.wait_ge(in_chunk[half], 48 * (i + 1))
                    for k in range(CELLS):
                        cell(CELLS * c + k, k, half)
                    turn(c)

            pair(0)
            with pe.Fori(1, CHUNKS // 2) as i:
                pair(i)


def propagate_phase(nc, io, dram, out):
    with ExitStack() as stack:
        sbuf, psum, semaphore = memory(nc, stack)
        RING = 4
        x1 = sbuf("p3_x1", [P, TILES, H])
        scaled = sbuf("p3_scaled", [P, TILES, H])
        own = sbuf("p3_own", [P, ROWS, H])
        identity = sbuf("p3_identity", [P, P])
        w1 = sbuf("p3_w1", [H, H])
        adj_t = sbuf("p3_adj_t", [P, RING, ROWS, GROUP, P])
        gathered = sbuf("p3_gathered", [H, CHUNK])
        relu = sbuf("p3_relu", [P, ROWS, H])
        mixed = sbuf("p3_mixed", [P, ROWS, H])
        stats = sbuf("p3_stats", [P, ROWS, nc.vector.BN_STATS_DIM])
        moments = sbuf("p3_moments", [P, ROWS, 2])
        variance = sbuf("p3_variance", [P, ROWS])
        root = sbuf("p3_root", [P, ROWS])
        inverse = sbuf("p3_inverse", [P, ROWS])
        result = sbuf("p3_result", [P, 2, ROWS, H])
        ps_gathered = [psum(f"p3_ps_gathered{i}", [P, CHUNK]) for i in range(2)]
        ps_out = [psum(f"p3_ps_out{i}", [P, ROWS, H]) for i in range(2)]

        in_const = semaphore("p3_in_const")
        in_adj = [semaphore(f"p3_in_adj{i}") for i in range(RING)]
        own_ready = semaphore("p3_own_ready")
        group_done = semaphore("p3_group_done")
        chunk_done = semaphore("p3_chunk_done")
        gathered_ready = semaphore("p3_gathered_ready")
        out_summed = semaphore("p3_out_summed")
        relu_ready = semaphore("p3_relu_ready")
        mixed_ready = semaphore("p3_mixed_ready")
        stats_ready = semaphore("p3_stats_ready")
        moments_ready = semaphore("p3_moments_ready")
        variance_ready = semaphore("p3_variance_ready")
        root_ready = semaphore("p3_root_ready")
        inverse_ready = semaphore("p3_inverse_ready")
        result_ready = semaphore("p3_result_ready")
        out_done = [semaphore(f"p3_out_done{i}") for i in range(2)]
        passed = semaphore("p3_passed")

        block = stack.enter_context(nc.Block())

        @block.sync
        def _(sync):
            sync.dma_start(scaled[:], dram["x1_scaled"]).then_inc(in_const, 16)

            def load_chunk(c):
                for g in range(GROUPS):
                    slot = g % RING
                    wait(sync, group_done, GROUPS * c + g - RING + 1)
                    sync.dma_start(
                        adj_t[:, slot],
                        io["adj_t"][bass.ds(c * ROWS, ROWS), :, g * GROUP:(g + 1) * GROUP, :]
                        .rearrange("j p c r -> p j c r")).then_inc(in_adj[slot], 16)
                    if isinstance(c, int) and g == 0:
                        sync.dma_start(identity[:], io["identity"]).then_inc(in_const, 16)
                        sync.dma_start(w1[:], io["w1_t"]).then_inc(in_const, 16)
                        sync.dma_start(x1[:], dram["x1"]).then_inc(in_const, 16)

            load_chunk(0)
            with sync.Fori(1, CHUNKS) as c:
                load_chunk(c)

        @block.gpsimd
        def _(pool):
            pool.wait_ge(in_const, 64)

            def chunk(c):
                wait(pool, chunk_done, c)
                nc.gpsimd.tensor_copy(own[:], scaled[:, bass.ds(c * ROWS, ROWS), :]).then_inc(own_ready, 1)

            chunk(0)
            with pool.Fori(1, CHUNKS) as c:
                chunk(c)

        @block.scalar
        def _(act):
            def chunk(c, half):
                act.wait_ge(chunk_done, c + 1)
                wait(act, out_summed, c)
                nc.scalar.copy(gathered[:], ps_gathered[half][:]).then_inc(gathered_ready, 1)
                act.wait_ge(out_summed, c + 1)
                wait(act, mixed_ready, c)
                for j in range(ROWS):
                    last = nc.scalar.activation(relu[:, j], ps_out[half][:, j], ACT.Relu,
                                                scale=dram["d_inverse"][:, bass.ds(c * ROWS + j, 1)])
                last.then_inc(relu_ready, 1)
                act.wait_ge(variance_ready, c + 1)
                nc.scalar.activation(root[:], variance[:], ACT.Sqrt).then_inc(root_ready, 1)
                act.wait_ge(result_ready, c + 1)
                act.dma_start(out[bass.ds(c * CHUNK, CHUNK), :].rearrange("(j p) h -> p j h", p=P),
                              result[:, half]).then_inc(out_done[half], 16)

            def pair(i):
                for half in range(2):
                    chunk(2 * i + half, half)

            pair(0)
            with act.Fori(1, CHUNKS // 2) as i:
                pair(i)
            for half in range(2):
                act.wait_ge(out_done[half], 16 * CHUNKS // 2)

        @block.vector
        def _(dve):
            dve.wait_ge(in_const, 64)

            def chunk(c, i, half):
                dve.wait_ge(relu_ready, c + 1)
                nc.vector.tensor_tensor(mixed[:], relu[:], x1[:, bass.ds(c * ROWS, ROWS), :], ALU.add) \
                  .then_inc(mixed_ready, 1)
                dve.wait_ge(mixed_ready, c + 1)
                for j in range(ROWS):
                    last = nc.vector.bn_stats(stats[:, j], mixed[:, j])
                last.then_inc(stats_ready, 1)
                wait_apart(dve, stats_ready, c + 1, passed)
                for j in range(ROWS):
                    last = nc.vector.bn_aggr(moments[:, j], stats[:, j])
                last.then_inc(moments_ready, 1)
                dve.wait_ge(moments_ready, c + 1)
                wait(dve, root_ready, c)
                nc.vector.tensor_scalar(variance[:], moments[:, :, 1], EPS, None, ALU.add) \
                  .then_inc(variance_ready, 1)
                dve.wait_ge(root_ready, c + 1)
                nc.vector.reciprocal(inverse[:], root[:]).then_inc(inverse_ready, 1)
                dve.wait_ge(inverse_ready, c + 1)
                wait(dve, out_done[half], 16 * i)
                for j in range(ROWS):
                    last = nc.vector.tensor_scalar(result[:, half, j], mixed[:, j], moments[:, j, 0:1],
                                                   inverse[:, j:j + 1], ALU.subtract, ALU.mult)
                last.then_inc(result_ready, 1)

            def pair(i):
                for half in range(2):
                    chunk(2 * i + half, i, half)

            pair(0)
            with dve.Fori(1, CHUNKS // 2) as i:
                pair(i)

        @block.tensor
        def _(pe):
            pe.wait_ge(in_const, 64)

            def chunk(c, half):
                wait(pe, gathered_ready, c - 1)
                for g in range(GROUPS):
                    slot = g % RING
                    pe.wait_ge(in_adj[slot], 16 * (GROUPS // RING * c + g // RING + 1))
                    for k in range(GROUP):
                        t = g * GROUP + k
                        last = nc.tensor.matmul(ps_gathered[half][:], scaled[:, t, :], adj_t[:, slot, :, k, :],
                                                start=t == 0, stop=False)
                    last.then_inc(group_done, 1)
                pe.wait_ge(own_ready, c + 1)
                for j in range(ROWS):
                    last = nc.tensor.matmul(ps_gathered[half][:, j * P:(j + 1) * P], own[:, j], identity[:],
                                            start=False, stop=j == ROWS - 1)
                last.then_inc(chunk_done, 1)
                pe.wait_ge(gathered_ready, c + 1)
                wait(pe, relu_ready, c - 1)
                for j in range(ROWS):
                    last = nc.tensor.matmul(ps_out[half][:, j], gathered[:, j * P:(j + 1) * P], w1[:],
                                            start=True, stop=True)
                last.then_inc(out_summed, 1)

            def pair(i):
                for half in range(2):
                    chunk(2 * i + half, half)

            pair(0)
            with pe.Fori(1, CHUNKS // 2) as i:
                pair(i)


def two_layers(nc, io, out):
    dram = {
        "scores": nc.dram_tensor("neg_scores", [SCORES, N], F32).ap(),
        "sums": nc.dram_tensor("neighbour_sums", [H, N], F32).ap(),
        "support": nc.dram_tensor("edge_support", [H, N], F32).ap(),
        "row_parts": nc.dram_tensor("row_parts", [P, QUARTERS, TILES], F32).ap(),
        "flag": nc.dram_tensor("negative_flag", [1, 1], I32).ap(),
        "x1": nc.dram_tensor("x1", [P, TILES, H], F32).ap(),
        "x1_scaled": nc.dram_tensor("x1_scaled", [P, TILES, H], F32).ap(),
    }
    with nc.sbuf_tensor("d_inverse", [P, TILES], F32) as d_inverse:
        dram["d_inverse"] = d_inverse
        score_phase(nc, io, dram)
        attention_phase(nc, io, dram)
        update_phase(nc, io, dram)
        propagate_phase(nc, io, dram, out)


def score_selection():
    select = np.zeros((P, SCORES), np.float32)
    for h in range(HEADS):
        for score, positive_half in ((h, 0), (HEADS + h, 1)):
            for at, diag_at, half in ((POS, POS_DIAG, positive_half), (NEG, NEG_DIAG, 1 - positive_half)):
                column = 2 * h + half
                for s in range(SPLITS):
                    select[at + 1 + s * SCORES + column, score] = -1.0
                select[diag_at + column, score] = 1.0
    return select


def kernel(x, adj, L0_gnn_gat_W, L0_gnn_gat_a, L0_gnn_edge_Wih, L0_gnn_edge_Whh, L0_gnn_edge_bih,
           L0_gnn_edge_bhh, L0_gnn_node_Wih, L0_gnn_node_Whh, L0_gnn_node_bih, L0_gnn_node_bhh, L1_gnn_W):
    import concourse.bacc as bacc
    from concourse.bass_utils import run_bass_kernel_spmd

    x, adj = np.asarray(x), np.asarray(adj)
    gat_w, gat_a = np.asarray(L0_gnn_gat_W), np.asarray(L0_gnn_gat_a)
    diag = np.diagonal(adj)

    def gate_rows(w):
        return np.asarray(w).reshape(3, H, H).transpose(2, 0, 1)

    def gate_bias(b):
        return np.asarray(b).reshape(3, H).T

    arrays = {
        "x": x,
        "x_cols": x.T,
        "adj": adj,
        "adj_t": adj.reshape(TILES, P, TILES, P).transpose(0, 3, 2, 1),
        "diag_row": diag.reshape(1, N),
        "diag_cols": diag.reshape(TILES, P).T,
        "w": gat_w.transpose(1, 0, 2),
        "w_t": gat_w.transpose(2, 0, 1),
        "a": gat_a.reshape(HEADS, 2, H).transpose(2, 0, 1).reshape(H, SCORES),
        "edge_w_in": gate_rows(L0_gnn_edge_Wih),
        "edge_w_state": gate_rows(L0_gnn_edge_Whh),
        "edge_bias_in": gate_bias(L0_gnn_edge_bih),
        "edge_bias_state": gate_bias(L0_gnn_edge_bhh),
        "node_w_in": gate_rows(L0_gnn_node_Wih),
        "node_w_state": gate_rows(L0_gnn_node_Whh),
        "node_bias_in": gate_bias(L0_gnn_node_bih),
        "node_bias_state": gate_bias(L0_gnn_node_bhh),
        "w1_t": np.asarray(L1_gnn_W).T,
        "identity": np.eye(P, dtype=np.float32),
        "off_diagonal": 1 - np.eye(P, dtype=np.float32),
        "select": score_selection(),
    }
    arrays = {name: np.ascontiguousarray(a) for name, a in arrays.items()}
    nc = bacc.Bacc("TRN2", target_bir_lowering=False, num_devices=1, dynamic_dma_scratch_size=1024)
    io = {name: nc.dram_tensor(f"in_{name}", a.shape, mybir.dt.from_np(a.dtype), kind="ExternalInput").ap()
          for name, a in arrays.items()}
    out = nc.dram_tensor("out", (N, H), F32, kind="ExternalOutput").ap()
    two_layers(nc, io, out)
    ran = run_bass_kernel_spmd(nc, [{f"in_{name}": a for name, a in arrays.items()}], core_ids=[0])
    return ran.results[0]["out"]
```

```python
from contextlib import ExitStack

import numpy as np

import concourse.bass as bass
from concourse import mybir
from concourse.alu_op_type import AluOpType as ALU

F32 = mybir.dt.float32
F32R = mybir.dt.float32r
BF16 = mybir.dt.bfloat16
I32 = mybir.dt.int32
ACT = mybir.ActivationFunctionType
AX_X = mybir.AxisListType.X

P = 128
N = 4096
H = 128
HEADS = 3
TILES = N // P
CHUNK = 512
CHUNKS = N // CHUNK
ROWS = CHUNK // P
GROUP = 4
GROUPS = TILES // GROUP
QUARTERS = 4
QUARTER = N // QUARTERS
SPLITS = 3
SCORES = 2 * HEADS
PARTS = 1 + SPLITS * SCORES
BAND = 32
NEG, SIGNED = 0, BAND
ODD = 2 * BAND
NEG_DIAG, POS_DIAG = 0, BAND
COUNT = BAND
SELECTED = COUNT + 1
BIG = 1e30
ALPHA = 0.2
EPS = 1e-5


def memory(nc, stack):
    def sbuf(name, shape, dtype=F32):
        return stack.enter_context(nc.sbuf_tensor(name, shape, dtype))

    def psum(name, shape, dtype=F32):
        return stack.enter_context(nc.psum_tensor(name, shape, dtype))

    def semaphore(name):
        return stack.enter_context(nc.semaphore(name))

    return sbuf, psum, semaphore


def wait(engine, semaphore, count):
    if not isinstance(count, int) or count > 0:
        engine.wait_ge(semaphore, count)


def wait_apart(engine, semaphore, count, passed):
    wait(engine, semaphore, count)
    if not isinstance(count, int):
        engine.sem_inc(passed, 1)


def score_phase(nc, io, dram, x_rows):
    with ExitStack() as stack:
        sbuf, psum, semaphore = memory(nc, stack)
        RING = 4
        x_high = sbuf("p0_x_high", [P, TILES, H], F32R)
        x_low = sbuf("p0_x_low", [P, TILES, H], F32R)
        x_cols = sbuf("p0_x_cols", [H, N])
        w = sbuf("p0_w", [H, HEADS, H])
        a = sbuf("p0_a", [H, SCORES])
        wa = sbuf("p0_wa", [H, SCORES])
        wa_placed = sbuf("p0_wa_placed", [H, 2 * BAND])
        select = sbuf("p0_select", [P, SELECTED])
        select_diag = sbuf("p0_select_diag", [2 * BAND, SELECTED])
        u = sbuf("p0_u", [P, TILES, SCORES])
        rest = sbuf("p0_rest", [P, 2, TILES, SCORES])
        u_parts = sbuf("p0_u_parts", [P, TILES, BAND], BF16)
        adj_t = sbuf("p0_adj_t", [P, RING, ROWS, GROUP, P])
        high = sbuf("p0_high", [P, RING, ROWS, GROUP, P], F32R)
        low = sbuf("p0_low", [P, 2, ROWS, GROUP, P], F32R)
        signs = sbuf("p0_signs", [P, RING, ROWS, GROUP, P], BF16)
        negative = sbuf("p0_negative", [P, 2, ROWS, GROUP, P], BF16)
        diag = sbuf("p0_diag", [P, 2, CHUNK])
        diag_x = sbuf("p0_diag_x", [P, CHUNK])
        sums = sbuf("p0_sums", [P, 2, CHUNK])
        terms = sbuf("p0_terms", [P, 2, CHUNK])
        diag_terms = sbuf("p0_diag_terms", [2 * BAND, 2, CHUNK])
        raw = sbuf("p0_raw", [SELECTED, 2, CHUNK])
        scores = sbuf("p0_scores", [SCORES, 2, CHUNK])
        most = sbuf("p0_most", [SELECTED, CHUNK])
        flag = sbuf("p0_flag", [SELECTED, 1], I32)
        ps_sums = [psum(f"p0_ps_sums{i}", [P, CHUNK]) for i in range(2)]
        ps_masks = [psum(f"p0_ps_masks{i}", [P, CHUNK]) for i in range(2)]
        ps_scores = psum("p0_ps_scores", [P, CHUNK])
        ps_setup = psum("p0_ps_setup", [P, CHUNK])
        ps_diag = [psum(f"p0_ps_diag{i}", [P, CHUNK]) for i in range(2)]

        in_w = semaphore("p0_in_w")
        in_x = semaphore("p0_in_x")
        in_x_rows = semaphore("p0_in_x_rows")
        in_adj = [semaphore(f"p0_in_adj{i}") for i in range(RING)]
        in_diag = [semaphore(f"p0_in_diag{i}") for i in range(2)]
        wa_summed = semaphore("p0_wa_summed")
        wa_ready = semaphore("p0_wa_ready")
        u_summed = semaphore("p0_u_summed")
        u_step = semaphore("p0_u_step")
        u_ready = semaphore("p0_u_ready")
        x_high_ready = semaphore("p0_x_high_ready")
        x_low_ready = semaphore("p0_x_low_ready")
        cleared = semaphore("p0_cleared")
        diag_summed = semaphore("p0_diag_summed")
        high_ready = semaphore("p0_high_ready")
        signs_ready = semaphore("p0_signs_ready")
        parts_ready = semaphore("p0_parts_ready")
        group_done = semaphore("p0_group_done")
        sums_ready = semaphore("p0_sums_ready")
        diag_x_ready = semaphore("p0_diag_x_ready")
        terms_ready = semaphore("p0_terms_ready")
        scores_summed = semaphore("p0_scores_summed")
        raw_ready = semaphore("p0_raw_ready")
        scores_ready = semaphore("p0_scores_ready")
        most_ready = semaphore("p0_most_ready")
        out_sums = [semaphore(f"p0_out_sums{i}") for i in range(2)]
        out_scores = [semaphore(f"p0_out_scores{i}") for i in range(2)]
        flag_ready = semaphore("p0_flag_ready")
        out_flag = semaphore("p0_out_flag")

        block = stack.enter_context(nc.Block())

        @block.sync
        def _(sync):
            sync.dma_start(w[:], io["w_t"]).then_inc(in_w, 16)
            sync.dma_start(a[:], io["a"]).then_inc(in_w, 16)
            sync.dma_start(select[:], io["select"]).then_inc(in_w, 16)
            sync.dma_start(select_diag[:], io["select_diag"]).then_inc(in_w, 16)
            sync.dma_start(x_cols[:], io["x_cols"]).then_inc(in_x, 16)
            sync.dma_start(x_rows[:], io["x"].rearrange("(t p) h -> p t h", p=P)).then_inc(in_x_rows, 16)

            def load_chunk(c):
                for g in range(GROUPS):
                    slot = g % RING
                    wait(sync, parts_ready, GROUPS * c + g - RING + 1)
                    sync.dma_start(
                        adj_t[:, slot],
                        io["adj_t"][bass.ds(c * ROWS, ROWS), :, g * GROUP:(g + 1) * GROUP, :]
                        .rearrange("j p c r -> p j c r")).then_inc(in_adj[slot], 16)

            load_chunk(0)
            with sync.Fori(1, CHUNKS) as c:
                load_chunk(c)
            sync.wait_ge(flag_ready, 1)
            sync.dma_start(dram["flag"], flag[COUNT:SELECTED, :]).then_inc(out_flag, 16)
            sync.wait_ge(out_flag, 16)

        @block.scalar
        def _(act):
            def load_diag(c, half):
                act.dma_start(diag[:, half], io["diag_row"][:, bass.ds(c * CHUNK, CHUNK)]
                              .broadcast_to([P, CHUNK])).then_inc(in_diag[half], 16)

            def raw_scores(c, half):
                act.wait_ge(scores_summed, c + 1)
                wait(act, scores_ready, c - 1)
                nc.scalar.copy(raw[:, half], ps_scores[0:SELECTED, :]).then_inc(raw_ready, 1)

            def store(c, half, last):
                act.wait_ge(sums_ready, c + 1)
                act.dma_start(dram["sums"][:, bass.ds(c * CHUNK, CHUNK)], sums[:, half]) \
                   .then_inc(out_sums[half], 16)
                act.wait_ge(scores_ready, c + 1)
                act.dma_start(dram["scores"][:, bass.ds(c * CHUNK, CHUNK)], scores[:, half]) \
                   .then_inc(out_scores[half], 16)
                if not last:
                    load_diag(c + 2, half)

            def chunk(c, half, former, last):
                for g in range(GROUPS):
                    slot, n = g % RING, GROUPS * c + g
                    act.wait_ge(in_adj[slot], 16 * (GROUPS // RING * c + g // RING + 1))
                    wait(act, group_done, n - RING + 1)
                    nc.scalar.copy(high[:, slot], adj_t[:, slot]).then_inc(high_ready, 1)
                    nc.scalar.activation(signs[:, slot], adj_t[:, slot], ACT.Sign).then_inc(signs_ready, 1)
                    if former and g == 5:
                        raw_scores(c - 1, 1 - half)
                    if former and g == 7:
                        store(c - 1, 1 - half, last)

            load_diag(0, 0)
            load_diag(1, 1)
            act.wait_ge(wa_summed, 1)
            nc.scalar.copy(wa[:], ps_setup[:, 0:SCORES]).then_inc(wa_ready, 1)
            act.wait_ge(in_x_rows, 16)
            for q in range(QUARTERS):
                part = slice(q * TILES // QUARTERS, (q + 1) * TILES // QUARTERS)
                nc.scalar.copy(x_high[:, part], x_rows[:, part]).then_inc(x_high_ready, 1)
            chunk(0, 0, False, False)
            chunk(1, 1, True, False)
            chunk(2, 0, True, False)
            chunk(3, 1, True, False)
            with act.Fori(2, CHUNKS // 2 - 1) as i:
                chunk(2 * i, 0, True, False)
                chunk(2 * i + 1, 1, True, False)
            chunk(CHUNKS - 2, 0, True, False)
            chunk(CHUNKS - 1, 1, True, True)
            raw_scores(CHUNKS - 1, 1)
            store(CHUNKS - 1, 1, True)
            for half in range(2):
                act.wait_ge(out_sums[half], 16 * CHUNKS // 2)
                act.wait_ge(out_scores[half], 16 * CHUNKS // 2)

        @block.vector
        def _(dve):
            nc.vector.memset(diag_terms[:], 0.0).then_inc(cleared, 1)
            nc.vector.memset(wa_placed[:], 0.0).then_inc(cleared, 1)
            nc.vector.memset(u_parts[:, :, 0:1], 1.0).then_inc(cleared, 1)
            nc.vector.memset(u_parts[:, :, PARTS:BAND], 0.0).then_inc(cleared, 1)
            nc.vector.memset(most[:], 0.0).then_inc(cleared, 1)
            dve.wait_ge(wa_ready, 1)
            dve.wait_ge(cleared, 5)
            for at in (NEG_DIAG, POS_DIAG):
                nc.vector.tensor_copy(wa_placed[:, at:at + SCORES], wa[:]).then_inc(wa_ready, 1)
            for q in range(QUARTERS):
                part = slice(q * TILES // QUARTERS, (q + 1) * TILES // QUARTERS)
                dve.wait_ge(x_high_ready, q + 1)
                nc.vector.tensor_tensor(x_low[:, part], x_rows[:, part], x_high[:, part].bitcast(F32),
                                        ALU.subtract).then_inc(x_low_ready, 1)
            dve.wait_ge(u_summed, 1)
            nc.vector.tensor_copy(u[:], ps_setup[:, 0:TILES * SCORES]
                                  .rearrange("p (t s) -> p t s", s=SCORES)).then_inc(u_step, 1)
            dve.wait_ge(u_step, 1)
            source = u[:]
            for s in range(SPLITS):
                part = u_parts[:, :, 1 + s * SCORES:1 + (s + 1) * SCORES]
                last = nc.vector.tensor_copy(part, source)
                last.then_inc(u_ready if s == SPLITS - 1 else u_step, 1)
                if s < SPLITS - 1:
                    dve.wait_ge(u_step, 2 * s + 2)
                    nc.vector.tensor_tensor(rest[:, s], source, part, ALU.subtract).then_inc(u_step, 1)
                    dve.wait_ge(u_step, 2 * s + 3)
                    source = rest[:, s]

            def diag_scores(c, half, i):
                dve.wait_ge(in_diag[half], 16 * (i + 1))
                dve.wait_ge(diag_summed, c + 1)
                wait(dve, scores_summed, c - 1)
                for at, sign in ((NEG_DIAG, ALU.is_lt), (POS_DIAG, ALU.is_gt)):
                    nc.vector.scalar_tensor_tensor(
                        diag_terms[at:at + SCORES, half], diag[at:at + SCORES, half], 0.0,
                        ps_diag[half][at:at + SCORES, :], sign, ALU.mult)

            def mask_sums(c, half):
                dve.wait_ge(group_done, GROUPS * (c + 1))
                nc.vector.tensor_copy(terms[:, half], ps_masks[half][:]).then_inc(terms_ready, 1)

            def neighbour_sums(c, half, i):
                nc.vector.tensor_tensor(diag_x[:], diag[:, half], x_cols[:, bass.ds(c * CHUNK, CHUNK)],
                                        ALU.mult).then_inc(diag_x_ready, 1)
                dve.wait_ge(diag_x_ready, c + 1)
                wait(dve, out_sums[half], 16 * i)
                nc.vector.tensor_tensor(sums[:, half], ps_sums[half][:], diag_x[:], ALU.subtract) \
                  .then_inc(sums_ready, 1)

            def final_scores(c, half, i):
                dve.wait_ge(raw_ready, c + 1)
                wait(dve, most_ready, c)
                nc.vector.tensor_tensor(most[COUNT:SELECTED], most[COUNT:SELECTED], raw[COUNT:SELECTED, half],
                                        ALU.max).then_inc(most_ready, 1)
                wait(dve, out_scores[half], 16 * i)
                nc.vector.scalar_tensor_tensor(scores[:, half], raw[0:SCORES, half], ALPHA, raw[0:SCORES, half],
                                               ALU.mult, ALU.min).then_inc(scores_ready, 1)

            def chunk(c, half, i, former):
                d, d_half, d_i = c - 1, 1 - half, i if half else i - 1
                for g in range(GROUPS):
                    slot, n = g % RING, GROUPS * c + g
                    dve.wait_ge(high_ready, n + 1)
                    wait(dve, group_done, n - 1)
                    nc.vector.tensor_tensor(low[:, g % 2], adj_t[:, slot], high[:, slot].bitcast(F32),
                                            ALU.subtract)
                    dve.wait_ge(signs_ready, n + 1)
                    nc.vector.tensor_scalar(negative[:, g % 2], signs[:, slot], 0.0, None, ALU.is_lt) \
                      .then_inc(parts_ready, 1)
                    if former and g == 1:
                        diag_scores(d, d_half, d_i)
                    if former and g == 2:
                        mask_sums(d, d_half)
                    if former and g == 3:
                        neighbour_sums(d, d_half, d_i)
                    if former and g == 6:
                        final_scores(d, d_half, d_i)

            chunk(0, 0, 0, False)
            chunk(1, 1, 0, True)
            chunk(2, 0, 1, True)
            chunk(3, 1, 1, True)
            with dve.Fori(2, CHUNKS // 2) as i:
                chunk(2 * i, 0, i, True)
                chunk(2 * i + 1, 1, i, True)
            c, i = CHUNKS - 1, CHUNKS // 2 - 1
            diag_scores(c, 1, i)
            mask_sums(c, 1)
            neighbour_sums(c, 1, i)
            final_scores(c, 1, i)
            dve.wait_ge(most_ready, CHUNKS)
            nc.vector.tensor_reduce(flag[COUNT:SELECTED], most[COUNT:SELECTED], AX_X, ALU.max).then_inc(flag_ready, 1)

        @block.tensor
        def _(pe):
            pe.wait_ge(in_w, 64)
            for h in range(HEADS):
                last = nc.tensor.matmul(ps_setup[:, 2 * h:2 * h + 2], w[:, h, :], a[:, 2 * h:2 * h + 2],
                                        start=True, stop=True)
            last.then_inc(wa_summed, 1)
            pe.wait_ge(in_x, 16)
            pe.wait_ge(wa_ready, 3)
            for t in range(TILES):
                last = nc.tensor.matmul(ps_setup[:, t * SCORES:(t + 1) * SCORES],
                                        x_cols[:, t * P:(t + 1) * P], wa[:], start=True, stop=True)
            last.then_inc(u_summed, 1)
            pe.wait_ge(u_ready, 1)
            pe.wait_ge(x_low_ready, QUARTERS)

            def score_sum(c, half):
                pe.wait_ge(terms_ready, c + 1)
                wait(pe, raw_ready, c)
                nc.tensor.matmul(ps_scores[0:SELECTED, :], select[:], terms[:, half], start=True, stop=False)
                nc.tensor.matmul(ps_scores[0:SELECTED, :], select_diag[:], diag_terms[:, half],
                                 start=False, stop=True).then_inc(scores_summed, 1)

            def chunk(c, half, former):
                wait(pe, sums_ready, c - 1)
                wait(pe, terms_ready, c - 1)
                nc.tensor.matmul(ps_diag[half][0:2 * BAND, :], wa_placed[:], x_cols[:, bass.ds(c * CHUNK, CHUNK)],
                                 start=True, stop=True).then_inc(diag_summed, 1)
                for g in range(GROUPS):
                    slot = g % RING
                    pe.wait_ge(parts_ready, GROUPS * c + g + 1)
                    for k in range(GROUP):
                        t = g * GROUP + k
                        first, final = t == 0, t == TILES - 1
                        adj_high, adj_low = high[:, slot, :, k, :], low[:, g % 2, :, k, :]
                        nc.tensor.matmul(ps_sums[half][:], x_high[:, t, :], adj_high, start=first, stop=False)
                        nc.tensor.matmul(ps_sums[half][:], x_high[:, t, :], adj_low, start=False, stop=False)
                        nc.tensor.matmul(ps_sums[half][:], x_low[:, t, :], adj_high, start=False, stop=final)
                    for k in range(GROUP):
                        t = g * GROUP + k
                        first, final = t < 2, t >= TILES - 2
                        for kind, mask in ((NEG, negative[:, g % 2, :, k, :]), (SIGNED, signs[:, slot, :, k, :])):
                            at = kind + t % 2 * ODD
                            last = nc.tensor.matmul(ps_masks[half][at:at + BAND, :], u_parts[:, t, :], mask,
                                                    start=first, stop=final)
                    last.then_inc(group_done, 1)
                    if former and g == 2:
                        score_sum(c - 1, 1 - half)

            chunk(0, 0, False)
            chunk(1, 1, True)
            with pe.Fori(1, CHUNKS // 2) as i:
                chunk(2 * i, 0, True)
                chunk(2 * i + 1, 1, True)
            score_sum(CHUNKS - 1, 1)


def attention_phase(nc, io, dram, x_rows):
    with ExitStack() as stack:
        sbuf, psum, semaphore = memory(nc, stack)
        STAGES = QUARTERS
        RING = 4
        identity = sbuf("p1_identity", [P, P])
        flag = sbuf("p1_flag", [1, 1], I32)
        big_diag = sbuf("p1_big_diag", [P, P], BF16)
        w = sbuf("p1_w", [H, HEADS, H])
        least = sbuf("p1_least", [P, 2, HEADS, QUARTERS])
        total = sbuf("p1_total", [P, 2, HEADS])
        inverse = sbuf("p1_inverse", [P, 2, 2, HEADS])
        row_parts = sbuf("p1_row_parts", [P, QUARTERS, TILES])
        gathered = sbuf("p1_gathered", [H, HEADS, P])
        by_head = sbuf("p1_by_head", [P, HEADS, H])
        pair_sum = sbuf("p1_pair_sum", [P, H])
        support = sbuf("p1_support", [P, H])
        support_t = sbuf("p1_support_t", [H, 2, P])
        stage = sbuf("p1_stage", [P, STAGES, QUARTER])
        with ExitStack() as plain:
            place, _, _ = memory(nc, plain)
            any_rows = place("p1_any_rows", [P, N])
            any_adj_t = place("p1_any_adj_t", [P, TILES, P])
            any_neg_e = place("p1_any_neg_e", [P, 2, N])
            any_att = place("p1_any_att", [P, 2, N])
            any_weighted = place("p1_any_weighted", [P, 2, GROUP, P])
            any_off_diag = place("p1_any_off_diag", [P, P])
        neg_e = sbuf("p1_neg_e", [P, HEADS, N])
        spare = sbuf("p1_spare", [P, QUARTER], BF16)
        absent = sbuf("p1_absent", [P, 2, N], BF16)
        att = sbuf("p1_att", [P, 2, HEADS, N])
        adj_t = sbuf("p1_adj_t", [P, RING, GROUP, P])
        weighted = sbuf("p1_weighted", [P, 2, GROUP, HEADS, P])
        ps_att = [psum(f"p1_ps_att{i}", [P, GROUP, HEADS, P]) for i in range(2)]
        ps_gathered = psum("p1_ps_gathered", [P, CHUNK])
        ps_support = psum("p1_ps_support", [P, CHUNK])

        in_const = semaphore("p1_in_const")
        in_any_const = semaphore("p1_in_any_const")
        in_flag = semaphore("p1_in_flag")
        in_any_rows = semaphore("p1_in_any_rows")
        in_any_adj = semaphore("p1_in_any_adj")
        in_any_e = semaphore("p1_in_any_e")
        any_step = semaphore("p1_any_step")
        in_e = [[semaphore(f"p1_in_e{h}{q}") for q in range(QUARTERS)] for h in range(HEADS)]
        in_stage = [semaphore(f"p1_in_stage{i}") for i in range(STAGES)]
        in_adj = [semaphore(f"p1_in_adj{i}") for i in range(RING)]
        rows_summed = semaphore("p1_rows_summed")
        big_diag_ready = semaphore("p1_big_diag_ready")
        first_masked = semaphore("p1_first_masked")
        quarter_masked = semaphore("p1_quarter_masked")
        absent_ready = semaphore("p1_absent_ready")
        masked = semaphore("p1_masked")
        att_ready = semaphore("p1_att_ready")
        turned = semaphore("p1_turned")
        weighted_ready = semaphore("p1_weighted_ready")
        gathered_part = semaphore("p1_gathered_part")
        gathered_ready = semaphore("p1_gathered_ready")
        inverse_step = semaphore("p1_inverse_step")
        inverse_ready = semaphore("p1_inverse_ready")
        head_summed = semaphore("p1_head_summed")
        by_head_ready = semaphore("p1_by_head_ready")
        pair_ready = semaphore("p1_pair_ready")
        support_ready = semaphore("p1_support_ready")
        support_turned = semaphore("p1_support_turned")
        support_copied = semaphore("p1_support_copied")
        out_support = [semaphore(f"p1_out_support{i}") for i in range(2)]
        out_rows = semaphore("p1_out_rows")
        passed = semaphore("p1_passed")

        block = stack.enter_context(nc.Block())

        @block.sync
        def _(sync):
            def load_any(t):
                wait(sync, weighted_ready, HEADS * GROUPS * t)
                sync.dma_start(any_rows[:], io["adj"][bass.ds(t * P, P), :]).then_inc(in_any_rows, 16)
                sync.dma_start(any_adj_t[:], io["adj_t"][bass.ds(t, 1)].rearrange("j p c r -> p (j c) r")) \
                    .then_inc(in_any_adj, 16)
                for h in range(HEADS):
                    wait(sync, masked, HEADS * t + h)
                    for sign in range(2):
                        row = dram["scores"][sign * HEADS + h:sign * HEADS + h + 1, :]
                        sync.dma_start(any_neg_e[:, sign], row.broadcast_to([P, N])).then_inc(in_any_e, 16)

            def load_quarter(t, q):
                wait(sync, rows_summed, QUARTERS * (t - 1) + q + 1)
                wait(sync, quarter_masked, QUARTERS * (t - 1) + q + 1)
                sync.dma_start(stage[:, q], io["adj"][bass.ds(t * P, P), q * QUARTER:(q + 1) * QUARTER]) \
                    .then_inc(in_stage[q], 16)

            def load_turned(t, g):
                slot = g % RING
                wait(sync, weighted_ready, GROUPS * t + g - RING + 1)
                sync.dma_start(
                    adj_t[:, slot],
                    io["adj_t"][bass.ds(t, 1), :, g * GROUP:(g + 1) * GROUP, :]
                    .rearrange("j p c r -> p (j c) r")).then_inc(in_adj[slot], 16)

            def load(t, ahead, loaded=0):
                for g in range(loaded, GROUPS):
                    load_turned(t, g)
                    if ahead and g >= GROUPS - QUARTERS:
                        load_quarter(t + 3, g - (GROUPS - QUARTERS))

            def load_scores(h):
                for q in range(QUARTERS):
                    cut = slice(q * QUARTER, (q + 1) * QUARTER)
                    sync.dma_start(neg_e[:, h, cut], dram["scores"][h:h + 1, cut].broadcast_to([P, QUARTER])) \
                        .then_inc(in_e[h][q], 16)

            sync.dma_start(flag[:], dram["flag"]).then_inc(in_flag, 16)
            sync.dma_start(identity[:], io["identity"]).then_inc(in_const, 16)
            sync.dma_start(w[:], io["w"]).then_inc(in_const, 16)
            for q in range(QUARTERS):
                load_quarter(0, q)
            load_scores(0)
            for h in range(1, HEADS):
                load_scores(h)
            sync.wait_ge(in_flag, 16)
            negative = sync.value_load(flag[0:1, 0:1], min_val=0, max_val=N)
            with sync.If(negative > 0):
                for q in range(QUARTERS):
                    sync.wait_ge(in_stage[q], 16)
                    for h in range(HEADS):
                        sync.wait_ge(in_e[h][q], 16)
                sync.dma_start(any_off_diag[:], io["off_diagonal"]).then_inc(in_any_const, 16)
                load_any(0)
                with sync.Fori(1, TILES) as t:
                    load_any(t)
            with sync.Else():
                for q in range(QUARTERS):
                    load_quarter(1, q)
                for g in range(RING):
                    load_turned(0, g)
                for q in range(QUARTERS):
                    load_quarter(2, q)
                load(0, True, RING)
                with sync.Fori(1, TILES - 3) as t:
                    load(t, True)
                for t in range(TILES - 3, TILES):
                    load(t, False)

        @block.gpsimd
        def _(pool):
            pool.wait_ge(in_const, 32)
            nc.gpsimd.tensor_scalar(big_diag[:], identity[:], BIG, None, ALU.mult).then_inc(big_diag_ready, 1)
            pool.wait_ge(big_diag_ready, 1)

            def mask_tile(t, slot):
                wait(pool, masked, QUARTERS * HEADS * (t - 1))
                for q in range(QUARTERS):
                    wait_apart(pool, in_stage[q], 16 * (t + 1), passed)
                    nc.gpsimd.tensor_scalar(absent[:, slot, q * QUARTER:(q + 1) * QUARTER], stage[:, q],
                                            0.0, BIG, ALU.is_le, ALU.mult).then_inc(quarter_masked, 1)
                pool.wait_ge(quarter_masked, QUARTERS * (t + 1))
                own = absent[:, slot, bass.ds(t * P, P)]
                nc.gpsimd.tensor_tensor(own, own, big_diag[:], ALU.add).then_inc(absent_ready, 1)

            def add_heads(t):
                pool.wait_ge(by_head_ready, t + 1)
                nc.gpsimd.tensor_tensor(pair_sum[:], by_head[:, 0], by_head[:, 1], ALU.add) \
                  .then_inc(pair_ready, 1)
                pool.wait_ge(pair_ready, t + 1)
                wait(pool, support_turned, t)
                nc.gpsimd.tensor_tensor(support[:], pair_sum[:], by_head[:, 2], ALU.add) \
                  .then_inc(support_ready, 1)

            def pair(i, first, last):
                for slot in range(2):
                    t = 2 * i + slot
                    if not last:
                        mask_tile(t + 2, slot)
                    if not (first and slot == 0):
                        add_heads(t - 1)

            pool.wait_ge(in_flag, 16)
            negative = pool.value_load(flag[0:1, 0:1], min_val=0, max_val=N)
            with pool.If(negative > 0):
                add_heads(0)
                with pool.Fori(1, TILES) as t:
                    add_heads(t)
            with pool.Else():
                for t in range(2):
                    pool.wait_ge(first_masked, t * (QUARTERS + 1) + QUARTERS)
                    pool.sem_inc(quarter_masked, QUARTERS)
                pair(0, True, False)
                with pool.Fori(1, TILES // 2 - 1) as i:
                    pair(i, False, False)
                pair(TILES // 2 - 1, False, True)
                add_heads(TILES - 1)

        @block.scalar
        def _(act):
            def sum_rows(t, q):
                act.wait_ge(in_stage[q], 16 * (t + 1))
                wait(act, rows_summed, QUARTERS * t + q)
                nc.scalar.activation(spare[:], stage[:, q], ACT.Copy,
                                     accum_out=row_parts[:, q, bass.ds(t, 1)]).then_inc(rows_summed, 1)

            def exponentiate(t, slot, h):
                act.wait_ge(masked, QUARTERS * HEADS * t + QUARTERS * (h + 1))
                if h == 0:
                    wait(act, inverse_ready, t - 1)
                nc.scalar.activation(att[:, slot, h, :], att[:, slot, h, :], ACT.Exp,
                                     bias=least[:, slot, h, QUARTERS - 1:QUARTERS], scale=-1.0,
                                     accum_out=total[:, slot, h:h + 1]).then_inc(att_ready, 1)

            def exponentiate_any(t):
                for h in range(HEADS):
                    act.wait_ge(masked, HEADS * t + h + 1)
                    if h == 0:
                        wait(act, inverse_ready, t)
                    nc.scalar.activation(any_att[:, 0], any_att[:, 0], ACT.Exp, bias=least[:, 0, h, 0:1],
                                         scale=-1.0, accum_out=total[:, 0, h:h + 1]).then_inc(att_ready, 1)

            def scale_heads(t, slot, parts=GROUPS):
                act.wait_ge(gathered_part, parts * (t + 1))
                nc.scalar.copy(gathered[:], ps_gathered[:, 0:HEADS * P]
                               .rearrange("p (h r) -> p h r", h=HEADS)).then_inc(gathered_ready, 1)
                act.wait_ge(head_summed, t + 1)
                act.wait_ge(inverse_ready, t + 1)
                wait(act, support_ready, t)
                for h in range(HEADS):
                    last = nc.scalar.activation(by_head[:, h], ps_support[:, h * P:(h + 1) * P], ACT.Copy,
                                                scale=inverse[:, slot, 1, h:h + 1])
                last.then_inc(by_head_ready, 1)

            def store_support(t, slot, i):
                act.wait_ge(support_turned, t + 1)
                wait(act, out_support[slot], 16 * i)
                nc.scalar.copy(support_t[:, slot], ps_support[:, HEADS * P:(HEADS + 1) * P]) \
                  .then_inc(support_copied, 1)
                act.wait_ge(support_copied, t + 1)
                act.dma_start(dram["support"][:, bass.ds(t * P, P)], support_t[:, slot]) \
                   .then_inc(out_support[slot], 16)

            def pair(i, first, last):
                for slot in range(2):
                    t = 2 * i + slot
                    before, attend = not (first and slot == 0), not (last and slot)
                    if before:
                        scale_heads(t - 1, 1 - slot)
                    for h in range(HEADS):
                        if attend:
                            exponentiate(t + 1, 1 - slot, h)
                        if h < HEADS - 1 and not last:
                            sum_rows(t + 2, 2 * h)
                            sum_rows(t + 2, 2 * h + 1)
                    if before:
                        store_support(t - 1, 1 - slot, i - 1 + slot)

            act.wait_ge(in_flag, 16)
            negative = act.value_load(flag[0:1, 0:1], min_val=0, max_val=N)
            with act.If(negative > 0):
                def any_tile(t):
                    exponentiate_any(t)
                    scale_heads(t, 0, HEADS * GROUPS)
                    store_support(t, 0, t)

                any_tile(0)
                with act.Fori(1, TILES) as t:
                    any_tile(t)
                act.dma_start(dram["row_parts"], row_parts[:]).then_inc(out_rows, 16)
                act.wait_ge(out_rows, 16)
                act.wait_ge(out_support[0], 16 * TILES)
            with act.Else():
                for q in range(QUARTERS):
                    sum_rows(0, q)
                for h in range(HEADS):
                    exponentiate(0, 0, h)
                for q in range(QUARTERS):
                    sum_rows(1, q)
                pair(0, True, False)
                with act.Fori(1, TILES // 2 - 1) as i:
                    pair(i, False, False)
                pair(TILES // 2 - 1, False, True)
                scale_heads(TILES - 1, 1)
                store_support(TILES - 1, 1, TILES // 2 - 1)
                act.wait_ge(rows_summed, QUARTERS * TILES)
                act.dma_start(dram["row_parts"], row_parts[:]).then_inc(out_rows, 16)
                act.wait_ge(out_rows, 16)
                for slot in range(2):
                    act.wait_ge(out_support[slot], 16 * TILES // 2)

        @block.vector
        def _(dve):
            def mask_scores(t, slot, k):
                h, q = divmod(k, QUARTERS)
                if k == 0:
                    wait(dve, absent_ready, t - 1)
                    wait(dve, att_ready, HEADS * (t - 1))
                if h == 0:
                    wait_apart(dve, turned, GROUPS * (t - 2) + GROUPS // QUARTERS * (q + 1), passed)
                if q:
                    wait_apart(dve, masked, QUARTERS * HEADS * t + k, passed)
                cut = slice(q * QUARTER, (q + 1) * QUARTER)
                nc.vector.tensor_tensor_reduce(
                    out=att[:, slot, h, cut], in0=absent[:, slot, cut], in1=neg_e[:, h, cut],
                    scale=1.0, scalar=least[:, slot, h, q - 1:q] if q else 3e38,
                    op0=ALU.add, op1=ALU.min, accum_out=least[:, slot, h, q:q + 1]).then_inc(masked, 1)

            def weigh(t, g):
                n = GROUPS * t + g
                slot = g % RING
                dve.wait_ge(turned, n + 1)
                dve.wait_ge(in_adj[slot], 16 * (GROUPS // RING * t + g // RING + 1))
                wait(dve, gathered_part, n - 1)
                tile = adj_t[:, slot]
                nc.vector.tensor_tensor(weighted[:, g % 2], ps_att[g % 2][:],
                                        tile.unsqueeze(2).broadcast_to([P, GROUP, HEADS, P]), ALU.mult) \
                  .then_inc(weighted_ready, 1)

            def invert(t, slot, former=1):
                dve.wait_ge(att_ready, HEADS * (t + 1))
                wait(dve, by_head_ready, t - former)
                nc.vector.tensor_scalar(inverse[:, slot, 0], total[:, slot], float(HEADS), None, ALU.mult) \
                  .then_inc(inverse_step, 1)
                dve.wait_ge(inverse_step, t + 1)
                nc.vector.reciprocal(inverse[:, slot, 1], inverse[:, slot, 0]).then_inc(inverse_ready, 1)

            STEPS = 2 + 5 * HEADS

            def mask_any(t):
                def settled(n, instruction):
                    instruction.then_inc(any_step, 1)
                    dve.wait_ge(any_step, STEPS * t + n + 2)

                dve.wait_ge(in_any_rows, 16 * (t + 1))
                settled(0, nc.vector.tensor_reduce(row_parts[:, 0, bass.ds(t, 1)], any_rows[:], AX_X, ALU.add))
                own = any_rows[:, bass.ds(t * P, P)]
                settled(1, nc.vector.tensor_tensor(own, own, any_off_diag[:], ALU.mult))
                for h in range(HEADS):
                    dve.wait_ge(in_any_e, 32 * (HEADS * t + h + 1))
                    wait(dve, turned, GROUPS * (HEADS * t + h))
                    n = 2 + 5 * h
                    settled(n, nc.vector.tensor_scalar(any_att[:, 0], any_rows[:], 0.0, BIG,
                                                       ALU.is_le, ALU.mult))
                    settled(n + 1, nc.vector.tensor_tensor(any_att[:, 0], any_att[:, 0], any_neg_e[:, 0],
                                                           ALU.add))
                    settled(n + 2, nc.vector.tensor_scalar(any_att[:, 1], any_rows[:], 0.0, BIG,
                                                           ALU.is_ge, ALU.mult))
                    settled(n + 3, nc.vector.tensor_tensor(any_att[:, 1], any_att[:, 1], any_neg_e[:, 1],
                                                           ALU.add))
                    settled(n + 4, nc.vector.tensor_tensor(any_att[:, 0], any_att[:, 0], any_att[:, 1],
                                                           ALU.min))
                    nc.vector.tensor_reduce(least[:, 0, h, 0:1], any_att[:, 0], AX_X, ALU.min) \
                      .then_inc(masked, 1)
                    dve.wait_ge(in_any_adj, 16 * (t + 1))
                    for g in range(GROUPS):
                        m = GROUPS * (HEADS * t + h) + g
                        dve.wait_ge(turned, m + 1)
                        wait(dve, gathered_part, m - 1)
                        nc.vector.tensor_tensor(any_weighted[:, g % 2], ps_att[g % 2][:, :, 0, :],
                                                any_adj_t[:, g * GROUP:(g + 1) * GROUP], ALU.mult) \
                          .then_inc(weighted_ready, 1)
                invert(t, 0, former=0)

            AHEAD = 3
            PER_TILE = QUARTERS * HEADS

            def pair(i, last):
                for slot in range(2):
                    t = 2 * i + slot
                    for g in range(GROUPS):
                        weigh(t, g)
                        if g == 0:
                            invert(t, slot)
                        for k in range(AHEAD + PER_TILE * g // GROUPS, AHEAD + PER_TILE * (g + 1) // GROUPS):
                            if k < PER_TILE and not (last and slot):
                                mask_scores(t + 1, 1 - slot, k)
                            elif k >= PER_TILE and not last:
                                mask_scores(t + 2, slot, k - PER_TILE)

            dve.wait_ge(in_flag, 16)
            negative = dve.value_load(flag[0:1, 0:1], min_val=0, max_val=N)
            with dve.If(negative > 0):
                dve.wait_ge(in_any_const, 16)
                nc.vector.memset(row_parts[:], 0.0).then_inc(any_step, 1)
                dve.wait_ge(any_step, 1)
                mask_any(0)
                with dve.Fori(1, TILES) as t:
                    mask_any(t)
            with dve.Else():
                def mask_first(t):
                    for q in range(QUARTERS):
                        dve.wait_ge(in_stage[q], 16 * (t + 1))
                        nc.vector.tensor_scalar(absent[:, t, q * QUARTER:(q + 1) * QUARTER], stage[:, q],
                                                0.0, BIG, ALU.is_le, ALU.mult).then_inc(first_masked, 1)
                    dve.wait_ge(first_masked, t * (QUARTERS + 1) + QUARTERS)
                    dve.wait_ge(big_diag_ready, 1)
                    own = absent[:, t, t * P:(t + 1) * P]
                    nc.vector.tensor_tensor(own, own, big_diag[:], ALU.add).then_inc(first_masked, 1)
                    dve.wait_ge(first_masked, (t + 1) * (QUARTERS + 1))

                mask_first(0)
                for k in range(PER_TILE):
                    dve.wait_ge(in_e[k // QUARTERS][k % QUARTERS], 16)
                    mask_scores(0, 0, k)
                mask_first(1)
                for k in range(AHEAD):
                    mask_scores(1, 1, k)
                pair(0, False)
                with dve.Fori(1, TILES // 2 - 1) as i:
                    pair(i, False)
                pair(TILES // 2 - 1, True)

        @block.tensor
        def _(pe):
            pe.wait_ge(in_const, 32)

            def turn(t, slot, g):
                n = GROUPS * t + g
                if g == 0:
                    pe.wait_ge(att_ready, HEADS * (t + 1))
                wait(pe, weighted_ready, n - 1)
                for k in range(GROUP):
                    c = g * GROUP + k
                    for h in range(HEADS):
                        last = nc.tensor.transpose(ps_att[g % 2][:, k, h, :],
                                                   att[:, slot, h, c * P:(c + 1) * P], identity[:])
                last.then_inc(turned, 1)

            def gather(t, g):
                pe.wait_ge(weighted_ready, GROUPS * t + g + 1)
                if g == 0:
                    wait(pe, gathered_ready, t)
                for k in range(GROUP):
                    c = g * GROUP + k
                    last = nc.tensor.matmul(ps_gathered[:, 0:HEADS * P], x_rows[:, c, :],
                                            weighted[:, g % 2, k].rearrange("p h r -> p (h r)"),
                                            start=c == 0, stop=c == TILES - 1)
                last.then_inc(gathered_part, 1)

            def project(t):
                pe.wait_ge(gathered_ready, t + 1)
                wait(pe, support_copied, t)
                for h in range(HEADS):
                    last = nc.tensor.matmul(ps_support[:, h * P:(h + 1) * P], gathered[:, h, :], w[:, h, :],
                                            start=True, stop=True)
                last.then_inc(head_summed, 1)

            def turn_support(t):
                pe.wait_ge(support_ready, t + 1)
                nc.tensor.transpose(ps_support[:, HEADS * P:(HEADS + 1) * P], support[:], identity[:]) \
                  .then_inc(support_turned, 1)

            def any_tile(t):
                for h in range(HEADS):
                    pe.wait_ge(att_ready, HEADS * t + h + 1)
                    if h == 0:
                        wait(pe, gathered_ready, t)
                    for g in range(GROUPS):
                        m = GROUPS * (HEADS * t + h) + g
                        wait(pe, weighted_ready, m - 1)
                        for k in range(GROUP):
                            c = g * GROUP + k
                            last = nc.tensor.transpose(ps_att[g % 2][:, k, 0, :],
                                                       any_att[:, 0, c * P:(c + 1) * P], identity[:])
                        last.then_inc(turned, 1)
                        pe.wait_ge(weighted_ready, m + 1)
                        for k in range(GROUP):
                            c = g * GROUP + k
                            last = nc.tensor.matmul(ps_gathered[:, h * P:(h + 1) * P], x_rows[:, c, :],
                                                    any_weighted[:, g % 2, k], start=c == 0,
                                                    stop=c == TILES - 1)
                        last.then_inc(gathered_part, 1)
                project(t)
                turn_support(t)

            def pair(i, first, last):
                for slot in range(2):
                    t = 2 * i + slot
                    for g in range(GROUPS):
                        if g < GROUPS - 1:
                            turn(t, slot, g + 1)
                        elif not (last and slot):
                            turn(t + 1, 1 - slot, 0)
                        gather(t, g)
                        if not (first and slot == 0):
                            if g == 0:
                                project(t - 1)
                            if g == 5:
                                turn_support(t - 1)

            pe.wait_ge(in_flag, 16)
            negative = pe.value_load(flag[0:1, 0:1], min_val=0, max_val=N)
            with pe.If(negative > 0):
                any_tile(0)
                with pe.Fori(1, TILES) as t:
                    any_tile(t)
            with pe.Else():
                turn(0, 0, 0)
                pair(0, True, False)
                with pe.Fori(1, TILES // 2 - 1) as i:
                    pair(i, False, False)
                pair(TILES // 2 - 1, False, True)
                project(TILES - 1)
                turn_support(TILES - 1)


def update_phase(nc, io, dram, x_rows, out):
    with ExitStack() as stack:
        sbuf, psum, semaphore = memory(nc, stack)
        GATES = 3
        CELLS = 2
        EDGE, NODE = 0, 1
        STATE = 2
        INPUTS = 3
        IN, OF_STATE = 0, 1
        w = sbuf("p2_w", [H, CELLS, 2, GATES, H])
        w_high = sbuf("p2_w_high", [H, CELLS, 2, GATES, H], F32R)
        w_low = sbuf("p2_w_low", [H, CELLS, 2, GATES, H], F32R)
        bias_in = sbuf("p2_bias_in", [H, CELLS, GATES])
        bias_state = sbuf("p2_bias_state", [H, CELLS, GATES])
        bias_sum = sbuf("p2_bias_sum", [H, CELLS, GATES])
        bias_half = sbuf("p2_bias_half", [H, CELLS, GATES])
        bias_state_half = sbuf("p2_bias_state_half", [H, CELLS, GATES])
        identity = sbuf("p2_identity", [P, P])
        diag = sbuf("p2_diag", [P, TILES])
        mixed = sbuf("p2_mixed", [P, TILES, H])
        stats = sbuf("p2_stats", [P, TILES, nc.vector.BN_STATS_DIM])
        moments = sbuf("p2_moments", [P, TILES, 2])
        row_parts = sbuf("p2_row_parts", [P, QUARTERS, TILES])
        row_sum = sbuf("p2_row_sum", [P, 3, TILES])
        roots = sbuf("p2_roots", [P, 2, TILES])
        inverse = sbuf("p2_inverse", [P, 2, TILES])
        variance = sbuf("p2_variance", [P, TILES])
        RING = 4
        scaled_high = sbuf("p3_scaled_high", [P, TILES, H], F32R)
        scaled_low = sbuf("p3_scaled_low", [P, TILES, H], F32R)
        own = sbuf("p3_own", [P, ROWS, H])
        w1 = sbuf("p3_w1", [H, H])
        adj_t = sbuf("p3_adj_t", [P, RING, ROWS, GROUP, P])
        with ExitStack() as cells:
            place, _, _ = memory(nc, cells)
            inputs = place("p2_inputs", [H, 2, INPUTS, CHUNK])
            inputs_high = place("p2_inputs_high", [H, 2, INPUTS, CHUNK], F32R)
            inputs_low = place("p2_inputs_low", [H, 2, INPUTS, CHUNK], F32R)
            state = place("p2_state", [H, 2, CHUNK])
            reset = place("p2_reset", [H, CELLS, CHUNK])
            update = place("p2_update", [H, CELLS, CHUNK])
            half_state = place("p2_half_state", [H, CELLS, CHUNK])
            gated = place("p2_gated", [H, CELLS, CHUNK])
            pre = place("p2_pre", [H, CELLS, CHUNK])
            new = place("p2_new", [H, CELLS, CHUNK])
            change = place("p2_change", [H, CELLS, CHUNK])
            scaled = place("p2_scaled", [H, CELLS, CHUNK])
            cell_out = place("p2_cell_out", [H, CELLS, CHUNK])
            both = place("p2_both", [H, 2, CHUNK])
        high = sbuf("p3_high", [P, RING, ROWS, GROUP, P], F32R)
        low = sbuf("p3_low", [P, RING, ROWS, GROUP, P], F32R)
        gathered = sbuf("p3_gathered", [H, CHUNK])
        relu = sbuf("p3_relu", [P, ROWS, H])
        second = sbuf("p3_second", [P, ROWS, H])
        second_stats = sbuf("p3_stats", [P, ROWS, nc.vector.BN_STATS_DIM])
        second_moments = sbuf("p3_moments", [P, ROWS, 2])
        second_variance = sbuf("p3_variance", [P, ROWS])
        root = sbuf("p3_root", [P, ROWS])
        second_inverse = sbuf("p3_inverse", [P, ROWS])
        result = sbuf("p3_result", [P, 2, ROWS, H])
        gates = [[psum(f"p2_gate{c}{g}", [P, CHUNK]) for g in range(4)] for c in range(CELLS)]
        turned = gates[1][0]
        ps_gathered = gates[0][0:2]
        ps_out = [bank[:].rearrange("p (j h) -> p j h", j=ROWS) for bank in gates[0][2:4]]

        in_const = semaphore("p2_in_const")
        w_high_ready = semaphore("p2_w_high_ready")
        w_low_ready = semaphore("p2_w_low_ready")
        inputs_high_ready = semaphore("p2_inputs_high_ready")
        inputs_low_ready = semaphore("p2_inputs_low_ready")
        in_chunk = [semaphore(f"p2_in_chunk{i}") for i in range(2)]
        in_state = [semaphore(f"p2_in_state{i}") for i in range(2)]
        bias_step = semaphore("p2_bias_step")
        bias_ready = semaphore("p2_bias_ready")
        gates_summed = semaphore("p2_gates_summed")
        act_gates = semaphore("p2_act_gates")
        gated_ready = semaphore("p2_gated_ready")
        pre_ready = semaphore("p2_pre_ready")
        new_ready = semaphore("p2_new_ready")
        change_ready = semaphore("p2_change_ready")
        scaled_ready = semaphore("p2_scaled_ready")
        cell_ready = semaphore("p2_cell_ready")
        both_ready = semaphore("p2_both_ready")
        both_turned = semaphore("p2_both_turned")
        mixed_ready = semaphore("p2_mixed_ready")
        stats_ready = semaphore("p2_stats_ready")
        moments_ready = semaphore("p2_moments_ready")
        end_step = semaphore("p2_end_step")
        roots_ready = semaphore("p2_roots_ready")
        inverse_ready = semaphore("p2_inverse_ready")
        normed = semaphore("p2_normed")
        scaled_high_ready = semaphore("p3_scaled_high_ready")
        scaled_low_ready = semaphore("p3_scaled_low_ready")
        in_w1 = semaphore("p3_in_w1")
        in_adj = [semaphore(f"p3_in_adj{i}") for i in range(RING)]
        high_ready = semaphore("p3_high_ready")
        low_ready = semaphore("p3_low_ready")
        group_done = semaphore("p3_group_done")
        own_ready = semaphore("p3_own_ready")
        chunk_done = semaphore("p3_chunk_done")
        gathered_ready = semaphore("p3_gathered_ready")
        out_summed = semaphore("p3_out_summed")
        relu_ready = semaphore("p3_relu_ready")
        second_ready = semaphore("p3_second_ready")
        second_stats_ready = semaphore("p3_stats_ready")
        second_moments_ready = semaphore("p3_moments_ready")
        variance_ready = semaphore("p3_variance_ready")
        root_ready = semaphore("p3_root_ready")
        second_inverse_ready = semaphore("p3_inverse_ready")
        result_ready = semaphore("p3_result_ready")
        out_done = [semaphore(f"p3_out_done{i}") for i in range(2)]
        passed = semaphore("p2_passed")

        block = stack.enter_context(nc.Block())

        @block.sync
        def _(sync):
            def load_inputs(c, half):
                wait(sync, inputs_low_ready, c - 1)
                at = bass.ds(c * CHUNK, CHUNK)
                sync.dma_start(inputs[:, half, EDGE], dram["sums"][:, at]).then_inc(in_chunk[half], 16)
                sync.dma_start(inputs[:, half, NODE], dram["support"][:, at]).then_inc(in_chunk[half], 16)
                sync.dma_start(inputs[:, half, STATE], io["x_cols"][:, at]).then_inc(in_chunk[half], 16)

            def load_state(c, half):
                wait(sync, change_ready, CELLS * (c - 1))
                sync.dma_start(state[:, half], io["x_cols"][:, bass.ds(c * CHUNK, CHUNK)]) \
                    .then_inc(in_state[half], 16)

            load_inputs(0, 0)
            for c, cell in enumerate(("edge", "node")):
                sync.dma_start(w[:, c, IN], io[f"{cell}_w_in"]).then_inc(in_const, 16)
                sync.dma_start(w[:, c, OF_STATE], io[f"{cell}_w_state"]).then_inc(in_const, 16)
                sync.dma_start(bias_in[:, c], io[f"{cell}_bias_in"]).then_inc(in_const, 16)
                sync.dma_start(bias_state[:, c], io[f"{cell}_bias_state"]).then_inc(in_const, 16)
            sync.dma_start(identity[:], io["identity"]).then_inc(in_const, 16)
            sync.dma_start(diag[:], io["diag_cols"]).then_inc(in_const, 16)
            sync.dma_start(row_parts[:], dram["row_parts"]).then_inc(in_const, 16)
            load_inputs(1, 1)
            load_state(0, 0)
            load_inputs(2, 0)
            load_state(1, 1)
            with sync.Fori(1, CHUNKS // 2 - 1) as i:
                load_inputs(2 * i + 1, 1)
                load_state(2 * i, 0)
                load_inputs(2 * i + 2, 0)
                load_state(2 * i + 1, 1)
            load_inputs(CHUNKS - 1, 1)
            load_state(CHUNKS - 2, 0)
            load_state(CHUNKS - 1, 1)
            sync.dma_start(w1[:], io["w1_t"]).then_inc(in_w1, 16)

            def store(c, half):
                sync.wait_ge(result_ready, c + 1)
                sync.dma_start(out[bass.ds(c * CHUNK, CHUNK), :].rearrange("(j p) h -> p j h", p=P),
                               result[:, half]).then_inc(out_done[half], 16)

            def load_chunk(c, half, stores):
                for g in range(GROUPS):
                    slot = g % RING
                    wait(sync, low_ready, GROUPS * c + g - RING + 1)
                    sync.dma_start(
                        adj_t[:, slot],
                        io["adj_t"][bass.ds(c * ROWS, ROWS), :, g * GROUP:(g + 1) * GROUP, :]
                        .rearrange("j p c r -> p j c r")).then_inc(in_adj[slot], 16)
                    if stores and g == 4:
                        store(c - 2, half)

            load_chunk(0, 0, False)
            load_chunk(1, 1, False)
            with sync.Fori(1, CHUNKS // 2) as i:
                load_chunk(2 * i, 0, True)
                load_chunk(2 * i + 1, 1, True)
            store(CHUNKS - 2, 0)
            store(CHUNKS - 1, 1)
            for half in range(2):
                sync.wait_ge(out_done[half], 16 * CHUNKS // 2)

        @block.gpsimd
        def _(pool):
            def state_change(n, k, half):
                pool.wait_ge(new_ready, n + 1)
                wait(pool, scaled_ready, n - 1)
                nc.gpsimd.tensor_tensor(change[:, k], state[:, half], new[:, k], ALU.subtract) \
                  .then_inc(change_ready, 1)

            def add_cells(c, half):
                pool.wait_ge(cell_ready, CELLS * (c + 1))
                wait(pool, both_turned, c - 1)
                nc.gpsimd.tensor_tensor(both[:, half], cell_out[:, EDGE], cell_out[:, NODE], ALU.add) \
                  .then_inc(both_ready, 1)

            def chunk(c, half, i, former):
                if former:
                    state_change(CELLS * c - 1, NODE, 1 - half)
                    add_cells(c - 1, 1 - half)
                pool.wait_ge(in_state[half], 16 * (i + 1))
                state_change(CELLS * c, EDGE, half)

            chunk(0, 0, 0, False)
            chunk(1, 1, 0, True)
            with pool.Fori(1, CHUNKS // 2) as i:
                chunk(2 * i, 0, i, True)
                chunk(2 * i + 1, 1, i, True)
            state_change(CELLS * CHUNKS - 1, NODE, 1)
            add_cells(CHUNKS - 1, 1)

            def own_rows(c):
                wait(pool, chunk_done, c)
                at = bass.ds(c * ROWS, ROWS)
                nc.gpsimd.tensor_tensor(own[:], scaled_high[:, at, :].bitcast(F32),
                                        scaled_low[:, at, :].bitcast(F32), ALU.add).then_inc(own_ready, 1)

            pool.wait_ge(scaled_low_ready, TILES)
            own_rows(0)
            with pool.Fori(1, CHUNKS) as c:
                own_rows(c)

        @block.scalar
        def _(act):
            def high_inputs(c, half, i):
                act.wait_ge(in_chunk[half], 48 * (i + 1))
                wait(act, gates_summed, CELLS * (c - 1))
                nc.scalar.copy(inputs_high[:, half], inputs[:, half]).then_inc(inputs_high_ready, 1)

            high_inputs(0, 0, 0)
            act.wait_ge(in_const, 16 * 11)
            nc.scalar.copy(w_high[:], w[:]).then_inc(w_high_ready, 1)

            def gate_values(n, k):
                ps = gates[k]
                act.wait_ge(gates_summed, n + 1)
                wait(act, scaled_ready, n - 1)
                nc.scalar.activation(reset[:, k], ps[0][:], ACT.Tanh, bias=bias_half[:, k, 0:1], scale=0.5)
                nc.scalar.activation(half_state[:, k], ps[3][:], ACT.Identity,
                                     bias=bias_state_half[:, k, 2:3], scale=0.5)
                nc.scalar.activation(update[:, k], ps[1][:], ACT.Tanh, bias=bias_half[:, k, 1:2], scale=0.5) \
                  .then_inc(act_gates, 1)

            def new_state(n, k):
                act.wait_ge(pre_ready, n + 1)
                wait(act, change_ready, n - 1)
                wait(act, cell_ready, n - 1)
                nc.scalar.activation(new[:, k], pre[:, k], ACT.Tanh, bias=bias_in[:, k, 2:3]) \
                  .then_inc(new_ready, 1)

            def cells(c, half, i, former, last):
                n = CELLS * c
                if not last:
                    high_inputs(c + 1, 1 - half, i + half)
                if former:
                    new_state(n - 1, NODE)
                gate_values(n, EDGE)
                new_state(n, EDGE)
                gate_values(n + 1, NODE)

            act.wait_ge(bias_ready, 1)
            cells(0, 0, 0, False, False)
            cells(1, 1, 0, True, False)
            with act.Fori(1, CHUNKS // 2 - 1) as i:
                cells(2 * i, 0, i, True, False)
                cells(2 * i + 1, 1, i, True, False)
            cells(CHUNKS - 2, 0, CHUNKS // 2 - 1, True, False)
            cells(CHUNKS - 1, 1, CHUNKS // 2 - 1, True, True)
            new_state(CELLS * CHUNKS - 1, NODE)
            act.wait_ge(in_adj[0], 16)
            nc.scalar.copy(high[:, 0], adj_t[:, 0]).then_inc(high_ready, 1)
            act.wait_ge(end_step, 5)
            nc.scalar.activation(roots[:, 0], variance[:], ACT.Sqrt)
            nc.scalar.activation(roots[:, 1], row_sum[:, 2], ACT.Sqrt).then_inc(roots_ready, 1)
            def scale_rows(g):
                for t in range(g * GROUP, (g + 1) * GROUP):
                    act.wait_ge(normed, t + 1)
                    nc.scalar.activation(scaled_high[:, t], mixed[:, t], ACT.Copy,
                                         scale=inverse[:, 1, t:t + 1]).then_inc(scaled_high_ready, 1)

            def gather_end(c, half):
                act.wait_ge(chunk_done, c + 1)
                wait(act, out_summed, c)
                nc.scalar.copy(gathered[:], ps_gathered[half][:]).then_inc(gathered_ready, 1)

            def positive(c, half):
                act.wait_ge(out_summed, c + 1)
                wait(act, second_ready, c)
                for j in range(ROWS):
                    last = nc.scalar.activation(relu[:, j], ps_out[half][:, j], ACT.Relu,
                                                scale=inverse[:, 1, bass.ds(c * ROWS + j, 1)])
                last.then_inc(relu_ready, 1)

            def second_root(c):
                act.wait_ge(variance_ready, c + 1)
                nc.scalar.activation(root[:], second_variance[:], ACT.Sqrt).then_inc(root_ready, 1)

            def chunk(c, half, former):
                d, d_half = c - 1, 1 - half
                for g in range(GROUPS):
                    slot, n = g % RING, GROUPS * c + g
                    if not former:
                        scale_rows(g)
                    if not former and g == 0:
                        continue
                    act.wait_ge(in_adj[slot], 16 * (GROUPS // RING * c + g // RING + 1))
                    wait(act, group_done, n - RING + 1)
                    nc.scalar.copy(high[:, slot], adj_t[:, slot]).then_inc(high_ready, 1)
                    if former and g == 1:
                        gather_end(d, d_half)
                    if former and g == 4:
                        positive(d, d_half)
                    if former and g == 7:
                        second_root(d)

            act.wait_ge(inverse_ready, 1)
            chunk(0, 0, False)
            chunk(1, 1, True)
            with act.Fori(1, CHUNKS // 2) as i:
                chunk(2 * i, 0, True)
                chunk(2 * i + 1, 1, True)
            gather_end(CHUNKS - 1, 1)
            positive(CHUNKS - 1, 1)
            second_root(CHUNKS - 1)

        @block.vector
        def _(dve):
            def low_inputs(c, half):
                dve.wait_ge(inputs_high_ready, c + 1)
                nc.vector.tensor_tensor(inputs_low[:, half], inputs[:, half],
                                        inputs_high[:, half].bitcast(F32), ALU.subtract) \
                  .then_inc(inputs_low_ready, 1)

            def split_low(n, g=0):
                slot = g % RING
                dve.wait_ge(high_ready, n + 1)
                wait(dve, group_done, n - RING + 1)
                nc.vector.tensor_tensor(low[:, slot], adj_t[:, slot], high[:, slot].bitcast(F32),
                                        ALU.subtract).then_inc(low_ready, 1)

            low_inputs(0, 0)
            dve.wait_ge(in_const, 16 * 11)
            nc.vector.tensor_tensor(bias_sum[:], bias_in[:], bias_state[:], ALU.add).then_inc(bias_step, 1)
            nc.vector.tensor_scalar(bias_state_half[:], bias_state[:], 0.5, None, ALU.mult)
            dve.wait_ge(bias_step, 1)
            nc.vector.tensor_scalar(bias_half[:], bias_sum[:], 0.5, None, ALU.mult).then_inc(bias_ready, 1)

            dve.wait_ge(w_high_ready, 1)
            nc.vector.tensor_tensor(w_low[:], w[:], w_high[:].bitcast(F32), ALU.subtract) \
              .then_inc(w_low_ready, 1)

            def gate(n, k):
                dve.wait_ge(act_gates, n + 1)
                nc.vector.scalar_tensor_tensor(gated[:, k], reset[:, k], 1.0, half_state[:, k],
                                               ALU.add, ALU.mult).then_inc(gated_ready, 1)
                dve.wait_ge(gated_ready, n + 1)
                wait(dve, new_ready, n - 1)
                nc.vector.tensor_tensor(pre[:, k], gates[k][2][:], gated[:, k], ALU.add).then_inc(pre_ready, 1)

            def blend(c, n, k):
                dve.wait_ge(change_ready, n + 1)
                nc.vector.scalar_tensor_tensor(scaled[:, k], update[:, k], 1.0, change[:, k],
                                               ALU.add, ALU.mult).then_inc(scaled_ready, 1)
                dve.wait_ge(scaled_ready, n + 1)
                wait(dve, both_ready, c)
                nc.vector.scalar_tensor_tensor(cell_out[:, k], scaled[:, k], 0.5, new[:, k],
                                               ALU.mult, ALU.add).then_inc(cell_ready, 1)

            def mix(c):
                dve.wait_ge(both_turned, c + 1)
                for j in range(ROWS):
                    last = nc.vector.scalar_tensor_tensor(
                        mixed[:, bass.ds(c * ROWS + j, 1), :].rearrange("p j h -> p (j h)"),
                        turned[:, j * P:(j + 1) * P], diag[:, bass.ds(c * ROWS + j, 1)],
                        x_rows[:, bass.ds(c * ROWS + j, 1), :].rearrange("p j h -> p (j h)"),
                        ALU.mult, ALU.add)
                last.then_inc(mixed_ready, 1)

            def row_stats(c):
                wait_apart(dve, mixed_ready, c + 1, passed)
                for j in range(ROWS):
                    last = nc.vector.bn_stats(
                        stats[:, bass.ds(c * ROWS + j, 1), :].rearrange("p j s -> p (j s)"),
                        mixed[:, bass.ds(c * ROWS + j, 1), :].rearrange("p j h -> p (j h)"))
                last.then_inc(stats_ready, 1)

            def cells(c, half, former, mixes, last):
                n = CELLS * c
                if not last:
                    low_inputs(c + 1, 1 - half)
                if mixes:
                    mix(c - 2)
                gate(n, EDGE)
                if former:
                    blend(c - 1, n - 1, NODE)
                if mixes:
                    row_stats(c - 2)
                gate(n + 1, NODE)
                blend(c, n, EDGE)

            cells(0, 0, False, False, False)
            cells(1, 1, True, False, False)
            with dve.Fori(1, CHUNKS // 2 - 1) as i:
                cells(2 * i, 0, True, True, False)
                cells(2 * i + 1, 1, True, True, False)
            cells(CHUNKS - 2, 0, True, True, False)
            cells(CHUNKS - 1, 1, True, True, True)
            blend(CHUNKS - 1, CELLS * CHUNKS - 1, NODE)
            mix(CHUNKS - 2)
            row_stats(CHUNKS - 2)
            dve.wait_ge(cell_ready, CELLS * CHUNKS)
            split_low(0)
            dve.wait_ge(stats_ready, CHUNKS - 1)
            for t in range(TILES - ROWS):
                nc.vector.bn_aggr(moments[:, t], stats[:, t])
            mix(CHUNKS - 1)
            row_stats(CHUNKS - 1)
            dve.wait_ge(stats_ready, CHUNKS)
            for t in range(TILES - ROWS, TILES):
                last = nc.vector.bn_aggr(moments[:, t], stats[:, t])
            last.then_inc(moments_ready, 1)
            dve.wait_ge(moments_ready, 1)
            nc.vector.tensor_scalar(variance[:], moments[:, :, 1], EPS, None, ALU.add).then_inc(end_step, 1)
            for k in range(2):
                nc.vector.tensor_tensor(row_sum[:, k], row_parts[:, 2 * k], row_parts[:, 2 * k + 1], ALU.add) \
                  .then_inc(end_step, 1)
            dve.wait_ge(end_step, 3)
            nc.vector.tensor_tensor(row_sum[:, 0], row_sum[:, 0], row_sum[:, 1], ALU.add).then_inc(end_step, 1)
            dve.wait_ge(end_step, 4)
            nc.vector.tensor_scalar(row_sum[:, 2], row_sum[:, 0], 1.0, None, ALU.add).then_inc(end_step, 1)
            dve.wait_ge(roots_ready, 1)
            nc.vector.reciprocal(inverse[:], roots[:]).then_inc(inverse_ready, 1)
            dve.wait_ge(inverse_ready, 1)

            def rows_of(g):
                return range(g * GROUP, (g + 1) * GROUP)

            def norm_rows(g):
                for t in rows_of(g):
                    nc.vector.tensor_scalar(mixed[:, t], mixed[:, t], moments[:, t, 0:1],
                                            inverse[:, 0, t:t + 1], ALU.subtract, ALU.mult).then_inc(normed, 1)

            def scaled_rest(g):
                for t in rows_of(g):
                    dve.wait_ge(scaled_high_ready, t + 1)
                    nc.vector.scalar_tensor_tensor(scaled_low[:, t], mixed[:, t], inverse[:, 1, t:t + 1],
                                                   scaled_high[:, t].bitcast(F32), ALU.mult, ALU.subtract) \
                      .then_inc(scaled_low_ready, 1)

            def second_mix(c):
                dve.wait_ge(relu_ready, c + 1)
                wait(dve, result_ready, c)
                nc.vector.tensor_tensor(second[:], relu[:], mixed[:, bass.ds(c * ROWS, ROWS), :], ALU.add) \
                  .then_inc(second_ready, 1)
                dve.wait_ge(second_ready, c + 1)
                for j in range(ROWS):
                    last = nc.vector.bn_stats(second_stats[:, j], second[:, j])
                last.then_inc(second_stats_ready, 1)
                wait_apart(dve, second_stats_ready, c + 1, passed)
                for j in range(ROWS):
                    last = nc.vector.bn_aggr(second_moments[:, j], second_stats[:, j])
                last.then_inc(second_moments_ready, 1)
                dve.wait_ge(second_moments_ready, c + 1)
                wait(dve, root_ready, c)
                nc.vector.tensor_scalar(second_variance[:], second_moments[:, :, 1], EPS, None, ALU.add) \
                  .then_inc(variance_ready, 1)

            def second_norm(c, half, i):
                dve.wait_ge(root_ready, c + 1)
                nc.vector.reciprocal(second_inverse[:], root[:]).then_inc(second_inverse_ready, 1)
                dve.wait_ge(second_inverse_ready, c + 1)
                wait(dve, out_done[half], 16 * i)
                for j in range(ROWS):
                    last = nc.vector.tensor_scalar(
                        result[:, half, j], second[:, j], second_moments[:, j, 0:1],
                        second_inverse[:, j:j + 1], ALU.subtract, ALU.mult)
                last.then_inc(result_ready, 1)

            def second_chunk(c, half, i, former):
                d, d_half, d_i = c - 1, 1 - half, i if half else i - 1
                for g in range(GROUPS):
                    if not former:
                        if g < GROUPS - 1:
                            norm_rows(g + 1)
                        scaled_rest(g)
                    if former or g:
                        split_low(GROUPS * c + g, g)
                    if former and g == 5:
                        second_mix(d)
                    if former and g == 7:
                        second_norm(d, d_half, d_i)

            norm_rows(0)
            second_chunk(0, 0, 0, False)
            second_chunk(1, 1, 0, True)
            second_chunk(2, 0, 1, True)
            second_chunk(3, 1, 1, True)
            with dve.Fori(2, CHUNKS // 2) as i:
                second_chunk(2 * i, 0, i, True)
                second_chunk(2 * i + 1, 1, i, True)
            second_mix(CHUNKS - 1)
            second_norm(CHUNKS - 1, 1, CHUNKS // 2 - 1)

        @block.tensor
        def _(pe):
            pe.wait_ge(in_const, 16 * 11)

            def banks_free(n):
                wait(pe, pre_ready, n - 1)
                wait(pe, act_gates, n - 1)

            def product(ps, weights, source, start, stop):
                k, of, g = weights
                half, kind = source
                high_w, low_w = w_high[:, k, of, g], w_low[:, k, of, g]
                high_s, low_s = inputs_high[:, half, kind], inputs_low[:, half, kind]
                nc.tensor.matmul(ps, high_w, high_s, start=start, stop=False)
                nc.tensor.matmul(ps, high_w, low_s, start=False, stop=False)
                return nc.tensor.matmul(ps, low_w, high_s, start=False, stop=stop)

            def gate_sum(k, g, half):
                product(gates[k][g][:], (k, IN, g), (half, k), True, False)
                return product(gates[k][g][:], (k, OF_STATE, g), (half, STATE), False, True)

            def new_sums(k, half):
                product(gates[k][2][:], (k, IN, 2), (half, k), True, True)
                return product(gates[k][3][:], (k, OF_STATE, 2), (half, STATE), True, True)

            def turn(c, half):
                pe.wait_ge(both_ready, c + 1)
                for j in range(ROWS):
                    last = nc.tensor.transpose(turned[:, j * P:(j + 1) * P], both[:, half, j * P:(j + 1) * P],
                                               identity[:])
                last.then_inc(both_turned, 1)

            def chunk(c, half, turns):
                pe.wait_ge(inputs_low_ready, c + 1)
                n = CELLS * c
                banks_free(n)
                gate_sum(EDGE, 0, half)
                gate_sum(EDGE, 1, half)
                new_sums(EDGE, half).then_inc(gates_summed, 1)
                banks_free(n + 1)
                if turns:
                    turn(c - 2, half)
                gate_sum(NODE, 1, half)
                new_sums(NODE, half)
                if turns:
                    pe.wait_ge(mixed_ready, c - 1)
                gate_sum(NODE, 0, half).then_inc(gates_summed, 1)

            pe.wait_ge(w_low_ready, 1)
            chunk(0, 0, False)
            chunk(1, 1, False)
            with pe.Fori(1, CHUNKS // 2) as i:
                chunk(2 * i, 0, True)
                chunk(2 * i + 1, 1, True)
            pe.wait_ge(act_gates, CELLS * CHUNKS)
            turn(CHUNKS - 2, 0)
            pe.wait_ge(mixed_ready, CHUNKS - 1)
            turn(CHUNKS - 1, 1)

            def rows_out(c, half):
                pe.wait_ge(gathered_ready, c + 1)
                wait(pe, relu_ready, c - 1)
                for j in range(ROWS):
                    last = nc.tensor.matmul(ps_out[half][:, j], gathered[:, j * P:(j + 1) * P], w1[:],
                                            start=True, stop=True)
                last.then_inc(out_summed, 1)

            def second_chunk(c, half, former):
                wait(pe, gathered_ready, c - 1)
                for g in range(GROUPS):
                    if not former:
                        pe.wait_ge(scaled_low_ready, GROUP * (g + 1))
                    pe.wait_ge(low_ready, GROUPS * c + g + 1)
                    for k in range(GROUP):
                        t = g * GROUP + k
                        adj_high, adj_low = high[:, g % RING, :, k, :], low[:, g % RING, :, k, :]
                        bank = ps_gathered[half][:]
                        nc.tensor.matmul(bank, scaled_high[:, t, :], adj_high, start=t == 0, stop=False)
                        nc.tensor.matmul(bank, scaled_high[:, t, :], adj_low, start=False, stop=False)
                        last = nc.tensor.matmul(bank, scaled_low[:, t, :], adj_high, start=False, stop=False)
                    last.then_inc(group_done, 1)
                    if former and g == 1:
                        rows_out(c - 1, 1 - half)
                pe.wait_ge(own_ready, c + 1)
                for j in range(ROWS):
                    last = nc.tensor.matmul(ps_gathered[half][:, j * P:(j + 1) * P], own[:, j], identity[:],
                                            start=False, stop=j == ROWS - 1)
                last.then_inc(chunk_done, 1)

            pe.wait_ge(in_w1, 16)
            second_chunk(0, 0, False)
            second_chunk(1, 1, True)
            with pe.Fori(1, CHUNKS // 2) as i:
                second_chunk(2 * i, 0, True)
                second_chunk(2 * i + 1, 1, True)
            rows_out(CHUNKS - 1, 1)


def two_layers(nc, io, out):
    dram = {
        "scores": nc.dram_tensor("neg_scores", [SCORES, N], F32).ap(),
        "sums": nc.dram_tensor("neighbour_sums", [H, N], F32).ap(),
        "support": nc.dram_tensor("edge_support", [H, N], F32).ap(),
        "row_parts": nc.dram_tensor("row_parts", [P, QUARTERS, TILES], F32).ap(),
        "flag": nc.dram_tensor("negative_flag", [1, 1], I32).ap(),
    }
    with nc.sbuf_tensor("x_rows", [P, TILES, H], F32) as x_rows:
        score_phase(nc, io, dram, x_rows)
        attention_phase(nc, io, dram, x_rows)
        update_phase(nc, io, dram, x_rows, out)


def score_selection():
    select = np.zeros((P, SELECTED), np.float32)
    select_diag = np.zeros((2 * BAND, SELECTED), np.float32)
    for h in range(HEADS):
        for score, positive_half in ((h, 0), (HEADS + h, 1)):
            positive, negative = 2 * h + positive_half, 2 * h + 1 - positive_half
            for odd in (0, ODD):
                for s in range(SPLITS):
                    select[odd + SIGNED + 1 + s * SCORES + positive, score] = -1.0
                    select[odd + NEG + 1 + s * SCORES + positive, score] = -1.0
                    select[odd + NEG + 1 + s * SCORES + negative, score] = -1.0
            select_diag[POS_DIAG + positive, score] = 1.0
            select_diag[NEG_DIAG + negative, score] = 1.0
    for odd in (0, ODD):
        select[odd + NEG, COUNT] = 1.0
    return select, select_diag


def kernel(x, adj, L0_gnn_gat_W, L0_gnn_gat_a, L0_gnn_edge_Wih, L0_gnn_edge_Whh, L0_gnn_edge_bih,
           L0_gnn_edge_bhh, L0_gnn_node_Wih, L0_gnn_node_Whh, L0_gnn_node_bih, L0_gnn_node_bhh, L1_gnn_W):
    import concourse.bacc as bacc
    from concourse.bass_utils import run_bass_kernel_spmd

    x, adj = np.asarray(x), np.asarray(adj)
    gat_w, gat_a = np.asarray(L0_gnn_gat_W), np.asarray(L0_gnn_gat_a)
    diag = np.diagonal(adj)

    def gate_rows(w):
        return np.asarray(w).reshape(3, H, H).transpose(2, 0, 1)

    def gate_bias(b):
        return np.asarray(b).reshape(3, H).T

    select, select_diag = score_selection()
    arrays = {
        "x": x,
        "x_cols": x.T,
        "adj": adj,
        "adj_t": adj.reshape(TILES, P, TILES, P).transpose(0, 3, 2, 1),
        "diag_row": diag.reshape(1, N),
        "diag_cols": diag.reshape(TILES, P).T,
        "w": gat_w.transpose(1, 0, 2),
        "w_t": gat_w.transpose(2, 0, 1),
        "a": gat_a.reshape(HEADS, 2, H).transpose(2, 0, 1).reshape(H, SCORES),
        "edge_w_in": gate_rows(L0_gnn_edge_Wih),
        "edge_w_state": gate_rows(L0_gnn_edge_Whh),
        "edge_bias_in": gate_bias(L0_gnn_edge_bih),
        "edge_bias_state": gate_bias(L0_gnn_edge_bhh),
        "node_w_in": gate_rows(L0_gnn_node_Wih),
        "node_w_state": gate_rows(L0_gnn_node_Whh),
        "node_bias_in": gate_bias(L0_gnn_node_bih),
        "node_bias_state": gate_bias(L0_gnn_node_bhh),
        "w1_t": np.asarray(L1_gnn_W).T,
        "identity": np.eye(P, dtype=np.float32),
        "off_diagonal": 1 - np.eye(P, dtype=np.float32),
        "select": select,
        "select_diag": select_diag,
    }
    arrays = {name: np.ascontiguousarray(a) for name, a in arrays.items()}
    nc = bacc.Bacc("TRN2", target_bir_lowering=False, num_devices=1, dynamic_dma_scratch_size=1024)
    io = {name: nc.dram_tensor(f"in_{name}", a.shape, mybir.dt.from_np(a.dtype), kind="ExternalInput").ap()
          for name, a in arrays.items()}
    out = nc.dram_tensor("out", (N, H), F32, kind="ExternalOutput").ap()
    two_layers(nc, io, out)
    ran = run_bass_kernel_spmd(nc, [{f"in_{name}": a for name, a in arrays.items()}], core_ids=[0])
    return ran.results[0]["out"]
```
